# Optimizing a Trainium2 kernel written in Bass

```python
import numpy as np
import jax
import jax.numpy as jnp

def _softmax(x, axis=-1):
    return jax.nn.softmax(x, axis=axis)

def _gelu(x):
    return jax.nn.gelu(x, approximate=True)

def _silu(x):
    return jax.nn.silu(x)

def _sigmoid(x):
    return jax.nn.sigmoid(x)

def _layernorm(x, axis=-1, eps=1e-05):
    m = jnp.mean(x, axis=axis, keepdims=True)
    v = jnp.var(x, axis=axis, keepdims=True)
    return (x - m) / jnp.sqrt(v + eps)

def _scatter_add(tgt, idx, src, axis=0):
    return tgt.at[idx].add(src)

def _segment_sum(src, seg, n):
    return jax.ops.segment_sum(src, seg, n)
kernel_name = 'mk_gnn_preln_d4_gnn_r32_43f6e4'

def setup_inputs(seed: int=0):
    np.random.seed(seed)
    _w = jnp.asarray

    def _rec_inputs():
        import jax
        import jax.numpy as jnp
        _gk = jax.random.key(seed)
        x = -8.776e-05 + 1 * jax.random.normal(jax.random.fold_in(_gk, 1), (1250, 128), jnp.float32)
        _s = jax.random.randint(jax.random.fold_in(_gk, 2), (10000,), 0, 1250, jnp.int32)
        _d = jax.random.randint(jax.random.fold_in(_gk, 3), (10000,), 0, 1250, jnp.int32)
        _loop = jnp.arange(1250, dtype=jnp.int32)
        src = jnp.concatenate([_s, _d, _loop])
        dst = jnp.concatenate([_d, _s, _loop])
        _o = jnp.argsort(dst, stable=True)
        src = src[_o]
        dst = dst[_o]
        edge_attr_16 = 0.000130101 + 1.00012 * jax.random.normal(jax.random.fold_in(_gk, 13), (21250, 16), jnp.float32)
        edge_weight1 = jax.random.uniform(jax.random.fold_in(_gk, 15), (21250, 1), jnp.float32, 0.0, 0.999998)
        return (x, src, dst, edge_attr_16, edge_weight1)
    x, src, dst, edge_attr_16, edge_weight1 = _rec_inputs()

    def _L0_gnn_setup():
        import jax, jax.numpy as jnp
        import numpy as np
        N = 1250
        E = 20000
        D = 128
        G = 8
        NPG = N // G
        EPS = 1e-06
        SLOPE = 0.01

        def leaky(x):
            return jnp.where(x >= 0, x, SLOPE * x)
        key = jax.random.key(seed)
        ks = jax.random.split(key, 8)
        x = jax.random.normal(ks[0], (N, D), dtype=jnp.float32)
        edge_index = jax.random.randint(ks[1], (2, E), 0, N, dtype=jnp.int32)
        w = jax.random.uniform(ks[2], (E, 1), dtype=jnp.float32)
        batch = jnp.repeat(jnp.arange(G, dtype=jnp.int32), NPG)
        batch_num = jnp.full((G,), NPG, dtype=jnp.int32)
        s = 1.0 / np.sqrt(D)
        W1 = jax.random.uniform(ks[3], (D, D), jnp.float32, -s, s)
        W2 = jax.random.uniform(ks[4], (D, D), jnp.float32, -s, s)
        Wo = jax.random.uniform(ks[5], (D, D), jnp.float32, -s, s)
        Wn = jax.random.uniform(ks[6], (D, D), jnp.float32, -s, s)
        gamma = jnp.ones((D,), jnp.float32)
        beta = jnp.zeros((D,), jnp.float32)
        return {'x': x, 'edge_index': edge_index, 'w': w, 'batch': batch, 'batch_num': batch_num, 'W1': W1, 'W2': W2, 'Wo': Wo, 'Wn': Wn, 'gamma': gamma, 'beta': beta}
    _L0_gnn_all = _L0_gnn_setup()
    _L0_gnn_in = {k: v for k, v in _L0_gnn_all.items() if k in ('batch_num', 'W1', 'W2', 'Wo', 'Wn', 'gamma', 'beta')}
    del _L0_gnn_all

    def _L1_gnn_setup():
        import jax, jax.numpy as jnp
        import numpy as np
        N, F_IN, F_OUT, H, E = (50000, 128, 32, 4, 50000)
        key = jax.random.key(seed)
        ks = jax.random.split(key, 8)
        features = jax.random.normal(ks[0], (N, F_IN), dtype=jnp.float32)
        edge_src = jax.random.randint(ks[1], (E,), 0, N, dtype=jnp.int32)
        edge_dst = jax.random.randint(ks[2], (E,), 0, N, dtype=jnp.int32)
        W_w = jax.random.normal(ks[3], (F_IN, F_OUT * H), dtype=jnp.float32) * 0.05
        W_b = jax.random.normal(ks[4], (F_OUT * H,), dtype=jnp.float32) * 0.05
        a_w = jax.random.normal(ks[5], (H, 2 * F_OUT), dtype=jnp.float32) * 0.05
        a_b = jax.random.normal(ks[6], (H,), dtype=jnp.float32) * 0.05
        return {'features': features, 'edge_src': edge_src, 'edge_dst': edge_dst, 'W_w': W_w, 'W_b': W_b, 'a_w': a_w, 'a_b': a_b}
    _L1_gnn_all = _L1_gnn_setup()
    _L1_gnn_in = {k: v for k, v in _L1_gnn_all.items() if k in ('W_w', 'W_b', 'a_w', 'a_b')}
    del _L1_gnn_all

    def _L2_gnn_setup():
        import jax, jax.numpy as jnp
        import numpy as np
        HEADS = 2
        NEG_SLOPE = 0.2
        EPS = 1e-16

        def _gat_layer(x, src, dst, edge_attr_full, W, att, b, ew, eb):
            N, D = x.shape
            H = HEADS
            edge_emb = edge_attr_full @ ew.T + eb
            xw = x @ W
            xj = xw[src].reshape(-1, H, D) + edge_emb.reshape(-1, H, D)
            xi = xw[dst].reshape(-1, H, D)
            att_i, att_j = (att[:, :D], att[:, D:])
            alpha = jnp.einsum('ehd,hd->eh', xi, att_i) + jnp.einsum('ehd,hd->eh', xj, att_j)
            alpha = jax.nn.leaky_relu(alpha, NEG_SLOPE)
            amax = jax.ops.segment_max(alpha, dst, num_segments=N)
            ea = jnp.exp(alpha - amax[dst])
            denom = jax.ops.segment_sum(ea, dst, num_segments=N)
            alpha = ea / (denom[dst] + EPS)
            msg = xj * alpha[..., None]
            aggr = jax.ops.segment_sum(msg, dst, num_segments=N)
            return aggr.mean(axis=1) + b
        N, E, D, F = (10000, 10000, 128, 16)
        key = jax.random.key(seed)
        ks = jax.random.split(key, 8)
        return {'x': jax.random.normal(ks[0], (N, D), dtype=jnp.float32), 'edge_index': jax.random.randint(ks[1], (2, E), 0, N, dtype=jnp.int64), 'edge_attr': jax.random.normal(ks[2], (E, F), dtype=jnp.float32), 'weights': jax.random.normal(ks[3], (5, D, HEADS * D), dtype=jnp.float32) * 0.08, 'atts': jax.random.normal(ks[4], (5, HEADS, 2 * D), dtype=jnp.float32) * 0.08, 'biases': jnp.zeros((5, D), dtype=jnp.float32), 'edge_ws': jax.random.normal(ks[5], (5, HEADS * D, F), dtype=jnp.float32) * 0.2, 'edge_bs': jnp.zeros((5, HEADS * D), dtype=jnp.float32)}
    _L2_gnn_all = _L2_gnn_setup()
    _L2_gnn_in = {k: v for k, v in _L2_gnn_all.items() if k in ('weights', 'atts', 'biases', 'edge_ws', 'edge_bs')}
    del _L2_gnn_all

    def _L3_gnn_setup():
        import jax, jax.numpy as jnp
        import numpy as np
        N_NODES = 50000
        N_EDGES = 25000
        IN_DIM = 128
        HID = 128
        TIME = 6.0
        STEPS = 12
        key = jax.random.key(seed)
        ks = jax.random.split(key, 8)
        gat_out = jax.random.normal(ks[0], (N_NODES, IN_DIM), dtype=jnp.float32)
        edge_index = jax.random.randint(ks[1], (2, N_EDGES), 0, N_NODES, dtype=jnp.int64)
        W_in = jax.random.normal(ks[2], (IN_DIM, HID), dtype=jnp.float32) * (1.0 / np.sqrt(IN_DIM))
        b_in = jnp.zeros((HID,), dtype=jnp.float32)
        W1 = jax.random.normal(ks[3], (HID, 2 * HID), dtype=jnp.float32) * (1.0 / np.sqrt(HID))
        b1 = jnp.zeros((2 * HID,), dtype=jnp.float32)
        W2 = jax.random.normal(ks[4], (2 * HID, HID), dtype=jnp.float32) * (1.0 / np.sqrt(2 * HID))
        b2 = jnp.zeros((HID,), dtype=jnp.float32)
        clearance = jnp.full((1,), 0.1, dtype=jnp.float32)
        return {'gat_out': gat_out, 'edge_index': edge_index, 'W_in': W_in, 'b_in': b_in, 'W1': W1, 'b1': b1, 'W2': W2, 'b2': b2, 'clearance': clearance}
    _L3_gnn_all = _L3_gnn_setup()
    _L3_gnn_in = {k: v for k, v in _L3_gnn_all.items() if k in ('W_in', 'b_in', 'W1', 'b1', 'W2', 'b2', 'clearance')}
    del _L3_gnn_all
    return {'x': x, 'src': src, 'dst': dst, 'edge_attr_16': edge_attr_16, 'edge_weight1': edge_weight1, 'L0_gnn_batch_num': _L0_gnn_in['batch_num'], 'L0_gnn_W1': _L0_gnn_in['W1'], 'L0_gnn_W2': _L0_gnn_in['W2'], 'L0_gnn_Wo': _L0_gnn_in['Wo'], 'L0_gnn_Wn': _L0_gnn_in['Wn'], 'L0_gnn_gamma': _L0_gnn_in['gamma'], 'L0_gnn_beta': _L0_gnn_in['beta'], 'L1_gnn_W_w': _L1_gnn_in['W_w'], 'L1_gnn_W_b': _L1_gnn_in['W_b'], 'L1_gnn_a_w': _L1_gnn_in['a_w'], 'L1_gnn_a_b': _L1_gnn_in['a_b'], 'L2_gnn_weights': _L2_gnn_in['weights'], 'L2_gnn_atts': _L2_gnn_in['atts'], 'L2_gnn_biases': _L2_gnn_in['biases'], 'L2_gnn_edge_ws': _L2_gnn_in['edge_ws'], 'L2_gnn_edge_bs': _L2_gnn_in['edge_bs'], 'L3_gnn_W_in': _L3_gnn_in['W_in'], 'L3_gnn_b_in': _L3_gnn_in['b_in'], 'L3_gnn_W1': _L3_gnn_in['W1'], 'L3_gnn_b1': _L3_gnn_in['b1'], 'L3_gnn_W2': _L3_gnn_in['W2'], 'L3_gnn_b2': _L3_gnn_in['b2'], 'L3_gnn_clearance': _L3_gnn_in['clearance']}

def reference(x, src, dst, edge_attr_16, edge_weight1, L0_gnn_batch_num, L0_gnn_W1, L0_gnn_W2, L0_gnn_Wo, L0_gnn_Wn, L0_gnn_gamma, L0_gnn_beta, L1_gnn_W_w, L1_gnn_W_b, L1_gnn_a_w, L1_gnn_a_b, L2_gnn_weights, L2_gnn_atts, L2_gnn_biases, L2_gnn_edge_ws, L2_gnn_edge_bs, L3_gnn_W_in, L3_gnn_b_in, L3_gnn_W1, L3_gnn_b1, L3_gnn_W2, L3_gnn_b2, L3_gnn_clearance):
    import jax
    import jax.numpy as jnp

    def _L0_gnn_ref(x, edge_index, w, batch, batch_num, W1, W2, Wo, Wn, gamma, beta):
        import jax, jax.numpy as jnp
        import numpy as np
        N = 1250
        E = 20000
        D = 128
        G = 8
        NPG = N // G
        EPS = 1e-06
        SLOPE = 0.01

        def leaky(x):
            return jnp.where(x >= 0, x, SLOPE * x)
        h = leaky(x @ W1) @ W2
        xj = w * h[edge_index[1]]
        xn = leaky(jax.ops.segment_sum(xj, edge_index[0], num_segments=N))
        out = h @ Wo + xn @ Wn
        cnt = batch_num.astype(jnp.float32)[:, None]
        mu = jax.ops.segment_sum(out, batch, num_segments=G) / cnt
        diff = out - mu[batch]
        var = jax.ops.segment_sum(diff * diff, batch, num_segments=G) / (cnt - 1.0)
        sigma = jnp.sqrt(var)
        return diff / (sigma[batch] + EPS) * gamma + beta

    def _L1_gnn_ref(features, edge_src, edge_dst, W_w, W_b, a_w, a_b):
        import jax, jax.numpy as jnp
        import numpy as np
        N, F_IN, F_OUT, H, E = (50000, 128, 32, 4, 50000)
        n = features.shape[0]
        h = a_w.shape[0]
        f_out = a_w.shape[1] // 2
        self_idx = jnp.arange(n, dtype=edge_src.dtype)
        src = jnp.concatenate([edge_src, self_idx])
        dst = jnp.concatenate([edge_dst, self_idx])
        key = (features @ W_w + W_b).reshape(n, h, f_out)
        a_dst = a_w[:, :f_out]
        a_src = a_w[:, f_out:]
        s_dst = jnp.einsum('nhf,hf->nh', key, a_dst)
        s_src = jnp.einsum('nhf,hf->nh', key, a_src)
        e = jax.nn.leaky_relu(s_dst[dst] + s_src[src] + a_b, negative_slope=0.2)
        m = jax.ops.segment_max(e, dst, num_segments=n)
        e_exp = jnp.exp(e - m[dst])
        denom = jax.ops.segment_sum(e_exp, dst, num_segments=n)
        alpha = e_exp / denom[dst]
        out = jax.ops.segment_sum(alpha[:, :, None] * key[src], dst, num_segments=n)
        return out.reshape(n, h * f_out)

    def _L2_gnn_ref(x, edge_index, edge_attr, weights, atts, biases, edge_ws, edge_bs):
        import jax, jax.numpy as jnp
        import numpy as np
        HEADS = 2
        NEG_SLOPE = 0.2
        EPS = 1e-16

        def _gat_layer(x, src, dst, edge_attr_full, W, att, b, ew, eb):
            N, D = x.shape
            H = HEADS
            edge_emb = edge_attr_full @ ew.T + eb
            xw = x @ W
            xj = xw[src].reshape(-1, H, D) + edge_emb.reshape(-1, H, D)
            xi = xw[dst].reshape(-1, H, D)
            att_i, att_j = (att[:, :D], att[:, D:])
            alpha = jnp.einsum('ehd,hd->eh', xi, att_i) + jnp.einsum('ehd,hd->eh', xj, att_j)
            alpha = jax.nn.leaky_relu(alpha, NEG_SLOPE)
            amax = jax.ops.segment_max(alpha, dst, num_segments=N)
            ea = jnp.exp(alpha - amax[dst])
            denom = jax.ops.segment_sum(ea, dst, num_segments=N)
            alpha = ea / (denom[dst] + EPS)
            msg = xj * alpha[..., None]
            aggr = jax.ops.segment_sum(msg, dst, num_segments=N)
            return aggr.mean(axis=1) + b
        N = x.shape[0]
        E = edge_index.shape[1]
        F = edge_attr.shape[1]
        loop = jnp.arange(N, dtype=edge_index.dtype)
        src = jnp.concatenate([edge_index[0], loop])
        dst = jnp.concatenate([edge_index[1], loop])
        edge_attr_full = jnp.concatenate([edge_attr, jnp.zeros((N, F), dtype=edge_attr.dtype)], axis=0)
        h = x
        for l in range(5):
            h = _gat_layer(h, src, dst, edge_attr_full, weights[l], atts[l], biases[l], edge_ws[l], edge_bs[l])
            if l < 4:
                h = jax.nn.relu(h)
        return h

    def _L3_gnn_ref(gat_out, edge_index, W_in, b_in, W1, b1, W2, b2, clearance):
        import jax, jax.numpy as jnp
        import numpy as np
        N_NODES = 50000
        N_EDGES = 25000
        IN_DIM = 128
        HID = 128
        TIME = 6.0
        STEPS = 12
        N = gat_out.shape[0]
        dt = TIME / STEPS
        src, dst = (edge_index[0], edge_index[1])
        h = jnp.tanh(gat_out @ W_in + b_in)
        deg = jax.ops.segment_sum(jnp.ones((src.shape[0],), dtype=h.dtype), dst, num_segments=N)
        deg = jnp.clip(deg, 1.0, None)[:, None]
        decay = jax.nn.relu(clearance)

        def step(h, _):
            agg = jax.ops.segment_sum(h[src], dst, num_segments=N) / deg
            diff = jnp.tanh(jax.nn.gelu(agg @ W1 + b1, approximate=False) @ W2 + b2)
            h = h + (diff - decay * h) * dt
            return (h, None)
        h, _ = jax.lax.scan(step, h, None, length=STEPS)
        return h
    edge_index = jnp.stack([src, dst])
    batch0 = jnp.zeros((1250,), jnp.int32)
    h = jnp.maximum(_layernorm(x, axis=-1), 0.0)
    x = x + _L0_gnn_ref(h, edge_index, edge_weight1, batch0, L0_gnn_batch_num, L0_gnn_W1, L0_gnn_W2, L0_gnn_Wo, L0_gnn_Wn, L0_gnn_gamma, L0_gnn_beta)
    h = jnp.maximum(_layernorm(x, axis=-1), 0.0)
    x = x + _L1_gnn_ref(h, src, dst, L1_gnn_W_w, L1_gnn_W_b, L1_gnn_a_w, L1_gnn_a_b)
    h = jnp.maximum(_layernorm(x, axis=-1), 0.0)
    x = x + _L2_gnn_ref(h, edge_index, edge_attr_16, L2_gnn_weights, L2_gnn_atts, L2_gnn_biases, L2_gnn_edge_ws, L2_gnn_edge_bs)
    h = jnp.maximum(_layernorm(x, axis=-1), 0.0)
    x = x + _L3_gnn_ref(h, edge_index, L3_gnn_W_in, L3_gnn_b_in, L3_gnn_W1, L3_gnn_b1, L3_gnn_W2, L3_gnn_b2, L3_gnn_clearance)
    return x

_drawn_inputs = setup_inputs


def setup_inputs(seed=0):
    import zlib

    import numpy as np

    out = dict(_drawn_inputs(seed))
    spreads = {'L0_gnn_gamma': (1.0, 0.2),
     'L0_gnn_beta': (0.0, 0.1),
     'L2_gnn_biases': (0.0, 0.1),
     'L2_gnn_edge_bs': (0.0, 0.1),
     'L3_gnn_b_in': (0.0, 0.1),
     'L3_gnn_b1': (0.0, 0.1),
     'L3_gnn_b2': (0.0, 0.1)}
    factors = {'edge_weight1': 4.061, 'L1_gnn_a_w': 8.0, 'L1_gnn_a_b': 8.0}
    for name, (base, spread) in spreads.items():
        noise = np.random.default_rng([zlib.crc32(name.encode()), seed]).standard_normal(out[name].shape)
        drawn = base * np.exp(spread * noise) if base else spread * noise
        out[name] = jnp.asarray(drawn.astype(out[name].dtype))
    for name, factor in factors.items():
        out[name] = (out[name] * factor).astype(out[name].dtype)
    return out
```

```python
from contextlib import ExitStack

import concourse.bass as bass
from concourse import mybir

F32 = mybir.dt.float32
BF16 = mybir.dt.bfloat16
F16 = mybir.dt.float16
I32 = mybir.dt.int32
ALU = mybir.AluOpType
ACT = mybir.ActivationFunctionType
AX_X = mybir.AxisListType.X

P = 128
BIG = 1.0e30
NA = 17
REC = 24
(R_SHI, R_SLO, R_DHI, R_DLO, R_W, R_ORIG, R_SRC, R_ATTR) = range(8)
R_REAL = R_ATTR + NA - 1
RING = 6


class Chain:

    def __init__(self, eng, done, start=0):
        self.eng, self.done, self.start, self.n = eng, done, start, 0

    def step(self, ins):
        self.n += 1
        ins.then_inc(self.done, 1)
        self.eng.wait_ge(self.done, self.start + self.n)


class Lot:

    def __init__(self, area):
        self.area, self.at = area, 0

    def take(self, shape, dt=F32):
        n = 1
        for k in shape[1:]:
            n *= k
        size = mybir.dt.size(dt) * n
        view = self.area[0:shape[0], self.at // 2:(self.at + size) // 2].bitcast(dt)
        self.at += -(-size // 32) * 32
        assert self.at <= 2 * self.area.shape[1]
        names = "abcd"[:len(shape) - 1]
        return view.rearrange(f"p ({' '.join(names)}) -> p {' '.join(names)}", **dict(zip(names, shape[1:])))


class Graph:
    pass


class Stage:

    def __init__(self, nc):
        self.nc, self.first = nc, min(nc.free_semaphores)
        self.used, self.held = 0, ExitStack()

    def sem(self, name):
        self.used += 1
        return self.held.enter_context(self.nc.semaphore(name, num=self.first + self.used - 1))

    def clear(self):
        self.nc.gpsimd.sem_clear(range(self.first, self.first + self.used))
        self.nc.all_engine_barrier()

    def end(self):
        if self.used:
            self.clear()
        self.held.close()
        self.used, self.held = 0, ExitStack()


def graph_kernel(nc, a, out):
    N, D = a["x"].shape
    E = a["src"].shape[0]
    T = -(-N // P)
    LAST = N - (T - 1) * P
    NP = T * P
    EA = E + N
    UP = 125
    UE, UN = E // UP, N // UP
    UC = UE + UN
    assert UP * UE == E and UP * UN == N and UC % 10 == 0
    USED = (EA + T * (P - 1)) // P
    CH = -(-USED // RING) * RING
    G = 2
    GC = 96
    NCH = G * GC
    assert CH <= NCH
    H1, F1 = a["L1_gnn_a_w"].shape[0], a["L1_gnn_a_w"].shape[1] // 2
    L, _, HF2 = a["L2_gnn_weights"].shape
    H2, F2 = a["L2_gnn_atts"].shape[1], a["L2_gnn_atts"].shape[2] // 2
    HID = a["L3_gnn_W1"].shape[1]
    STEPS, DT = 12, 0.5
    AT = H2 * NA
    ATT0 = 5 * 512

    table = nc.dram_tensor("node_rows", [NP, HF2], F32).ap()
    table1 = nc.dram_tensor("node_rows_narrow", [NP, D], F32).ap()
    sorted_d = nc.dram_tensor("sorted_edges", [NCH * P, REC], F32).ap()

    ctx = ExitStack()
    with ctx:
        def sb(name, shape, dt=F32):
            return ctx.enter_context(nc.sbuf_tensor(name, shape, dt))

        ps = ctx.enter_context(nc.psum_tensor("ps", [P, 4096], F32))

        lane = sb("lane", [P, P])
        lane16 = sb("lane16", [P, P], BF16)
        part = sb("part", [P, 1])
        ident = sb("ident", [P, P])
        ident16 = sb("ident16", [P, P], F16)
        identb = sb("identb", [P, P], BF16)
        upper = sb("upper", [P, P])
        lower = sb("lower", [P, P])
        ones = sb("ones", [P, P])
        zerob = sb("zerob", [P, 512], BF16)
        tens = sb("tens", [P, 10])
        nodeid = sb("nodeid", [P, NP], F16)
        chunkid = sb("chunkid", [P, NCH])
        x = sb("x_sb", [P, T, D])
        h = sb("h_sb", [P, T, D])
        hT = sb("hT", [P, NP])
        wide = sb("wide", [P, T, HF2])
        small = sb("small", [P, T, 8])
        stat = sb("stat", [P, 4, T])
        rec = sb("rec", [P, NCH, REC])
        onehotT = sb("onehotT", [P, 2, NCH * P], BF16)
        himask = sb("himask", [P, NCH, 2, T], BF16)
        idx = sb("idx", [P, 2, NCH], I32)
        round_tiles = sb("round_tiles", [P, NCH // RING], I32)
        tile_end = sb("tile_end", [P, T], I32)
        ring = sb("ring", [P, RING, HF2])
        slot_idx = sb("slot_idx", [P, RING], I32)
        scratch = sb("scratch", [P, 3600])
        carry_in = sb("carry_in", [4, 2, NCH])
        carry_on = sb("carry_on", [4, 2, NCH])
        reset = sb("reset", [GC, 2, 4, G, P], BF16)
        unreal = sb("unreal", [P, NCH])
        logits = sb("logits", [P, NCH, 4])
        attr_part = sb("attr_part", [P, NCH, L * H2])
        w0 = logits[:].rearrange("p c h -> p (c h)")[:, 0:4 * D].rearrange("p (n d) -> p n d", n=4)
        w1x = sb("w1x", [P, D + 2 * H1])
        w2x = sb("w2x", [P, L, HF2 + 2 * H2])
        ew = sb("ew", [AT, L, D])
        bias1 = sb("bias1", [P, D + 2 * H1])
        ab1 = sb("ab1", [P, H1])
        bias2 = sb("bias2", [P, L, D])
        floor2 = sb("floor2", [P, L])
        cols = sb("cols", [P, 8])

        g = Graph()
        g.nc, g.a, g.out, g.N, g.D, g.T = nc, a, out, N, D, T
        g.LAST, g.NP, g.E, g.EA, g.UP, g.UE = LAST, NP, E, EA, UP, UE
        g.UN, g.UC, g.CH, g.G, g.GC, g.NCH = UN, UC, CH, G, GC, NCH
        g.H1, g.F1, g.H2, g.F2, g.L, g.HF2 = H1, F1, H2, F2, L, HF2
        g.HID, g.STEPS, g.DT, g.AT, g.ATT0, g.table = HID, STEPS, DT, AT, ATT0, table
        g.table1, g.sorted_d, g.ps, g.lane, g.lane16, g.part = table1, sorted_d, ps, lane, lane16, part
        g.ident, g.ident16, g.identb, g.upper, g.lower, g.ones = ident, ident16, identb, upper, lower, ones
        g.zerob, g.tens, g.nodeid, g.chunkid, g.x, g.h = zerob, tens, nodeid, chunkid, x, h
        g.hT, g.wide, g.small, g.stat, g.rec, g.onehotT = hT, wide, small, stat, rec, onehotT
        g.himask, g.idx, g.round_tiles, g.tile_end, g.ring, g.slot_idx, g.scratch = himask, idx, round_tiles, tile_end, ring, slot_idx, scratch
        g.carry_in, g.carry_on, g.reset, g.unreal, g.logits, g.attr_part = carry_in, carry_on, reset, unreal, logits, attr_part
        g.w0, g.w1x, g.w2x, g.ew, g.bias1, g.ab1 = w0, w1x, w2x, ew, bias1, ab1
        g.bias2, g.floor2, g.cols = bias2, floor2, cols
        g.chunk_rows = sorted_d.rearrange("(c p) k -> p c k", p=P)
        g.got = [ctx.enter_context(nc.semaphore(f"gathered{k}")) for k in range(RING)]
        g.put = [ctx.enter_context(nc.semaphore(f"scattered{k}")) for k in range(2)]
        g.gathered = 0
        g.stage = Stage(nc)
        g.sem = g.stage.sem
        g.scan_a, g.scan_b = h[:].rearrange("p t d -> p (t d)"), hT[:]
        for work in (constants, sort_edges, sorted_views, weights, norm0, block0, norm1, block1, norm2, block2, norm3, block3):
            work(g)
            g.stage.end()
    return nc


def norm0(g):
    node_norm(g, "n0")


def norm1(g):
    node_norm(g, "n1")


def norm2(g):
    node_norm(g, "n2")


def norm3(g):
    node_norm(g, "n3")


def constants(g):
    nc = g.nc
    made, split, xin = g.sem("const_made"), g.sem("const_dve"), g.sem("x_loaded")
    T, LAST, NP = g.T, g.LAST, g.NP
    with nc.Block(name="constants") as block:
        @block.gpsimd
        def _(pool):
            pool.iota(g.lane[:], [[1, P]], base=1, channel_multiplier=0, allow_small_or_imprecise_dtypes=True)
            pool.iota(g.lane16[:], [[1, P]], base=1, channel_multiplier=0, allow_small_or_imprecise_dtypes=True)
            pool.iota(g.part[:], [[0, 1]], base=1, channel_multiplier=1, allow_small_or_imprecise_dtypes=True)
            pool.iota(g.tens[:], [[1, T]], base=0, channel_multiplier=0, allow_small_or_imprecise_dtypes=True)
            pool.iota(g.nodeid[:], [[1, NP]], base=0, channel_multiplier=0, allow_small_or_imprecise_dtypes=True)
            pool.iota(g.chunkid[:], [[1, g.NCH]], base=0, channel_multiplier=0,
                      allow_small_or_imprecise_dtypes=True).then_inc(made, 1)

        @block.vector
        def _(dve):
            dve.memset(g.x[:, T - 1, :], 0.0).then_inc(split, 1)
            dve.memset(g.ones[:], 1.0)
            dve.memset(g.zerob[:], 0.0)
            dve.wait_ge(made, 1)
            for out, op in ((g.ident, ALU.is_equal), (g.ident16, ALU.is_equal), (g.identb, ALU.is_equal),
                            (g.upper, ALU.is_gt), (g.lower, ALU.is_lt)):
                dve.tensor_scalar(out[:], g.lane[:], g.part[:, 0:1], None, op)

        @block.sync
        def _(sp):
            sp.dma_start(g.x[:, 0:T - 1, :], g.a["x"][0:(T - 1) * P, :].rearrange("(t p) d -> p t d", p=P)).then_inc(xin, 16)
            sp.wait_ge(split, 1)
            sp.dma_start(g.x[0:LAST, T - 1, :], g.a["x"][(T - 1) * P:, :]).then_inc(xin, 16)
            sp.wait_ge(xin, 32)


def sort_edges(g):
    nc, a = g.nc, g.a
    UP, UC, UE, UN, T, NCH = g.UP, g.UC, g.UE, g.UN, g.T, g.NCH
    B = 5
    PAIRS = UC // (2 * B)
    rec, scr = g.rec, g.scratch
    s_in, s_self, s_dve = g.sem("sort_in"), g.sem("sort_self"), g.sem("sort_dve")
    s_hot, s_tr, s_ev = g.sem("sort_onehot"), g.sem("sort_transposed"), g.sem("sort_evacuated")
    s_cnt, s_base, s_look, s_rank = g.sem("sort_counted"), g.sem("sort_base"), g.sem("sort_looked"), g.sem("sort_ranked")
    s_zero, s_pos = g.sem("sort_zeroed"), g.sem("sort_positions")
    s_put = g.put
    s_stage, s_round = g.sem("sort_staged"), g.sem("sort_put_round")

    if True:
        lot = Lot(g.onehotT[:, 1, :])

        def sb(name, shape, dt=F32):
            return lot.take(shape, dt)
        ends_i = sb("ends_i", [P, 2, UC], I32)
        digits_i = sb("digits_i", [P, 4, UC], I32)
        attr_in = sb("attr_in", [P, UE, 16])
        w_in = sb("w_in", [P, UE])
        dst16 = sb("dst16", [P, UC], F16)
        dstf = sb("dstf", [P, UC])
        dhi = sb("dhi", [P, UC, T], BF16)
        hot = sb("hot", [P, 2, B, P], BF16)
        before = sb("before", [P, 2, UC, T], BF16)
        rank = sb("rank", [P, UC])
        eqs = sb("eqs", [P, 2, B, P], BF16)
        pos = sb("pos", [P, UC], I32)
        posf = sb("posf", [P, UC])
        stage = sb("stage", [P, 2, RING, REC])
        stage_i = sb("stage_i", [P, 2, RING], I32)
        nch = sb("nch", [P, 6, T])
        nch_i = sb("nch_i", [P, T], I32)
        tilef = sb("tilef", [P, NCH])
        past = sb("past", [P, NCH, T])
        packed = sb("packed", [P, NCH // RING])
        cnt = scr[:, 0:UC * T].rearrange("p (c t) -> p c t", t=T)
        cum = scr[:, UC * T:2 * UC * T].rearrange("p (c t) -> p c t", t=T)
        picked = g.wide[:].rearrange("p t f -> p (t f)")[:, 0:UC * T].rearrange("p (c t) -> p c t", t=T)
        hotT = g.onehotT[:, 0, 0:UC * P].rearrange("p (c e) -> p c e", e=P)
        bank = [g.ps[:, 512 * k:512 * k + 512] for k in range(8)]

        with nc.Block(name="sort") as block:
            @block.sync
            def _(sp):
                sp.dma_start(ends_i[0:UP, 1, 0:UE], a["dst"].rearrange("(p c) -> p c", c=UE)).then_inc(s_in, 16)
                sp.dma_start(ends_i[0:UP, 0, 0:UE], a["src"].rearrange("(p c) -> p c", c=UE)).then_inc(s_in, 16)
                sp.dma_start(w_in[0:UP, :], a["edge_weight1"].rearrange("(p c) o -> p (c o)", c=UE)).then_inc(s_in, 16)
                sp.dma_start(attr_in[0:UP], a["edge_attr_16"].rearrange("(p c) k -> p c k", c=UE)).then_inc(s_in, 16)
                sp.wait_ge(s_zero, 1)
                sp.dma_start(g.sorted_d.rearrange("(p c) k -> p (c k)", p=P),
                             rec[:].rearrange("p c k -> p (c k)")).then_inc(s_zero, 16)
                sp.wait_ge(s_zero, 17)

            @block.gpsimd
            def _(pool):
                for side in range(2):
                    last = pool.iota(ends_i[0:UP, side, UE:UC], [[1, UN]], base=0, channel_multiplier=UN)
                last.then_inc(s_self, 1)
                with pool.Fori(0, UC // (2 * RING)) as i:
                    for u in range(2):
                        pool.wait_ge(s_zero, 17)
                        pool.wait_ge(s_stage, 2 * i + u + 1)
                        pool.sem_inc(s_round, 1)
                        for k in range(RING):
                            pool.indirect_dma_start(g.sorted_d, bass.IndirectOffsetOnAxis(ap=stage_i[0:UP, u, k:k + 1], axis=0),
                                                    stage[0:UP, u, k, :], None).then_inc(s_put[u], 16)
                for u in range(2):
                    pool.wait_ge(s_put[u], 16 * RING * (UC // (2 * RING)))

            @block.vector
            def _(dve):
                c = Chain(dve, s_dve)
                dve.memset(rec[:], 0.0).then_inc(s_zero, 1)
                dve.wait_ge(s_in, 64)
                dve.wait_ge(s_self, 1)
                for side in range(2):
                    dve.tensor_scalar(digits_i[0:UP, 2 * side, :], ends_i[0:UP, side, :], 7, None, ALU.arith_shift_right)
                    last = dve.tensor_scalar(digits_i[0:UP, 2 * side + 1, :], ends_i[0:UP, side, :], P - 1, None, ALU.bitwise_and)
                c.step(last)
                dve.wait_ge(s_zero, 17)
                for f, d in ((R_SHI, 0), (R_SLO, 1), (R_DHI, 2)):
                    dve.tensor_copy(rec[0:UP, 0:UC, f], digits_i[0:UP, d, :])
                dve.tensor_scalar(rec[0:UP, 0:UC, R_DLO], digits_i[0:UP, 3, :], 1.0, None, ALU.add)
                dve.tensor_copy(rec[0:UP, 0:UC, R_SRC], ends_i[0:UP, 0, :])
                dve.tensor_copy(rec[0:UP, 0:UE, R_W], w_in[0:UP, :])
                dve.memset(rec[0:UP, 0:UE, R_ORIG], 1.0)
                dve.memset(rec[0:UP, 0:UC, R_REAL], 1.0)
                dve.tensor_copy(rec[0:UP, 0:UE, R_ATTR:R_ATTR + 16], attr_in[0:UP])
                dve.tensor_copy(dst16[0:UP, :], ends_i[0:UP, 1, :])
                c.step(dve.tensor_copy(dstf[0:UP, :], ends_i[0:UP, 1, :]))
                c.step(dve.tensor_tensor(dhi[0:UP], g.tens[0:UP, :].unsqueeze(1).broadcast_to([UP, UC, T]),
                                         rec[0:UP, 0:UC, R_DHI].unsqueeze(2).broadcast_to([UP, UC, T]), ALU.is_equal))
                with dve.Fori(0, PAIRS) as i:
                    for u in range(2):
                        dve.wait_ge(s_cnt, 2 * i + u + 1)
                        dve.tensor_tensor(hot[0:UP, u], g.lane16[0:UP, :].unsqueeze(1).broadcast_to([UP, B, P]),
                                          rec[0:UP, bass.ds((2 * i + u) * B, B), R_DLO].unsqueeze(2).broadcast_to([UP, B, P]),
                                          ALU.is_equal).then_inc(s_hot, 1)
                dve.wait_ge(s_ev, 2 + 2 * PAIRS)
                for t in range(T):
                    last = dve.tensor_tensor_scan(cum[:, :, t], g.ones[:, 0:1].broadcast_to([P, UC]), cnt[:, :, t],
                                                  0.0, ALU.mult, ALU.add)
                last.then_inc(s_base, 1)
                dve.wait_ge(s_look, 1)
                dve.tensor_copy(nch[:, 0, :], bank[0][:, 0:T])
                c.step(dve.tensor_scalar(nch_i[:], bank[1][:, 0:T], float(P - 1), None, ALU.add))
                c.step(dve.tensor_scalar(nch_i[:], nch_i[:], 7, None, ALU.arith_shift_right))
                c.step(dve.tensor_copy(nch[:, 1, :], nch_i[:]))
                c.step(dve.tensor_tensor_scan(nch[:, 2, :], g.ones[:, 0:T], nch[:, 1, :], 0.0, ALU.mult, ALU.add))
                c.step(dve.tensor_tensor(nch[:, 3, :], nch[:, 2, :], nch[:, 1, :], ALU.subtract))
                c.step(dve.scalar_tensor_tensor(nch[:, 4, :], nch[:, 3, :], float(P), nch[:, 0, :], ALU.mult, ALU.add))
                c.step(dve.tensor_tensor(cum, cum, cnt, ALU.subtract))
                c.step(dve.tensor_tensor(cum, cum, nch[:, 4, :].unsqueeze(1).broadcast_to([P, UC, T]), ALU.add))
                c.step(dve.tensor_copy(before[:, 0], cum))
                dve.tensor_tensor(before[:, 1], cum, before[:, 0], ALU.subtract).then_inc(s_base, 1)
                c.step(dve.tensor_tensor(past[:, :, 0:T - 1], g.chunkid[:].unsqueeze(2).broadcast_to([P, NCH, T - 1]),
                                         nch[:, 2, 0:T - 1].unsqueeze(1).broadcast_to([P, NCH, T - 1]), ALU.is_ge))
                c.step(dve.tensor_reduce(tilef[:], past[:, :, 0:T - 1], AX_X, ALU.add))
                tiles = tilef.rearrange("p (r k) -> p r k", k=RING)
                for k in range(RING - 2, -1, -1):
                    c.step(dve.scalar_tensor_tensor(packed, packed if k < RING - 2 else tiles[:, :, RING - 1], 16.0, tiles[:, :, k],
                                                    ALU.mult, ALU.add))
                dve.tensor_copy(g.round_tiles[:], packed)
                dve.tensor_copy(g.tile_end[:, 0:T - 1], nch[:, 2, 0:T - 1])
                dve.memset(g.tile_end[:, T - 1:T], g.CH)
                with dve.Fori(0, PAIRS) as i:
                    for u in range(2):
                        dve.wait_ge(s_look, 2 * i + u + 2)
                        for k in range(B):
                            col = (2 * i + u) * B + k
                            dve.scalar_tensor_tensor(eqs[0:UP, u, k, 0:UP], bank[2 + 3 * u + k // 4][0:UP, (k % 4) * P:(k % 4) * P + UP],
                                                     dstf[0:UP, bass.ds(col, 1)], g.lower[0:UP, 0:UP], ALU.is_equal, ALU.mult,
                                                     accum_out=rank[0:UP, bass.ds(col, 1)])
                        dve.tensor_tensor(picked[0:UP, bass.ds((2 * i + u) * B, B), :],
                                          bank[4 + 3 * u][0:UP, 0:B * T].rearrange("p (c t) -> p c t", t=T),
                                          dhi[0:UP, bass.ds((2 * i + u) * B, B), :], ALU.mult).then_inc(s_rank, 1)
                dve.wait_ge(s_rank, 2 + 2 * PAIRS)
                c.step(dve.tensor_reduce(posf[0:UP, :], picked[0:UP], AX_X, ALU.add))
                c.step(dve.tensor_tensor(pos[0:UP, :], posf[0:UP, :], rank[0:UP, :], ALU.add))
                for u in range(2):
                    dve.tensor_copy(stage_i[0:UP, u, :], pos[0:UP, u * RING:(u + 1) * RING])
                    dve.tensor_copy(stage[0:UP, u], rec[0:UP, u * RING:(u + 1) * RING, :]).then_inc(s_stage, 1)
                with dve.Fori(1, UC // (2 * RING)) as i:
                    for u in range(2):
                        dve.wait_ge(s_put[u], 16 * RING * i)
                        dve.tensor_copy(stage_i[0:UP, u, :], pos[0:UP, bass.ds((2 * i + u) * RING, RING)])
                        dve.tensor_copy(stage[0:UP, u], rec[0:UP, bass.ds((2 * i + u) * RING, RING), :]).then_inc(s_stage, 1)

            @block.tensor
            def _(pe):
                pe.sem_inc(s_cnt, 2)
                pe.wait_ge(s_dve, 1)
                with pe.Fori(0, PAIRS) as i:
                    for u in range(2):
                        pe.wait_ge(s_hot, 2 * i + u + 1)
                        pe.wait_ge(s_ev, 2 * i + u + 1)
                        turned = bank[2 + u].bitcast(BF16)
                        for k in range(B):
                            pe.transpose(turned[:, k * P:k * P + UP], hot[0:UP, u, k, :], g.identb[0:UP, 0:UP])
                        for k in range(B):
                            mm = pe.matmul(bank[4 + u][:, k * T:(k + 1) * T], hot[0:UP, u, k, :],
                                           dhi[0:UP, bass.ds((2 * i + u) * B + k, 1), :].rearrange("p o t -> p (o t)"), start=True, stop=True)
                        mm.then_inc(s_cnt, 1)
                pe.wait_ge(s_base, 1)
                pe.wait_ge(s_ev, 2 + 2 * PAIRS)
                pe.matmul(bank[0][:, 0:T], g.upper[:], cum[:, UC - 1, :], start=True, stop=True)
                pe.matmul(bank[1][:, 0:T], g.ones[:], cum[:, UC - 1, :], start=True, stop=True).then_inc(s_look, 1)
                pe.sem_inc(s_rank, 2)
                pe.wait_ge(s_base, 2)
                with pe.Fori(0, PAIRS) as i:
                    for u in range(2):
                        pe.wait_ge(s_rank, 2 * i + u + 1)
                        for k in range(B):
                            col = (2 * i + u) * B + k
                            for p in range(2):
                                pe.matmul(bank[4 + 3 * u][0:UP, k * T:(k + 1) * T],
                                          hotT[:, bass.ds(col, 1), 0:UP].rearrange("p o e -> p (o e)"),
                                          before[:, p, bass.ds(col, 1), :].rearrange("p o t -> p (o t)"), start=p == 0, stop=p == 1)
                            mm = pe.matmul(bank[2 + 3 * u + k // 4][0:UP, (k % 4) * P:(k % 4) * P + UP],
                                           dst16[0:UP, bass.ds(col, 1)].broadcast_to([UP, UP]), g.ident16[0:UP, 0:UP],
                                           start=True, stop=True)
                        mm.then_inc(s_look, 1)

            @block.scalar
            def _(act):
                act.sem_inc(s_ev, 2)
                with act.Fori(0, PAIRS) as i:
                    for u in range(2):
                        act.wait_ge(s_cnt, 2 * i + u + 3)
                        turned = bank[2 + u].bitcast(BF16)[:, 0:B * P].rearrange("p (c e) -> p c e", e=P)
                        act.copy(hotT[:, bass.ds((2 * i + u) * B, B), 0:UP], turned[:, :, 0:UP])
                        act.copy(cnt[:, bass.ds((2 * i + u) * B, B), :],
                                 bank[4 + u][:, 0:B * T].rearrange("p (c t) -> p c t", t=T)).then_inc(s_ev, 1)


def sorted_views(g):
    nc = g.nc
    P_, T, NCH, GC, G = P, g.T, g.NCH, g.GC, g.G
    rec = g.rec
    B = 3
    BATCHES = NCH // (2 * B)
    s_rec, s_dve, s_hot, s_tr, s_ev = (g.sem(f"view_{n}") for n in ("records", "dve", "onehot", "turned", "copied"))
    s_dst, s_rows, s_near, s_inner, s_carry = (g.sem(f"view_{n}") for n in ("dst", "dst_rows", "first_last", "inner", "carry"))
    bank = [g.ps[:, 512 * k:512 * k + 512] for k in range(8)]
    lot = Lot(g.scratch[:].bitcast(BF16))
    hot = lot.take([P, 2, 2, B, P], BF16)
    dstf = lot.take([P, NCH])
    ends = lot.take([P, 2, 4])
    dstrow = lot.take([P, G, P])
    inner = lot.take([P, G, 4])
    near = lot.take([P, 2, NCH])

    with nc.Block(name="views") as block:
        @block.sync
        def _(sp):
            sp.dma_start(rec[:], g.chunk_rows).then_inc(s_rec, 16)
            sp.wait_ge(s_rec, 16)

        @block.vector
        def _(dve):
            c = Chain(dve, s_dve)
            dve.tensor_scalar(ends[:, 0, :], g.part[:, 0:1].broadcast_to([P, 4]), 1.0, None, ALU.is_equal)
            dve.tensor_scalar(ends[:, 1, :], g.part[:, 0:1].broadcast_to([P, 4]), float(P), None, ALU.is_equal)
            dve.wait_ge(s_rec, 16)
            dve.tensor_copy(g.idx[:, 0, :], rec[:, :, R_SRC])
            dve.tensor_scalar(g.unreal[:], rec[:, :, R_REAL], -1.0, BIG, ALU.add, ALU.mult)
            dve.scalar_tensor_tensor(dstf, rec[:, :, R_DHI], float(P), rec[:, :, R_DLO], ALU.mult, ALU.add).then_inc(s_dst, 1)
            dve.wait_ge(s_dst, 1)
            dve.tensor_scalar(g.idx[:, 1, :], dstf, -1.0, 0.0, ALU.add, ALU.max)
            for side, field in ((0, R_DHI), (1, R_SHI)):
                dve.tensor_tensor(g.himask[:, :, side, :], g.tens[:].unsqueeze(1).broadcast_to([P, NCH, T]),
                                  rec[:, :, field].unsqueeze(2).broadcast_to([P, NCH, T]), ALU.is_equal)
            with dve.Fori(0, BATCHES) as i:
                for u in range(2):
                    dve.wait_ge(s_tr, 2 * i + u + 1)
                    chunks = bass.ds((2 * i + u) * B, B)
                    dve.tensor_tensor(hot[:, u, 0], g.lane16[:].unsqueeze(1).broadcast_to([P, B, P]),
                                      rec[:, chunks, R_DLO].unsqueeze(2).broadcast_to([P, B, P]), ALU.is_equal)
                    for k in range(B):
                        last = dve.tensor_scalar(hot[:, u, 1, k, :], g.nodeid[:, 0:P], rec[:, bass.ds((2 * i + u) * B + k, 1), R_SLO],
                                                 None, ALU.is_equal)
                    last.then_inc(s_hot, 1)
            dve.wait_ge(s_rows, 1)
            rows = bank[6][0:GC, 0:G * P].rearrange("p (g e) -> p g e", g=G)
            c.step(dve.tensor_copy(dstrow[0:GC], rows))
            fwd, bwd = g.reset[:, 0, 0], g.reset[:, 1, 0]
            for way, own, nxt, edge in ((fwd, slice(1, P), slice(0, P - 1), 0), (bwd, slice(0, P - 1), slice(1, P), P - 1)):
                dve.tensor_tensor(way[:, :, own], dstrow[0:GC, :, own], dstrow[0:GC, :, nxt], ALU.not_equal)
                last = dve.memset(way[:, :, edge:edge + 1], 1.0)
            c.step(last)
            for way in (fwd, bwd):
                last = dve.tensor_scalar(way, way, -BIG, None, ALU.mult)
            c.step(last)
            for hd in range(1, 4):
                for d in range(2):
                    dve.tensor_copy(g.reset[:, d, hd], g.reset[:, d, 0])
            for k in range(4):
                last = dve.tensor_reduce(inner[0:GC, :, k], fwd[:, :, 1:P], AX_X, ALU.min)
            last.then_inc(s_inner, 1)
            dve.wait_ge(s_near, 1)
            c.step(dve.tensor_copy(near[0:4], bank[7][0:4, 0:2 * NCH].rearrange("p (s c) -> p s c", s=2)))
            dve.memset(g.carry_in[:, 0, 0:1], 1.0)
            dve.memset(g.carry_in[:, 1, NCH - 1:NCH], 1.0)
            for at in (slice(1, NCH), slice(0, NCH - 1)):
                last = dve.tensor_tensor(g.carry_in[:, 0 if at.start else 1, at], near[0:4, 0, 1:NCH], near[0:4, 1, 0:NCH - 1],
                                         ALU.not_equal)
            c.step(last)
            c.step(dve.tensor_scalar(g.carry_in[:], g.carry_in[:], -BIG, None, ALU.mult))
            dve.wait_ge(s_carry, 1)
            for d in range(2):
                dve.tensor_tensor(g.carry_on[:, d, :], g.carry_in[:, d, :], bank[5][0:4, 0:NCH], ALU.add)

        @block.tensor
        def _(pe):
            pe.sem_inc(s_tr, 2)
            pe.wait_ge(s_dst, 1)
            for n in range(G):
                pe.transpose(bank[6][0:GC, n * P:(n + 1) * P], dstf[:, n * GC:(n + 1) * GC], g.ident[:]).then_inc(s_rows, 1) \
                    if n == G - 1 else pe.transpose(bank[6][0:GC, n * P:(n + 1) * P], dstf[:, n * GC:(n + 1) * GC], g.ident[:])
            for side in range(2):
                mm = pe.matmul(bank[7][0:4, side * NCH:(side + 1) * NCH], ends[:, side, :], dstf, start=True, stop=True)
            mm.then_inc(s_near, 1)
            with pe.Fori(0, BATCHES) as i:
                for u in range(2):
                    pe.wait_ge(s_hot, 2 * i + u + 1)
                    pe.wait_ge(s_ev, 2 * i + u + 1)
                    for side in range(2):
                        turned = bank[2 * u + side].bitcast(BF16)
                        for k in range(B):
                            tr = pe.transpose(turned[:, k * P:(k + 1) * P], hot[:, u, side, k, :], g.identb[:])
                    tr.then_inc(s_tr, 1)
            pe.wait_ge(s_inner, 1)
            for n in range(G):
                tr = pe.transpose(bank[5][0:4, n * GC:(n + 1) * GC], inner[0:GC, n, :], g.ident[0:GC, 0:GC])
            tr.then_inc(s_carry, 1)

        @block.scalar
        def _(act):
            act.sem_inc(s_ev, 2)
            with act.Fori(0, BATCHES) as i:
                for u in range(2):
                    act.wait_ge(s_tr, 2 * i + u + 3)
                    for side in range(2):
                        last = act.copy(g.onehotT[:, side, bass.ds((2 * i + u) * B * P, B * P)],
                                        bank[2 * u + side].bitcast(BF16)[:, 0:B * P])
                    last.then_inc(s_ev, 1)


def weights(g):
    nc, a, T, D, L, H1, F1, H2, F2, NCH = g.nc, g.a, g.T, g.D, g.L, g.H1, g.F1, g.H2, g.F2, g.NCH
    HF2, HID, AT = g.HF2, g.HID, g.AT
    s_in, s_dve, s_ewn, s_turn, s_v, s_vc = (g.sem(f"wts_{n}") for n in ("loaded", "dve", "edge", "turned", "v", "v_copied"))
    s_col, s_stage = g.sem("wts_columns"), g.sem("wts_attr_staged")
    s_at, s_atc, s_q, s_qc = (g.sem(f"wts_{n}") for n in ("attr_turned", "attr_copied", "q", "q_copied"))
    bank = [g.ps[:, 512 * k:512 * k + 512] for k in range(8)]
    lot = Lot(g.scratch[:].bitcast(BF16))
    att = lot.take([P, L * H2 * 2 * F2])
    a1 = lot.take([P, H1 * 2 * F1])
    ewn = lot.take([P, L, H2, NA])
    attj = lot.take([P, L, H2])
    vk = lot.take([P, L * H2])
    attr = lot.take([P, 2, 4, NA])
    rows = lot.take([P, P])
    NR = 2 * L * H2 + 4
    attrT = g.ring[:].rearrange("p k f -> p (k f)")[:, 0:2 * 4 * P].rearrange("p (u e) -> p u e", u=2)
    count = lot.take([P, 1], I32)
    prod = g.wide[:].rearrange("p t f -> p (t f)")
    B = 4
    LOADS = 19

    with nc.Block(name="weights") as block:
        @block.sync
        def _(sp):
            def load(dst, src):
                sp.dma_start(dst, src).then_inc(s_in, 16)
            load(ewn[:, :, :, 0:NA - 1], a["L2_gnn_edge_ws"].rearrange("l (h f) k -> f l h k", h=H2))
            load(rows[0:L * H2, :], a["L2_gnn_edge_bs"].rearrange("l (h f) -> (l h) f", h=H2))
            load(rows[L * H2:2 * L * H2, :], a["L2_gnn_atts"].rearrange("l h f -> (l h) f")[:, F2:])
            load(rows[2 * L * H2:2 * L * H2 + 1, :], a["L0_gnn_gamma"].unsqueeze(0))
            load(rows[2 * L * H2 + 1:2 * L * H2 + 2, :], a["L0_gnn_beta"].unsqueeze(0))
            load(rows[2 * L * H2 + 2:2 * L * H2 + 4, :], a["L3_gnn_b1"].rearrange("(k p) -> k p", p=P))
            load(att, a["L2_gnn_atts"].rearrange("l h f -> (l h f)").partition_broadcast(P))
            load(a1, a["L1_gnn_a_w"].rearrange("h f -> (h f)").partition_broadcast(P))
            load(g.w2x[:, :, 0:HF2], a["L2_gnn_weights"].rearrange("l i o -> i l o"))
            load(g.w1x[:, 0:D], a["L1_gnn_W_w"])
            load(g.bias1[:, 0:D], a["L1_gnn_W_b"].partition_broadcast(P))
            for n, name in enumerate(("W1", "W2", "Wo", "Wn")):
                load(g.w0[:, n, :], a["L0_gnn_" + name])
            load(g.ab1[:], a["L1_gnn_a_b"].partition_broadcast(P))
            load(g.bias2[:].rearrange("p l d -> p (l d)"), a["L2_gnn_biases"].rearrange("l d -> (l d)").partition_broadcast(P))
            load(count, a["L0_gnn_batch_num"][0:1].partition_broadcast(P))
            load(g.cols[:, 5:6], a["L3_gnn_clearance"].partition_broadcast(P))
            sp.wait_ge(s_in, 16 * LOADS)

        @block.vector
        def _(dve):
            c = Chain(dve, s_dve)
            dve.memset(g.floor2[:, 0:L - 1], 0.0)
            dve.memset(g.floor2[:, L - 1:L], -3.0e38)
            dve.wait_ge(s_in, 16 * LOADS)
            dve.tensor_copy(g.cols[:, 4:5], count)
            for src, folded, vec in ((g.w1x, g.w1x, a1), (g.bias1, g.bias1, a1)):
                for side in range(2):
                    c.step(dve.tensor_tensor(prod[:, 0:D].rearrange("p (h f) -> p h f", h=H1),
                                             src[:, 0:D].rearrange("p (h f) -> p h f", h=H1),
                                             vec.rearrange("p (h s f) -> p h s f", h=H1, s=2)[:, :, side, :], ALU.mult))
                    c.step(dve.tensor_reduce(folded[:, D + side * H1:D + (side + 1) * H1],
                                             prod[:, 0:D].rearrange("p (h f) -> p h f", h=H1), AX_X, ALU.add))
            for l in range(L):
                for side in range(2):
                    at = (l * 2 + side) % 4 * HF2
                    part = prod[:, at:at + HF2].rearrange("p (h f) -> p h f", h=H2)
                    c.step(dve.tensor_tensor(part, g.w2x[:, l, 0:HF2].rearrange("p (h f) -> p h f", h=H2),
                                             att.rearrange("p (l h s f) -> p l h s f", l=L, h=H2, s=2)[:, l, :, side, :], ALU.mult))
                    c.step(dve.tensor_reduce(g.w2x[:, l, HF2 + side * H2:HF2 + (side + 1) * H2], part, AX_X, ALU.add))
            dve.wait_ge(s_col, 1)
            dve.tensor_copy(ewn[:, :, :, NA - 1], bank[3][:, 0:L * H2].rearrange("p (l h) -> p l h", l=L))
            dve.tensor_copy(attj, bank[3][:, L * H2:2 * L * H2].rearrange("p (l h) -> p l h", l=L)).then_inc(s_ewn, 1)
            dve.tensor_copy(g.cols[:, 0:4], bank[3][:, 2 * L * H2:NR])
            dve.wait_ge(s_turn, 1)
            dve.tensor_copy(g.ew[:].rearrange("k l d -> k (l d)")[:, 0:512], bank[0][0:AT, 0:512])
            dve.tensor_copy(g.ew[:].rearrange("k l d -> k (l d)")[:, 512:L * D], bank[1][0:AT, 0:L * D - 512])
            dve.wait_ge(s_v, 1)
            dve.tensor_copy(vk[0:NA, :], bank[2][0:NA, 0:L * H2]).then_inc(s_vc, 1)
            with dve.Fori(0, NCH // (2 * B)) as i:
                for u in range(2):
                    dve.wait_ge(s_at, 2 * i + u + 1)
                    dve.tensor_copy(attr[:, u], g.rec[:, bass.ds((2 * i + u) * B, B), R_ATTR:R_ATTR + NA]).then_inc(s_stage, 1)
                for u in range(2):
                    dve.wait_ge(s_q, 2 * i + u + 1)
                    dve.tensor_copy(g.attr_part[:, bass.ds((2 * i + u) * B, B), :],
                                    bank[6 + u][:, 0:B * L * H2].rearrange("p (c q) -> p c q", c=B)).then_inc(s_qc, 1)

        @block.tensor
        def _(pe):
            pe.wait_ge(s_in, 16 * LOADS)
            pe.transpose(bank[3][:, 0:NR], rows[0:NR, :], g.ident[0:NR, 0:NR]).then_inc(s_col, 1)
            pe.wait_ge(s_ewn, 1)
            for l in range(L):
                tr = pe.transpose(bank[l // 4][0:AT, (l % 4) * D:(l % 4) * D + D],
                                  ewn[:, l].rearrange("p h k -> p (h k)"), g.ident[:])
            tr.then_inc(s_turn, 1)
            for l in range(L):
                for hd in range(H2):
                    mm = pe.matmul(bank[2][0:NA, l * H2 + hd:l * H2 + hd + 1], ewn[:, l, hd, :], attj[:, l, hd:hd + 1],
                                   start=True, stop=True)
            mm.then_inc(s_v, 1)
            pe.sem_inc(s_atc, 2)
            pe.sem_inc(s_at, 2)
            pe.sem_inc(s_qc, 2)
            pe.wait_ge(s_vc, 1)
            with pe.Fori(0, NCH // (2 * B)) as i:
                for u in range(2):
                    pe.wait_ge(s_stage, 2 * i + u + 1)
                    pe.wait_ge(s_atc, 2 * i + u + 1)
                    for k in range(B):
                        tr = pe.matmul(bank[4 + u][0:NA, k * P:(k + 1) * P],
                                       attr[:, u, k, :], g.ident[:], start=True, stop=True)
                    tr.then_inc(s_at, 1)
                    pe.wait_ge(s_atc, 2 * i + u + 3)
                    pe.wait_ge(s_qc, 2 * i + u + 1)
                    for k in range(B):
                        mm = pe.matmul(bank[6 + u][:, k * L * H2:(k + 1) * L * H2], attrT[0:NA, u, k * P:(k + 1) * P],
                                       vk[0:NA, :], start=True, stop=True)
                    mm.then_inc(s_q, 1)

        @block.scalar
        def _(act):
            with act.Fori(0, NCH // (2 * B)) as i:
                for u in range(2):
                    act.wait_ge(s_at, 2 * i + u + 3)
                    act.copy(attrT[0:NA, u, :], bank[4 + u][0:NA, 0:B * P]).then_inc(s_atc, 1)


def node_norm(g, name):
    nc, T, D = g.nc, g.T, g.D
    s_dve, s_var, s_std, s_h, s_turn, s_copy = (g.sem(f"{name}_{n}") for n in ("dve", "var", "std", "h", "turned", "copied"))
    st = g.stat
    with nc.Block(name=name) as block:
        @block.vector
        def _(dve):
            c = Chain(dve, s_dve)
            wide = [P, T, D]
            c.step(dve.tensor_reduce(st[:, 0, :], g.x[:], AX_X, ALU.add))
            c.step(dve.tensor_scalar(st[:, 1, :], st[:, 0, :], 1.0 / D, None, ALU.mult))
            c.step(dve.tensor_tensor(g.h[:], g.x[:], st[:, 1, :].unsqueeze(2).broadcast_to(wide), ALU.subtract))
            c.step(dve.tensor_tensor(g.wide[:, :, 0:D], g.h[:], g.h[:], ALU.mult))
            c.step(dve.tensor_reduce(st[:, 2, :], g.wide[:, :, 0:D], AX_X, ALU.add))
            dve.tensor_scalar(st[:, 2, :], st[:, 2, :], 1.0 / D, 1.0e-5, ALU.mult, ALU.add).then_inc(s_var, 1)
            dve.wait_ge(s_std, 1)
            c.step(dve.reciprocal(st[:, 1, :], st[:, 3, :]))
            dve.scalar_tensor_tensor(g.h[:], g.h[:], 0.0, st[:, 1, :].unsqueeze(2).broadcast_to(wide), ALU.max, ALU.mult).then_inc(s_h, 1)

        @block.scalar
        def _(act):
            act.wait_ge(s_var, 1)
            act.activation(st[:, 3, :], st[:, 2, :], ACT.Sqrt).then_inc(s_std, 1)
            turn_copies(g, act, s_turn)

        @block.tensor
        def _(pe):
            pe.wait_ge(s_h, 1)
            turn_nodes(g, pe, s_turn)


def turn_nodes(g, pe, turned, banks=0):
    for t in range(g.T):
        tr = pe.transpose(g.ps[:, 512 * banks + t * P:512 * banks + (t + 1) * P], g.h[:, t, :], g.ident[:])
        if t % 4 == 3 or t == g.T - 1:
            tr.then_inc(turned, 1)


def turn_copies(g, act, turned, banks=0, start=0):
    for n, at in enumerate(range(0, g.NP, 512)):
        act.wait_ge(turned, start + n + 1)
        to = min(at + 512, g.NP)
        last = act.copy(g.hT[:, at:to], g.ps[:, 512 * banks + at:512 * banks + to])
    return last


def halves(g):
    return [(at, min(at + 512, g.NP)) for at in range(0, g.NP, 512)]


def pool_gathers(pool, g, rows, width, staged, free, round_, got, ready=None):
    H = RING // 2
    with pool.Fori(0, g.CH // RING) as i:
        for u in range(2):
            pool.wait_ge(staged, 2 * i + u + 1)
            for k in range(H * u, H * (u + 1)):
                pool.wait_ge(free, i * RING + k + 1)
                pool.sem_inc(round_, 1)
                pool.indirect_dma_start(g.ring[:, k, 0:width], None, rows,
                                        bass.IndirectOffsetOnAxis(ap=g.slot_idx[:, k:k + 1], axis=0)).then_inc(got[k], 16)


def block0(g):
    nc, T, D, N, NP, CH = g.nc, g.T, g.D, g.N, g.NP, g.CH
    bank = [g.ps[:, 512 * k:512 * k + 512] for k in range(8)]
    flat = g.wide[:].rearrange("p t f -> p (t f)")
    l1T, h2T = flat[:, 0:NP], flat[:, NP:2 * NP]
    H = RING // 2
    s_mm, s_sc, s_act, s_h2, s_h2c, s_st = (g.sem(f"b0_{n}") for n in
                                            ("hidden", "scaled", "leaky", "h2", "h2_copied", "stored"))
    with nc.Block(name="b0_dense") as block:
        @block.tensor
        def _(pe):
            for n, (p, q) in enumerate(halves(g)):
                pe.matmul(bank[n][:, 0:q - p], g.w0[:, 0, :], g.hT[:, p:q], start=True, stop=True).then_inc(s_mm, 1)
            for n, (p, q) in enumerate(halves(g)):
                pe.wait_ge(s_act, n + 1)
                for t in range(p // P, q // P):
                    mm = pe.matmul(bank[3 + n][:, t * P - p:t * P - p + P], l1T[:, t * P:(t + 1) * P], g.w0[:, 1, :],
                                   start=True, stop=True)
                mm.then_inc(s_h2, 1)
            for n, (p, q) in enumerate(halves(g)):
                pe.matmul(bank[n][:, 0:q - p], g.w0[:, 1, :], l1T[:, p:q], start=True, stop=True).then_inc(s_h2, 1)

        @block.scalar
        def _(act):
            for n, (p, q) in enumerate(halves(g)):
                act.wait_ge(s_mm, n + 1)
                act.activation(l1T[:, p:q], bank[n][:, 0:q - p], ACT.Copy, scale=0.01).then_inc(s_sc, 1)
            for n, (p, q) in enumerate(halves(g)):
                act.wait_ge(s_h2, n + 4)
                act.copy(h2T[:, p:q], bank[n][:, 0:q - p])

        @block.vector
        def _(dve):
            for n, (p, q) in enumerate(halves(g)):
                dve.wait_ge(s_sc, n + 1)
                dve.tensor_tensor(l1T[:, p:q], bank[n][:, 0:q - p], l1T[:, p:q], ALU.max).then_inc(s_act, 1)
            for n, (p, q) in enumerate(halves(g)):
                dve.wait_ge(s_h2, n + 1)
                dve.tensor_copy(g.h[:, p // P:q // P, :].rearrange("p t d -> p (t d)"), bank[3 + n][:, 0:q - p]).then_inc(s_h2c, 1)

        @block.sync
        def _(sp):
            sp.wait_ge(s_h2c, 3)
            sp.dma_start(g.table1.rearrange("(t p) d -> p t d", p=P), g.h[:]).then_inc(s_st, 16)
            sp.wait_ge(s_st, 16)

    staged, free, round_ = g.sem("b0_staged"), g.sem("b0_slot_free"), g.sem("b0_round")
    got, before = g.got, g.gathered
    g.gathered += 16 * (CH // RING)
    s_hi, s_mid, s_rest, s_lo, s_sum = (g.sem(f"b0_{n}") for n in ("hi", "mid", "rest", "lo", "summed"))
    lot = Lot(g.scratch[:].bitcast(BF16))
    parts = lot.take([P, 3, 3, D], BF16)
    rest = lot.take([P, 3, D])
    hot = lot.take([P, 3, NP], BF16)
    with nc.Block(name="b0_edges") as block:
        @block.gpsimd
        def _(pool):
            pool.sem_inc(free, RING)
            pool_gathers(pool, g, g.table1, D, staged, free, round_, got)

        @block.scalar
        def _(act):
            for u in range(2):
                act.copy(g.slot_idx[:, u * H:(u + 1) * H], g.idx[:, 1, u * H:(u + 1) * H]).then_inc(staged, 1)
            with act.Fori(0, CH // RING) as i:
                for u in range(2):
                    for k in range(H * u, H * u + H):
                        c, m = i * RING + k, k % 3
                        act.wait_ge(got[k], before + 16 * (i + 1))
                        act.wait_ge(s_sum, c + 1)
                        act.activation(parts[:, m, 0, :], g.ring[:, k, 0:D], ACT.Copy,
                                       scale=g.rec[:, bass.ds(c, 1), R_W]).then_inc(s_hi, 1)
                        act.wait_ge(s_rest, c + 1)
                        act.copy(parts[:, m, 1, :], rest[:, m, :]).then_inc(s_mid, 1)
                    act.copy(g.slot_idx[:, H * u:H * u + H], g.idx[:, 1, bass.ds((2 * i + u + 2) * H, H)]).then_inc(staged, 1)

        @block.vector
        def _(dve):
            with dve.Fori(0, CH // RING) as i:
                for k in range(RING):
                    c, m = i * RING + k, k % 3
                    dve.wait_ge(s_hi, c + 1)
                    dve.scalar_tensor_tensor(rest[:, m, :], g.ring[:, k, 0:D], g.rec[:, bass.ds(c, 1), R_W], parts[:, m, 0, :],
                                             ALU.mult, ALU.subtract).then_inc(s_rest, 1)
                    dve.tensor_scalar(hot[:, m, :], g.nodeid[:], g.rec[:, bass.ds(c, 1), R_SRC], None, ALU.is_equal)
                    dve.wait_ge(s_mid, c + 1)
                    dve.tensor_tensor(parts[:, m, 2, :], rest[:, m, :], parts[:, m, 1, :], ALU.subtract).then_inc(s_lo, 1)

        @block.tensor
        def _(pe):
            for n, (p, q) in enumerate(halves(g)):
                pe.matmul(bank[n][:, 0:q - p], g.zerob[:, 0:P], g.zerob[:, 0:q - p], start=True, stop=True, skip_group_check=True)
            pe.sem_inc(s_sum, 3)
            with pe.Fori(0, CH // RING) as i:
                for k in range(RING):
                    c, m = i * RING + k, k % 3
                    pe.wait_ge(s_lo, c + 1)
                    pe.sem_inc(free, 1)
                    for part in range(3):
                        for n, (p, q) in enumerate(halves(g)):
                            mm = pe.matmul(bank[n][:, 0:q - p], parts[:, m, part, :], hot[:, m, p:q],
                                           start=False, stop=True, skip_group_check=True)
                    mm.then_inc(s_sum, 1)

    s_xn, s_out, s_dve, s_sq, s_std, s_norm, s_turn = (g.sem(f"b0_{n}") for n in
                                                       ("xn", "out", "dve", "var", "std", "normed", "turned"))
    s_sc2 = g.sem("b0_xn_scaled")
    lot = Lot(g.scratch[:].bitcast(BF16))
    xnT, oT, sq = lot.take([P, NP]), lot.take([P, NP]), l1T
    k = lot.take([P, 8])
    with nc.Block(name="b0_finish") as block:
        @block.scalar
        def _(act):
            for n, (p, q) in enumerate(halves(g)):
                act.activation(xnT[:, p:q], bank[n][:, 0:q - p], ACT.Copy, scale=0.01).then_inc(s_sc2, 1)
            act.wait_ge(s_sq, 1)
            act.activation(k[:, 4:5], k[:, 3:4], ACT.Sqrt).then_inc(s_std, 1)

        @block.tensor
        def _(pe):
            for n, (p, q) in enumerate(halves(g)):
                pe.matmul(bank[3 + n][:, 0:q - p], g.w0[:, 2, :], h2T[:, p:q], start=True, stop=False)
                pe.wait_ge(s_xn, n + 1)
                pe.matmul(bank[3 + n][:, 0:q - p], g.w0[:, 3, :], xnT[:, p:q], start=False, stop=True).then_inc(s_out, 1)
            pe.wait_ge(s_norm, 1)
            for t in range(T):
                w = P if t < T - 1 else g.LAST
                tr = pe.transpose(bank[t // 4][0:w, (t % 4) * D:(t % 4) * D + D], oT[:, t * P:t * P + w], g.ident[:])
                if t % 4 == 3 or t == T - 1:
                    tr.then_inc(s_turn, 1)

        @block.vector
        def _(dve):
            c = Chain(dve, s_dve)
            for n, (p, q) in enumerate(halves(g)):
                dve.wait_ge(s_sc2, n + 1)
                dve.tensor_tensor(xnT[:, p:q], bank[n][:, 0:q - p], xnT[:, p:q], ALU.max).then_inc(s_xn, 1)
            c.step(dve.tensor_scalar(k[:, 5:6], g.cols[:, 4:5], -1.0, None, ALU.add))
            dve.reciprocal(k[:, 6:7], g.cols[:, 4:5])
            c.step(dve.reciprocal(k[:, 7:8], k[:, 5:6]))
            for n, (p, q) in enumerate(halves(g)):
                dve.wait_ge(s_out, n + 1)
                last = dve.tensor_copy(oT[:, p:q], bank[3 + n][:, 0:q - p])
            c.step(last)
            c.step(dve.tensor_reduce(k[:, 0:1], oT[:, 0:N], AX_X, ALU.add))
            c.step(dve.tensor_tensor(k[:, 1:2], k[:, 0:1], k[:, 6:7], ALU.mult))
            c.step(dve.tensor_scalar(oT[:, 0:N], oT[:, 0:N], k[:, 1:2], None, ALU.subtract))
            c.step(dve.tensor_tensor(sq[:, 0:N], oT[:, 0:N], oT[:, 0:N], ALU.mult))
            c.step(dve.tensor_reduce(k[:, 2:3], sq[:, 0:N], AX_X, ALU.add))
            dve.tensor_tensor(k[:, 3:4], k[:, 2:3], k[:, 7:8], ALU.mult).then_inc(s_sq, 1)
            dve.wait_ge(s_std, 1)
            c.step(dve.tensor_scalar(k[:, 4:5], k[:, 4:5], 1.0e-6, None, ALU.add))
            c.step(dve.reciprocal(k[:, 3:4], k[:, 4:5]))
            c.step(dve.tensor_tensor(k[:, 3:4], k[:, 3:4], g.cols[:, 0:1], ALU.mult))
            dve.tensor_scalar(oT[:, 0:N], oT[:, 0:N], k[:, 3:4], g.cols[:, 1:2], ALU.mult, ALU.add).then_inc(s_norm, 1)
            add_nodes(g, dve, bank, s_turn)


def add_nodes(g, dve, bank, turned):
    for t in range(0, g.T, 4):
        dve.wait_ge(turned, t // 4 + 1)
        full = min(4, g.T - 1 - t)
        if full > 0:
            xs = g.x[:, t:t + full, :]
            dve.tensor_tensor(xs, xs, bank[t // 4][:, 0:full * g.D].rearrange("p (t d) -> p t d", d=g.D), ALU.add)
        if t + 4 >= g.T:
            xs = g.x[0:g.LAST, g.T - 1, :]
            at = (g.T - 1 - t) * g.D
            dve.tensor_tensor(xs, xs, bank[t // 4][0:g.LAST, at:at + g.D], ALU.add)


def tile_numbers(g, i):
    assert g.T <= 16 and 4 * RING <= 24
    _, packed = g.nc.values_load_multi_w_load_instructions(g.round_tiles[0:1, bass.ds(i, 1)], engines=[mybir.EngineType.PE],
                                                           min_val=0, max_val=(g.T - 1) * ((16 ** RING - 1) // 15))
    return [(packed[0] >> (4 * k)) & 15 for k in range(RING)]


def attention(g, name, H, F, weights_, bias, table, logit_terms, extra, layer=0, layers=1):
    nc, T, D, NCH, CH, G, GC = g.nc, g.T, g.D, g.NCH, g.CH, g.G, g.GC
    HF, S = H * F, 2 * H
    CB = 24 // H
    W20 = 2 * T
    WIDTH = CB * H * W20
    GROUPS = NCH // CB
    assert GROUPS % 2 == 0
    HG = H * G
    EX = g.AT if extra == "attributes" else H
    half = RING // 2
    bank = [g.ps[:, 512 * k:512 * k + 512] for k in range(8)]
    names = ("rows", "rows_copied", "rows_read", "stored", "dve", "split", "looked", "masked", "logits", "edge_rows",
             "scan0", "row0", "carry0", "carry0_turned", "scan1", "row1", "carry1", "carry1_turned", "maxima", "max_turned",
             "shifted", "weights", "staged", "free", "round", "act_msg", "dve_msg", "summed", "reduced")
    q = {n: g.sem(f"{name}_{n}") for n in names}
    got, before = g.got, g.gathered + 16 * (CH // RING) * layer
    g.gathered += 16 * (CH // RING) * layers
    lot = Lot(g.scratch[:].bitcast(BF16))
    scores = lot.take([P, 2, 3, H, T], BF16)
    rest = lot.take([P, 2, S, T])
    msg = lot.take([P, 3, HF + EX])
    hot = lot.take([P, 3, P])
    masked = lot.take([P, 2, WIDTH])
    ends = lot.take([P, 2, G, H])
    rowbuf = lot.take([4, 4, NCH])
    F0, M0 = g.scan_a[0:GC, 0:HG * P], g.scan_b[0:GC, 0:HG * P]
    lg = g.logits
    rows = bank[0:4]

    with nc.Block(name=name) as block:
        @block.tensor
        def _(pe):
            for t in range(T):
                if t >= 4:
                    pe.wait_ge(q["rows_read"], t - 3)
                pe.matmul(rows[t % 4][:, 0:HF + S], g.hT[:, t * P:(t + 1) * P], weights_, start=True, stop=True).then_inc(q["rows"], 1)
            pe.sem_inc(q["masked"], 2)
            pe.sem_inc(q["reduced"], 2)
            pe.wait_ge(q["split"], 1)
            with pe.Fori(0, GROUPS // 2) as i:
                for u in range(2):
                    pe.wait_ge(q["masked"], 2 * i + u + 1)
                    for k in range(CB):
                        c = (2 * i + u) * CB + k
                        out = bank[4 + u][:, k * H * W20:(k + 1) * H * W20].rearrange("p (h s t) -> p h s t", h=H, s=2)
                        for side in range(2):
                            for part in range(3):
                                mm = pe.matmul(out[:, :, side, :], g.onehotT[:, side, bass.ds(c * P, P)], scores[:, side, part],
                                               start=part == 0, stop=part == 2)
                    mm.then_inc(q["looked"], 1)
            pe.wait_ge(q["logits"], 1)
            for b in range(HG):
                tr = pe.transpose(bank[b // 4][0:GC, (b % 4) * P:(b % 4) * P + P], lg[:, (b % G) * GC:(b % G + 1) * GC, b // G], g.ident[:])
            tr.then_inc(q["edge_rows"], 1)
            for way, (scan, row_, carry, back) in enumerate(((q["scan0"], q["row0"], q["carry0"], q["carry0_turned"]),
                                                             (q["scan1"], q["row1"], q["carry1"], q["carry1_turned"]))):
                pe.wait_ge(scan, 1)
                for n in range(G):
                    tr = pe.transpose(bank[2 + way][0:H, n * GC:(n + 1) * GC], ends[0:GC, way, n, :], g.ident[0:GC, 0:GC])
                tr.then_inc(row_, 1)
                pe.wait_ge(carry, 1)
                for n in range(G):
                    tr = pe.transpose(bank[6 + way][0:GC, n * H:(n + 1) * H], rowbuf[0:H, 2 * way + 1, n * GC:(n + 1) * GC],
                                      g.ident[0:H, 0:H])
                tr.then_inc(back, 1)
            pe.wait_ge(q["maxima"], 1)
            for b in range(HG):
                tr = pe.transpose(bank[4 + b // 4][:, (b % 4) * GC:(b % 4 + 1) * GC], M0[:, b * P:(b + 1) * P], g.ident[0:GC, 0:GC])
            tr.then_inc(q["max_turned"], 1)
            pe.wait_ge(q["shifted"], 1)
            for b in range(6):
                pe.matmul(bank[b], g.zerob[:, 0:P], g.zerob[:], start=True, stop=True, skip_group_check=True)
            pe.sem_inc(q["summed"], 3)
            with pe.Fori(0, CH // RING) as i:
                tiles_ = tile_numbers(g, i)
                for k in range(RING):
                    c, m = i * RING + k, k % 3
                    t = tiles_[k]
                    pe.wait_ge(q["act_msg"], c + 1)
                    pe.wait_ge(q["dve_msg"], c + 1)
                    pe.sem_inc(q["free"], 1)
                    pe.matmul(g.ps[:, bass.ds(t * HF, HF)], hot[:, m, :], msg[:, m, 0:HF], start=False, stop=True,
                              skip_group_check=True)
                    pe.matmul(g.ps[:, bass.ds(t * EX + g.ATT0, EX)], hot[:, m, :], msg[:, m, HF:HF + EX], start=False, stop=True,
                              skip_group_check=True).then_inc(q["summed"], 1)

        @block.vector
        def _(dve):
            c = Chain(dve, q["dve"])
            small = g.small[:, :, 0:S]
            for t in range(T):
                dve.wait_ge(q["rows"], t + 1)
                if bias is not None:
                    dve.tensor_tensor(g.wide[:, t, 0:HF], rows[t % 4][:, 0:HF], bias[:, 0:HF], ALU.add).then_inc(q["rows_copied"], 1)
                    last = dve.tensor_tensor(small[:, t, :], rows[t % 4][:, HF:HF + S], bias[:, HF:HF + S], ALU.add)
                else:
                    dve.tensor_copy(g.wide[:, t, 0:HF], rows[t % 4][:, 0:HF]).then_inc(q["rows_copied"], 1)
                    last = dve.tensor_copy(small[:, t, :], rows[t % 4][:, HF:HF + S])
                last.then_inc(q["rows_read"], 1)
            dve.wait_ge(q["rows_read"], T)
            part = [scores[:, :, n] for n in range(3)]
            src4 = small.rearrange("p t (s h) -> p s h t", s=2)
            rest4 = [rest[:, n].rearrange("p (s h) t -> p s h t", s=2) for n in range(2)]
            c.step(dve.tensor_copy(part[0], src4))
            c.step(dve.tensor_tensor(rest4[0], src4, part[0], ALU.subtract))
            c.step(dve.tensor_copy(part[1], rest4[0]))
            dve.tensor_tensor(part[2], rest4[0], part[1], ALU.subtract).then_inc(q["split"], 1)
            with dve.Fori(0, GROUPS // 2) as i:
                for u in range(2):
                    chunks = bass.ds((2 * i + u) * CB, CB)
                    dve.wait_ge(q["looked"], 2 * i + u + 1)
                    dve.wait_ge(q["reduced"], 2 * i + u + 1)
                    dve.tensor_tensor(masked[:, u, :].rearrange("p (c h w) -> p c h w", c=CB, h=H),
                                      bank[4 + u][:, 0:WIDTH].rearrange("p (c h w) -> p c h w", c=CB, h=H),
                                      g.himask[:, chunks].rearrange("p c s t -> p c (s t)").unsqueeze(2).broadcast_to([P, CB, H, W20]),
                                      ALU.mult).then_inc(q["masked"], 1)
                for u in range(2):
                    chunks = bass.ds((2 * i + u) * CB, CB)
                    dve.wait_ge(q["masked"], 2 * i + u + 3)
                    dve.tensor_reduce(lg[:, chunks, 0:H], masked[:, u, :].rearrange("p (c h w) -> p c h w", c=CB, h=H),
                                      AX_X, ALU.add).then_inc(q["reduced"], 1)
            dve.wait_ge(q["reduced"], 2 + GROUPS)
            ls = lg[:, :, 0:H]
            c.step(dve.tensor_tensor(ls, ls, logit_terms, ALU.add))
            c.step(dve.scalar_tensor_tensor(ls, ls, 0.2, ls, ALU.mult, ALU.max))
            dve.tensor_tensor(ls, ls, g.unreal[:].unsqueeze(2).broadcast_to([P, NCH, H]), ALU.add).then_inc(q["logits"], 1)
            dve.wait_ge(q["edge_rows"], 1)
            line = g.ps[0:GC, 0:HG * P]
            blocks = line.rearrange("p (h n e) -> p h n e", h=H, n=G)
            F4, M4 = (v.rearrange("p (h n e) -> p h n e", h=H, n=G) for v in (F0, M0))
            resets = [g.reset[:, d].rearrange("p h n e -> p (h n e)")[:, 0:HG * P] for d in range(2)]
            for way, (scan, row_, carry, back) in enumerate(((q["scan0"], q["row0"], q["carry0"], q["carry0_turned"]),
                                                             (q["scan1"], q["row1"], q["carry1"], q["carry1_turned"]))):
                into, at, first = (F4, P - 1, 0) if way == 0 else (M4, 0, P - 1)

                def sweep():
                    if way == 0:
                        return dve.tensor_tensor_scan(F0, resets[0], line, -BIG, ALU.add, ALU.max)
                    return dve.tensor_tensor_scan(M0[:, ::-1], resets[1][:, ::-1], F0[:, ::-1], -BIG, ALU.add, ALU.max)
                c.step(sweep())
                dve.tensor_copy(ends[0:GC, way].rearrange("p n h -> p h n"), into[:, :, :, at]).then_inc(scan, 1)
                dve.wait_ge(row_, 1)
                run, out = rowbuf[0:H, 2 * way], rowbuf[0:H, 2 * way + 1]
                ins = bank[2 + way][0:H, 0:NCH]
                on = g.carry_on[0:H, way, :]
                if way == 0:
                    c.step(dve.tensor_tensor_scan(run, on, ins, -BIG, ALU.add, ALU.max))
                    dve.tensor_tensor(out[:, 1:NCH], run[:, 0:NCH - 1], g.carry_in[0:H, 0, 1:NCH], ALU.add)
                else:
                    c.step(dve.tensor_tensor_scan(run[:, ::-1], on[:, ::-1], ins[:, ::-1], -BIG, ALU.add, ALU.max))
                    dve.tensor_tensor(out[:, 0:NCH - 1], run[:, 1:NCH], g.carry_in[0:H, 1, 0:NCH - 1], ALU.add)
                dve.memset(out[:, 0:1] if way == 0 else out[:, NCH - 1:NCH], -BIG).then_inc(carry, 1)
                dve.wait_ge(back, 1)
                held = (blocks if way == 0 else F4)[:, :, :, first]
                c.step(dve.tensor_copy(ends[0:GC, way], bank[6 + way][0:GC, 0:G * H].rearrange("p (n h) -> p n h", n=G)))
                c.step(dve.tensor_tensor(held, held, ends[0:GC, way].rearrange("p n h -> p h n"), ALU.max))
                last = sweep()
                if way == 0:
                    c.step(last)
            last.then_inc(q["maxima"], 1)
            dve.wait_ge(q["max_turned"], 1)
            for b in range(HG // 4):
                hs = lg[:, :, 2 * b:2 * b + 2].rearrange("p c h -> p h c")
                last = dve.tensor_tensor(hs, hs, bank[4 + b][:, 0:2 * NCH].rearrange("p (h c) -> p h c", h=2), ALU.subtract)
            last.then_inc(q["shifted"], 1)
            dve.wait_ge(q["weights"], 1)
            with dve.Fori(0, CH // RING) as i:
                for k in range(RING):
                    ch, m = i * RING + k, k % 3
                    one = bass.ds(ch, 1)
                    dve.wait_ge(q["summed"], ch + 1)
                    dve.tensor_scalar(hot[:, m, :], g.lane[:], g.rec[:, one, R_DLO], None, ALU.is_equal)
                    wt = lg[:, one, 0:H].rearrange("p o h -> p (o h)")
                    if extra == "attributes":
                        dve.tensor_tensor(msg[:, m, HF:HF + EX].rearrange("p (h k) -> p h k", h=H),
                                          g.rec[:, one, R_ATTR:R_ATTR + NA].broadcast_to([P, H, NA]),
                                          wt.unsqueeze(2).broadcast_to([P, H, NA]), ALU.mult)
                        dve.wait_ge(got[k], before + 16 * (i + 1))
                        dve.tensor_scalar(msg[:, m, F:HF], g.ring[:, k, F:HF], lg[:, one, 1], None, ALU.mult).then_inc(q["dve_msg"], 1)
                    else:
                        dve.wait_ge(got[k], before + 16 * (i + 1))
                        dve.tensor_tensor(msg[:, m, 0:HF].rearrange("p (h f) -> p h f", h=H),
                                          g.ring[:, k, 0:HF].rearrange("p (h f) -> p h f", h=H),
                                          wt.unsqueeze(2).broadcast_to([P, H, F]), ALU.mult).then_inc(q["dve_msg"], 1)

        @block.scalar
        def _(act):
            for u in range(2):
                act.copy(g.slot_idx[:, u * half:(u + 1) * half], g.idx[:, 0, u * half:(u + 1) * half]).then_inc(q["staged"], 1)
            act.wait_ge(q["shifted"], 1)
            act.activation(lg[:, :, 0:H], lg[:, :, 0:H], ACT.Exp).then_inc(q["weights"], 1)
            act.wait_ge(q["weights"], 1)
            with act.Fori(0, CH // RING) as i:
                for u in range(2):
                    for k in range(half * u, half * u + half):
                        ch, m = i * RING + k, k % 3
                        act.wait_ge(q["summed"], ch + 1)
                        act.wait_ge(got[k], before + 16 * (i + 1))
                        if extra == "attributes":
                            act.activation(msg[:, m, 0:F], g.ring[:, k, 0:F], ACT.Copy, scale=lg[:, bass.ds(ch, 1), 0]).then_inc(q["act_msg"], 1)
                        else:
                            act.copy(msg[:, m, HF:HF + H], lg[:, bass.ds(ch, 1), 0:H].rearrange("p o h -> p (o h)")).then_inc(q["act_msg"], 1)
                    act.copy(g.slot_idx[:, half * u:half * u + half],
                             g.idx[:, 0, bass.ds((2 * i + u + 2) * half, half)]).then_inc(q["staged"], 1)

        @block.sync
        def _(sp):
            for n in range(2):
                ts = slice(n * T // 2, (n + 1) * T // 2)
                sp.wait_ge(q["rows_copied"], (n + 1) * T // 2)
                sp.dma_start(table.rearrange("(t p) d -> p t d", p=P)[:, ts, :], g.wide[:, ts, 0:HF]).then_inc(q["stored"], 16)

        @block.gpsimd
        def _(pool):
            pool.wait_ge(q["stored"], 32)
            pool.sem_inc(q["free"], RING)
            pool_gathers(pool, g, table, HF, q["staged"], q["free"], q["round"], got)


def block1(g):
    nc, T, D, H, F = g.nc, g.T, g.D, g.H1, g.F1
    attention(g, "b1", H, F, g.w1x[:], g.bias1, g.table1, g.ab1[:].unsqueeze(1).broadcast_to([P, g.NCH, H]), "weights")
    s_dve = g.sem("b1_finish")
    with nc.Block(name="b1_finish") as block:
        @block.vector
        def _(dve):
            c = Chain(dve, s_dve)
            den = g.small[:, :, 0:H]
            c.step(dve.tensor_scalar(den, g.ps[:, g.ATT0:g.ATT0 + T * H].rearrange("p (t h) -> p t h", t=T), 1.0e-30, None, ALU.max))
            c.step(dve.reciprocal(den, den))
            c.step(dve.tensor_tensor(g.h[:].rearrange("p t (h f) -> p t h f", h=H),
                                     g.ps[:, 0:T * D].rearrange("p (t h f) -> p t h f", t=T, h=H),
                                     den.unsqueeze(3).broadcast_to([P, T, H, F]), ALU.mult))
            dve.tensor_tensor(g.x[:], g.x[:], g.h[:], ALU.add)


def block2(g):
    nc, T, D, L, H, F, AT = g.nc, g.T, g.D, g.L, g.H2, g.F2, g.AT
    HF = H * F
    bank = [g.ps[:, 512 * k:512 * k + 512] for k in range(8)]
    with nc.Fori(0, L) as l:
        attention(g, "b2", H, F, g.w2x[:, bass.ds(l, 1), :].rearrange("p o w -> p (o w)"), None, g.table,
                         g.attr_part[:, :, bass.ds(l * H, H)], "attributes", l, L)
        names = ("dve", "attr", "attr_turned", "attr_copied", "attr_sum", "read", "h", "turned")
        q = {n: g.sem(f"b2_finish_{n}") for n in names}
        lot = Lot(g.scratch[:].bitcast(BF16))
        den = lot.take([P, T, H])
        att = lot.take([P, T, AT])
        attT = lot.take([AT, g.NP])
        with nc.Block(name="b2_finish") as block:
            @block.vector
            def _(dve):
                c = Chain(dve, q["dve"])
                sums = g.ps[:, g.ATT0:g.ATT0 + T * AT].rearrange("p (t h k) -> p t h k", t=T, h=H)
                c.step(dve.tensor_scalar(den, sums[:, :, :, NA - 1], 1.0e-16, None, ALU.add))
                c.step(dve.reciprocal(den, den))
                c.step(dve.tensor_scalar(den, den, 1.0 / H, None, ALU.mult))
                dve.tensor_tensor(att.rearrange("p t (h k) -> p t h k", h=H), sums,
                                  den.unsqueeze(3).broadcast_to([P, T, H, NA]), ALU.mult).then_inc(q["attr"], 1)
                c.step(dve.tensor_tensor(g.wide[:].rearrange("p t (h f) -> p t h f", h=H),
                                         g.ps[:, 0:T * HF].rearrange("p (t h f) -> p t h f", t=T, h=H),
                                         den.unsqueeze(3).broadcast_to([P, T, H, F]), ALU.mult))
                dve.sem_inc(q["read"], 1)
                c.step(dve.tensor_tensor(g.h[:], g.wide[:, :, 0:F], g.wide[:, :, F:HF], ALU.add))
                c.step(dve.tensor_tensor(g.h[:], g.h[:], g.bias2[:, bass.ds(l, 1), :].broadcast_to([P, T, D]), ALU.add))
                dve.wait_ge(q["attr_sum"], 1)
                c.step(dve.tensor_tensor(g.h[:], g.h[:], g.ps[:, 0:T * D].rearrange("p (t d) -> p t d", d=D), ALU.add))
                dve.tensor_scalar(g.h[:], g.h[:], g.floor2[:, bass.ds(l, 1)], None, ALU.max).then_inc(q["h"], 1)

            @block.tensor
            def _(pe):
                pe.wait_ge(q["attr"], 1)
                for t in range(T):
                    if t == 8:
                        pe.wait_ge(q["attr_copied"], 1)
                    b = 6 + t // 4 if t < 8 else 6
                    tr = pe.transpose(bank[b][0:AT, (t % 4) * P:(t % 4) * P + P], att[:, t, :], g.ident[:])
                    if t % 4 == 3 or t == T - 1:
                        tr.then_inc(q["attr_turned"], 1)
                pe.wait_ge(q["attr_copied"], 3)
                pe.wait_ge(q["read"], 1)
                for t in range(T):
                    mm = pe.matmul(g.ps[:, t * D:(t + 1) * D], attT[:, t * P:(t + 1) * P],
                                   g.ew[:, bass.ds(l, 1), :].rearrange("p o d -> p (o d)"), start=True, stop=True)
                mm.then_inc(q["attr_sum"], 1)
                pe.wait_ge(q["h"], 1)
                turn_nodes(g, pe, q["turned"], banks=4)

            @block.scalar
            def _(act):
                for n in range(3):
                    act.wait_ge(q["attr_turned"], n + 1)
                    w = min(4, T - 4 * n) * P
                    act.copy(attT[:, n * 512:n * 512 + w], bank[6 + n % 2][0:AT, 0:w]).then_inc(q["attr_copied"], 1)
                turn_copies(g, act, q["turned"], banks=4)
        g.stage.clear()
    with nc.Block(name="b2_add") as block:
        @block.vector
        def _(dve):
            dve.tensor_tensor(g.x[:], g.x[:], g.h[:], ALU.add)


def block3(g):
    nc, a, T, D, NP, CH, HID, DT = g.nc, g.a, g.T, g.D, g.NP, g.CH, g.HID, g.DT
    bank = [g.ps[:, 512 * k:512 * k + 512] for k in range(8)]
    flat = g.onehotT[:].rearrange("p s e -> p (s e)")
    C = flat[:, 0:2 * T * NP].bitcast(F32).rearrange("p (t n) -> p t n", t=T)
    lot = Lot(flat[:, 2 * T * NP:])
    w_in, w1, w2 = lot.take([P, D]), lot.take([P, HID]), lot.take([P, 2, D])
    b_in, b2 = lot.take([P, D]), lot.take([P, D])
    keep = lot.take([P, 1])
    deg, rdeg = lot.take([P, T]), lot.take([P, T])
    aggT = lot.take([P, NP])
    tmp = lot.take([P, T, D])
    hot_d = lot.take([P, RING, P], BF16)
    lots = [Lot(g.scratch[:].bitcast(BF16)), Lot(g.wide[:].rearrange("p t f -> p (t f)").bitcast(BF16))]
    hot_s = [lots[k % 2].take([P, NP], BF16) for k in range(RING)]
    zT = g.wide[:].rearrange("p t f -> p (t f)").rearrange("p (k n) -> p k n", k=2)

    REGION = 3 * 512
    names = ("loaded", "hots", "summed", "taken", "dve", "degrees", "apart", "divided", "turned", "rows_back", "cols_back")
    q = {n: g.sem(f"b3_{n}") for n in names}
    assert T % 2 == 0
    with nc.Block(name="b3_counts") as block:
        @block.sync
        def _(sp):
            for dst, src in ((w_in, a["L3_gnn_W_in"]), (w1, a["L3_gnn_W1"]), (w2, a["L3_gnn_W2"].rearrange("(k p) o -> p k o", p=P)),
                             (b_in, a["L3_gnn_b_in"].partition_broadcast(P)), (b2, a["L3_gnn_b2"].partition_broadcast(P))):
                sp.dma_start(dst, src).then_inc(q["loaded"], 16)
            sp.wait_ge(q["loaded"], 16 * 5)

        @block.vector
        def _(dve):
            c = Chain(dve, q["dve"])
            c.step(dve.tensor_scalar(keep, g.cols[:, 5:6], 0.0, None, ALU.max))
            c.step(dve.tensor_scalar(keep, keep, -DT, 1.0, ALU.mult, ALU.add))
            with dve.Fori(0, CH // RING) as i:
                for k in range(RING):
                    ch = i * RING + k
                    one = bass.ds(ch, 1)
                    dve.wait_ge(q["summed"], ch + 1)
                    dve.tensor_scalar(hot_d[:, k, :], g.lane16[:], g.rec[:, one, R_DLO], g.rec[:, one, R_ORIG],
                                      ALU.is_equal, ALU.mult)
                    dve.tensor_scalar(hot_s[k], g.nodeid[:], g.rec[:, one, R_SRC], None, ALU.is_equal).then_inc(q["hots"], 1)
            dve.wait_ge(q["taken"], 2 + T)
            c.step(dve.tensor_copy(rdeg, deg))
            c.step(dve.tensor_tensor(rdeg[:, 2:T], deg[:, 2:T], deg[:, 0:T - 2], ALU.subtract))
            c.step(dve.tensor_scalar(rdeg, rdeg, 1.0, None, ALU.max))
            dve.reciprocal(rdeg, rdeg).then_inc(q["degrees"], 1)
            for t in range(T - 2, 0, -2):
                dve.tensor_tensor(C[:, t:t + 2, :], C[:, t:t + 2, :], C[:, t - 2:t, :], ALU.subtract).then_inc(q["apart"], 1)
                dve.wait_ge(q["apart"], (T - t) // 2)
            for t in range(T - 1):
                dve.wait_ge(q["turned"], 2 * t + 2)
                dve.tensor_copy(C[:, t, (t + 1) * P:NP], g.ps[:, REGION:REGION + (T - 1 - t) * P]).then_inc(q["cols_back"], 1)

        @block.tensor
        def _(pe):
            pe.sem_inc(q["summed"], RING)
            for b in range(6):
                pe.matmul(bank[b], g.zerob[:, 0:P], g.zerob[:], start=True, stop=True, skip_group_check=True)
            with pe.Fori(0, CH // RING) as i:
                tiles_ = tile_numbers(g, i)
                for k in range(RING):
                    pe.wait_ge(q["taken"], tiles_[k] + 1)
                    pe.wait_ge(q["hots"], i * RING + k + 1)
                    for p, e in halves(g):
                        mm = pe.matmul(g.ps[:, bass.ds((tiles_[k] & 1) * REGION + p, e - p)], hot_d[:, k, :], hot_s[k][:, p:e],
                                       start=False, stop=True, skip_group_check=True)
                    mm.then_inc(q["summed"], 1)
            pe.wait_ge(q["divided"], T)
            for t in range(T):
                if t:
                    pe.wait_ge(q["rows_back"], t)
                for s_ in range(t, T):
                    tr = pe.transpose(g.ps[:, (s_ - t) * P:(s_ - t + 1) * P], C[:, t, s_ * P:(s_ + 1) * P], g.ident[:])
                tr.then_inc(q["turned"], 1)
                if t < T - 1:
                    if t:
                        pe.wait_ge(q["cols_back"], t)
                    for s_ in range(t + 1, T):
                        tr = pe.transpose(g.ps[:, REGION + (s_ - t - 1) * P:REGION + (s_ - t) * P], C[:, s_, t * P:(t + 1) * P], g.ident[:])
                    tr.then_inc(q["turned"], 1)

        @block.scalar
        def _(act):
            act.sem_inc(q["taken"], 2)
            with act.Fori(0, T // 2) as i:
                _, last_ = nc.values_load_multi_w_load_instructions(g.tile_end[0:1, bass.ds(2 * i, 2)], min_val=1, max_val=CH,
                                                                    engines=[mybir.EngineType.Activation])
                for u in range(2):
                    act.wait_ge(q["summed"], last_[u] + RING)
                    act.activation(C[:, bass.ds(2 * i + u, 1), :].rearrange("p o n -> p (o n)"), g.ps[:, u * REGION:u * REGION + NP],
                                   ACT.Copy, accum_out=deg[:, bass.ds(2 * i + u, 1)]).then_inc(q["taken"], 1)
            act.wait_ge(q["degrees"], 1)
            for n, t in enumerate(range(T - 2, -1, -2)):
                act.wait_ge(q["apart"], min(n + 1, T // 2 - 1))
                for t_ in (t, t + 1):
                    act.activation(C[:, t_, :], C[:, t_, :], ACT.Copy, scale=rdeg[:, t_:t_ + 1]).then_inc(q["divided"], 1)
            for t in range(T):
                act.wait_ge(q["turned"], min(2 * t + 2, 2 * T - 1))
                act.copy(C[:, t:T, t * P:(t + 1) * P], g.ps[:, 0:(T - t) * P].rearrange("p (s n) -> p s n", n=P)).then_inc(q["rows_back"], 1)
    g.stage.end()

    names = ("agg", "aggT", "z", "gelu", "out", "pre", "tanh", "h", "start", "start_sum", "dve", "kept", "done")
    q = {n: g.sem(f"b3_{n}") for n in names}
    parts = halves(g)
    with nc.Block(name="b3_steps") as block:
        @block.tensor
        def _(pe):
            for n, (p, e) in enumerate(parts):
                for t in range(p // P, e // P):
                    mm = pe.matmul(bank[5 + n][:, t * P - p:t * P - p + P], g.hT[:, t * P:(t + 1) * P], w_in, start=True, stop=True)
                mm.then_inc(q["start"], 1)

            def gather(i, n):
                p, e = parts[n]
                for s_ in range(T):
                    if n == 0 and s_ % 4 == 0:
                        pe.wait_ge(q["h"], 3 * i + s_ // 4 + 1)
                    mm = pe.matmul(bank[n][:, 0:e - p], g.h[:, s_, :], C[:, s_, p:e], start=s_ == 0, stop=s_ == T - 1)
                mm.then_inc(q["agg"], 1)

            def hidden(i, n):
                p, e = parts[n]
                pe.wait_ge(q["aggT"], 3 * i + n + 1)
                pe.wait_ge(q["gelu"], 3 * i + n + 1)
                for k in range(2):
                    mm = pe.matmul(bank[3 + k][:, 0:e - p], w1[:, k * P:(k + 1) * P], aggT[:, p:e], start=True, stop=True)
                mm.then_inc(q["z"], 1)

            def output(i, n):
                p, e = parts[n]
                pe.wait_ge(q["gelu"], 3 * i + n + 2)
                for t in range(p // P, e // P):
                    for k in range(2):
                        mm = pe.matmul(bank[5 + n][:, t * P - p:t * P - p + P], zT[:, k, t * P:(t + 1) * P], w2[:, k, :],
                                       start=k == 0, stop=k == 1)
                mm.then_inc(q["out"], 1)

            pe.sem_inc(q["gelu"], 1)
            with pe.Fori(0, g.STEPS) as i:
                gather(i, 0)
                gather(i, 1)
                hidden(i, 0)
                gather(i, 2)
                hidden(i, 1)
                output(i, 0)
                hidden(i, 2)
                output(i, 1)
                output(i, 2)

        @block.scalar
        def _(act):
            for n, (p, e) in enumerate(parts):
                act.wait_ge(q["start_sum"], n + 1)
                act.activation(g.h[:, p // P:e // P, :], tmp[:, p // P:e // P, :], ACT.Tanh).then_inc(q["h"], 1)

            def copy(i, n):
                p, e = parts[n]
                act.wait_ge(q["agg"], 3 * i + n + 1)
                act.copy(aggT[:, p:e], bank[n][:, 0:e - p]).then_inc(q["aggT"], 1)

            def gelu(i, n):
                p, e = parts[n]
                act.wait_ge(q["z"], 3 * i + n + 1)
                for k in range(2):
                    last = act.activation(zT[:, k, p:e], bank[3 + k][:, 0:e - p], ACT.Gelu, bias=g.cols[:, 2 + k:3 + k])
                last.then_inc(q["gelu"], 1)

            def tanh(i, n):
                p, e = parts[n]
                act.wait_ge(q["pre"], 3 * i + n + 1)
                act.activation(tmp[:, p // P:e // P, :], tmp[:, p // P:e // P, :], ACT.Tanh).then_inc(q["tanh"], 1)

            with act.Fori(0, g.STEPS) as i:
                copy(i, 0)
                copy(i, 1)
                gelu(i, 0)
                copy(i, 2)
                gelu(i, 1)
                gelu(i, 2)
                tanh(i, 0)
                tanh(i, 1)
                tanh(i, 2)

        @block.vector
        def _(dve):
            def summed(n, bias):
                p, e = parts[n]
                ts = slice(p // P, e // P)
                return dve.tensor_tensor(tmp[:, ts, :], bank[5 + n][:, 0:e - p].rearrange("p (t d) -> p t d", d=D),
                                         bias.unsqueeze(1).broadcast_to([P, (e - p) // P, D]), ALU.add)
            for n in range(3):
                dve.wait_ge(q["start"], n + 1)
                summed(n, b_in).then_inc(q["start_sum"], 1)
            dve.wait_ge(q["h"], 3)
            with dve.Fori(0, g.STEPS) as i:
                for n, (p, e) in enumerate(parts):
                    ts = slice(p // P, e // P)
                    dve.wait_ge(q["out"], 3 * i + n + 1)
                    summed(n, b2).then_inc(q["pre"], 1)
                    dve.tensor_scalar(g.h[:, ts, :], g.h[:, ts, :], keep, None, ALU.mult).then_inc(q["kept"], 1)
                for n, (p, e) in enumerate(parts):
                    ts = slice(p // P, e // P)
                    dve.wait_ge(q["tanh"], 3 * i + n + 1)
                    dve.wait_ge(q["kept"], 3 * i + n + 1)
                    dve.scalar_tensor_tensor(g.h[:, ts, :], tmp[:, ts, :], DT, g.h[:, ts, :], ALU.mult, ALU.add).then_inc(q["h"], 1)
            dve.wait_ge(q["h"], 3 + 3 * g.STEPS)
            dve.tensor_tensor(g.x[:], g.x[:], g.h[:], ALU.add).then_inc(q["dve"], 1)

        @block.sync
        def _(sp):
            sp.wait_ge(q["dve"], 1)
            sp.dma_start(g.out[0:(T - 1) * P, :].rearrange("(t p) d -> p t d", p=P), g.x[:, 0:T - 1, :]).then_inc(q["done"], 16)
            sp.dma_start(g.out[(T - 1) * P:, :], g.x[0:g.LAST, T - 1, :]).then_inc(q["done"], 16)
            sp.wait_ge(q["done"], 32)


_INS = ["x", "src", "dst", "edge_attr_16", "edge_weight1", "L0_gnn_batch_num", "L0_gnn_W1", "L0_gnn_W2", "L0_gnn_Wo",
        "L0_gnn_Wn", "L0_gnn_gamma", "L0_gnn_beta", "L1_gnn_W_w", "L1_gnn_W_b", "L1_gnn_a_w", "L1_gnn_a_b",
        "L2_gnn_weights", "L2_gnn_atts", "L2_gnn_biases", "L2_gnn_edge_ws", "L2_gnn_edge_bs", "L3_gnn_W_in",
        "L3_gnn_b_in", "L3_gnn_W1", "L3_gnn_b1", "L3_gnn_W2", "L3_gnn_b2", "L3_gnn_clearance"]


def kernel(**inputs):
    import numpy as _np
    import concourse.bacc as _bacc
    from concourse import mybir as _mybir
    from concourse.bass_utils import run_bass_kernel_spmd as _run

    nc = _bacc.Bacc("TRN2", target_bir_lowering=False, num_devices=1)
    arrays, views = {}, {}
    for name in _INS:
        v = _np.ascontiguousarray(inputs[name])
        arrays[f"in_{name}"] = v
        views[name] = nc.dram_tensor(f"in_{name}", v.shape, _mybir.dt.from_np(v.dtype), kind="ExternalInput").ap()
    out = nc.dram_tensor("out_0", inputs["x"].shape, _mybir.dt.float32, kind="ExternalOutput").ap()
    graph_kernel(nc, views, out)
    r = _run(nc, [arrays], core_ids=[0])
    return r.results[0]["out_0"]
```

```python
from contextlib import ExitStack

import concourse.bass as bass
from concourse import mybir

F32 = mybir.dt.float32
BF16 = mybir.dt.bfloat16
F16 = mybir.dt.float16
I32 = mybir.dt.int32
ALU = mybir.AluOpType
ACT = mybir.ActivationFunctionType
AX_X = mybir.AxisListType.X

P = 128
BIG = 1.0e30
NA = 17
REC = 24
(R_SHI, R_SLO, R_DHI, R_DLO, R_W, R_ORIG, R_SRC, R_ATTR) = range(8)
R_REAL = R_ATTR + NA - 1
HALF = 64
RING = 6
ALL_ONE = (16 ** RING - 1) // 15


class Chain:

    def __init__(self, eng, done, start=0):
        self.eng, self.done, self.start, self.n = eng, done, start, 0

    def step(self, ins):
        self.n += 1
        ins.then_inc(self.done, 1)
        self.eng.wait_ge(self.done, self.start + self.n)


class Lot:

    def __init__(self, area):
        self.area, self.at = area, 0

    def take(self, shape, dt=F32):
        n = 1
        for k in shape[1:]:
            n *= k
        size = mybir.dt.size(dt) * n
        view = self.area[0:shape[0], self.at // 2:(self.at + size) // 2].bitcast(dt)
        self.at += -(-size // 32) * 32
        assert self.at <= 2 * self.area.shape[1]
        names = "abcd"[:len(shape) - 1]
        return view.rearrange(f"p ({' '.join(names)}) -> p {' '.join(names)}", **dict(zip(names, shape[1:])))


class Graph:
    pass


class Stage:

    def __init__(self, nc):
        self.nc, self.first = nc, min(nc.free_semaphores)
        self.used, self.held = 0, ExitStack()

    def sem(self, name):
        self.used += 1
        return self.held.enter_context(self.nc.semaphore(name, num=self.first + self.used - 1))

    def clear(self):
        self.nc.gpsimd.sem_clear(range(self.first, self.first + self.used))
        self.nc.all_engine_barrier()

    def end(self):
        if self.used:
            self.clear()
        self.held.close()
        self.used, self.held = 0, ExitStack()


def graph_kernel(nc, a, out):
    N, D = a["x"].shape
    E = a["src"].shape[0]
    T = -(-N // P)
    LAST = N - (T - 1) * P
    NP = T * P
    EA = E + N
    UP = 125
    UE, UN = E // UP, N // UP
    UC = UE + UN
    assert UP * UE == E and UP * UN == N and UC % 10 == 0
    USED = (EA + T * (P - 1)) // P
    CH = -(-USED // RING) * RING
    EARLY = -(-USED // (RING + 1))
    EARLY0 = EARLY * RING
    G = 2
    GC = 96
    NCH = G * GC
    assert CH <= NCH
    H1, F1 = a["L1_gnn_a_w"].shape[0], a["L1_gnn_a_w"].shape[1] // 2
    L, _, HF2 = a["L2_gnn_weights"].shape
    H2, F2 = a["L2_gnn_atts"].shape[1], a["L2_gnn_atts"].shape[2] // 2
    HID = a["L3_gnn_W1"].shape[1]
    STEPS, DT = 12, 0.5
    AT = H2 * NA
    ATT0 = 5 * 512

    table = nc.dram_tensor("node_rows", [NP, HF2], F32).ap()
    table1 = nc.dram_tensor("node_rows_narrow", [NP, D], F32).ap()
    sorted_d = nc.dram_tensor("sorted_edges", [NCH * P, REC], F32).ap()

    ctx = ExitStack()
    with ctx:
        def sb(name, shape, dt=F32):
            return ctx.enter_context(nc.sbuf_tensor(name, shape, dt))

        ps = ctx.enter_context(nc.psum_tensor("ps", [P, 4096], F32))

        lane = sb("lane", [P, P])
        lane16 = sb("lane16", [P, P], BF16)
        part = sb("part", [P, 1])
        ident = sb("ident", [P, P])
        ident16 = sb("ident16", [P, P], F16)
        identb = sb("identb", [P, P], BF16)
        upper = sb("upper", [P, P])
        lower = sb("lower", [P, P])
        ones = sb("ones", [P, P])
        zerob = sb("zerob", [P, 512], BF16)
        tens = sb("tens", [P, 10])
        nodeid = sb("nodeid", [P, NP], F16)
        chunkid = sb("chunkid", [P, NCH])
        x = sb("x_sb", [P, T, D])
        h = sb("h_sb", [P, T, D])
        hT = sb("hT", [P, NP])
        wide = sb("wide", [P, T, HF2])
        small = sb("small", [P, T, 8])
        stat = sb("stat", [P, 4, T])
        rec = sb("rec", [P, NCH, REC])
        arena = sb("arena", [P, 2, NCH * P], BF16)
        onehotT = arena[:, 0, :]
        NB = NP // HALF
        blockmask = arena[:, 1, 0:NCH * 2 * NB].rearrange("p (c s b) -> p c s b", s=2, b=NB)
        early = arena[:, 1, NCH * 2 * NB:NCH * 2 * NB + 2 * EARLY * HF2].bitcast(F32)
        idx = sb("idx", [P, 2, NCH], I32)
        round_tiles = sb("round_tiles", [P, NCH // RING, 2], I32)
        tile_end = sb("tile_end", [P, T], I32)
        ring = sb("ring", [P, RING, HF2])
        slot_idx = sb("slot_idx", [P, RING], I32)
        scratch = sb("scratch", [P, 4000])
        carry_in = sb("carry_in", [4, 2, NCH])
        carry_on = sb("carry_on", [4, 2, NCH])
        reset = sb("reset", [GC, 2, 4, G, P], BF16)
        unreal = sb("unreal", [P, NCH])
        logits = sb("logits", [P, NCH, 4])
        attr_part = sb("attr_part", [P, NCH, L * H2])
        w0 = logits[:].rearrange("p c h -> p (c h)")[:, 0:4 * D].rearrange("p (n d) -> p n d", n=4)
        w1x = sb("w1x", [P, D + 2 * H1])
        w2x = sb("w2x", [P, L, HF2 + 2 * H2])
        ew = sb("ew", [AT, L, D])
        attr_vec = sb("attr_vec", [NA, L * H2])
        bias1 = sb("bias1", [P, D + 2 * H1])
        ab1 = sb("ab1", [P, H1])
        bias2 = sb("bias2", [P, L, D])
        floor2 = sb("floor2", [P, L])
        cols = sb("cols", [P, 8])

        g = Graph()
        g.nc, g.a, g.out, g.N, g.D, g.T = nc, a, out, N, D, T
        g.LAST, g.NP, g.E, g.EA, g.UP, g.UE = LAST, NP, E, EA, UP, UE
        g.UN, g.UC, g.CH, g.G, g.GC, g.NCH = UN, UC, CH, G, GC, NCH
        g.H1, g.F1, g.H2, g.F2, g.L, g.HF2 = H1, F1, H2, F2, L, HF2
        g.HID, g.STEPS, g.DT, g.AT, g.ATT0, g.table = HID, STEPS, DT, AT, ATT0, table
        g.table1, g.sorted_d, g.ps, g.lane, g.lane16, g.part = table1, sorted_d, ps, lane, lane16, part
        g.ident, g.ident16, g.identb, g.upper, g.lower, g.ones = ident, ident16, identb, upper, lower, ones
        g.zerob, g.tens, g.nodeid, g.chunkid, g.x, g.h = zerob, tens, nodeid, chunkid, x, h
        g.hT, g.wide, g.small, g.stat, g.rec, g.arena, g.onehotT = hT, wide, small, stat, rec, arena, onehotT
        g.blockmask, g.idx, g.round_tiles, g.tile_end, g.ring, g.slot_idx, g.scratch = blockmask, idx, round_tiles, tile_end, ring, slot_idx, scratch
        g.carry_in, g.carry_on, g.reset, g.unreal, g.logits, g.attr_part = carry_in, carry_on, reset, unreal, logits, attr_part
        g.w0, g.w1x, g.w2x, g.ew, g.attr_vec, g.bias1, g.ab1 = w0, w1x, w2x, ew, attr_vec, bias1, ab1
        g.bias2, g.floor2, g.cols = bias2, floor2, cols
        g.EARLY, g.EARLY0, g.early = EARLY, EARLY0, early
        g.chunk_rows = sorted_d.rearrange("(c p) k -> p c k", p=P)
        g.got = [ctx.enter_context(nc.semaphore(f"gathered{k}")) for k in range(RING)]
        g.put = [ctx.enter_context(nc.semaphore(f"scattered{k}")) for k in range(2)]
        g.got_early = ctx.enter_context(nc.semaphore("gathered_early"))
        g.gathered_early = 0
        g.gathered = 0
        g.stage = Stage(nc)
        g.sem = g.stage.sem
        g.scan_a, g.scan_b = h[:].rearrange("p t d -> p (t d)"), hT[:]
        for work in (constants, sort_edges, sorted_views, attribute_logits, norm0, block0, norm1, block1, norm2, block2, norm3, block3):
            work(g)
            g.stage.end()
    return nc


def norm0(g):
    node_norm(g, "n0")


def norm1(g):
    node_norm(g, "n1")


def norm2(g):
    node_norm(g, "n2")


def norm3(g):
    node_norm(g, "n3")


def constants(g):
    nc = g.nc
    made, split, xin = g.sem("const_made"), g.sem("const_dve"), g.sem("x_loaded")
    T, LAST, NP = g.T, g.LAST, g.NP
    with nc.Block(name="constants") as block:
        @block.gpsimd
        def _(pool):
            pool.iota(g.lane[:], [[1, P]], base=1, channel_multiplier=0, allow_small_or_imprecise_dtypes=True)
            pool.iota(g.lane16[:], [[1, P]], base=1, channel_multiplier=0, allow_small_or_imprecise_dtypes=True)
            pool.iota(g.part[:], [[0, 1]], base=1, channel_multiplier=1, allow_small_or_imprecise_dtypes=True)
            pool.iota(g.tens[:], [[1, T]], base=0, channel_multiplier=0, allow_small_or_imprecise_dtypes=True)
            pool.iota(g.nodeid[:], [[1, NP]], base=0, channel_multiplier=0, allow_small_or_imprecise_dtypes=True)
            pool.iota(g.chunkid[:], [[1, g.NCH]], base=0, channel_multiplier=0,
                      allow_small_or_imprecise_dtypes=True).then_inc(made, 1)

        @block.vector
        def _(dve):
            dve.memset(g.x[:, T - 1, :], 0.0).then_inc(split, 1)
            dve.memset(g.ones[:], 1.0)
            dve.memset(g.zerob[:], 0.0)
            dve.wait_ge(made, 1)
            for out, op in ((g.ident, ALU.is_equal), (g.ident16, ALU.is_equal), (g.identb, ALU.is_equal),
                            (g.upper, ALU.is_gt), (g.lower, ALU.is_lt)):
                dve.tensor_scalar(out[:], g.lane[:], g.part[:, 0:1], None, op)

        @block.sync
        def _(sp):
            sp.dma_start(g.x[:, 0:T - 1, :], g.a["x"][0:(T - 1) * P, :].rearrange("(t p) d -> p t d", p=P)).then_inc(xin, 16)
            sp.wait_ge(split, 1)
            sp.dma_start(g.x[0:LAST, T - 1, :], g.a["x"][(T - 1) * P:, :]).then_inc(xin, 16)
            sp.wait_ge(xin, 32)


def sort_edges(g):
    nc, a = g.nc, g.a
    UP, UC, UE, UN, T, NCH = g.UP, g.UC, g.UE, g.UN, g.T, g.NCH
    B = 5
    PAIRS = UC // (2 * B)
    rec, scr = g.rec, g.scratch
    s_in, s_self, s_dve = g.sem("sort_in"), g.sem("sort_self"), g.sem("sort_dve")
    s_hot, s_tr, s_ev = g.sem("sort_onehot"), g.sem("sort_transposed"), g.sem("sort_evacuated")
    s_cnt, s_base, s_look, s_rank = g.sem("sort_counted"), g.sem("sort_base"), g.sem("sort_looked"), g.sem("sort_ranked")
    s_zero, s_pos = g.sem("sort_zeroed"), g.sem("sort_positions")
    s_put = g.put
    s_stage, s_round, s_dst16 = g.sem("sort_staged"), g.sem("sort_put_round"), g.sem("sort_dst16")

    if True:
        lot = Lot(g.arena[:, 1, :])

        def sb(name, shape, dt=F32):
            return lot.take(shape, dt)
        ends_i = sb("ends_i", [P, 2, UC], I32)
        digits_i = sb("digits_i", [P, 4, UC], I32)
        attr_in = sb("attr_in", [P, UE, 16])
        w_in = sb("w_in", [P, UE])
        dst16 = sb("dst16", [P, UC], F16)
        dstf = sb("dstf", [P, UC])
        dhi = sb("dhi", [P, UC, T], BF16)
        hot = sb("hot", [P, 2, B, P], BF16)
        before = sb("before", [P, UC, 2, T], BF16)
        rank = sb("rank", [P, UC])
        eqs = sb("eqs", [P, 2, B, P], BF16)
        pos = sb("pos", [P, UC], I32)
        posf = sb("posf", [P, UC])
        stage = sb("stage", [P, 2, RING, REC])
        stage_i = sb("stage_i", [P, 2, RING], I32)
        nch = sb("nch", [P, 6, T])
        nch_i = sb("nch_i", [P, T], I32)
        tilef = sb("tilef", [P, NCH])
        past = sb("past", [P, NCH, T])
        packed = sb("packed", [P, NCH // RING])
        cnt = scr[:, 0:UC * T].rearrange("p (c t) -> p c t", t=T)
        cum = scr[:, UC * T:2 * UC * T].rearrange("p (c t) -> p c t", t=T)
        picked = scr[:, 0:2 * UC * T].rearrange("p (c s t) -> p c s t", s=2, t=T)
        hotT = g.arena[:, 0, 0:UC * P].rearrange("p (c e) -> p c e", e=P)
        bank = [g.ps[:, 512 * k:512 * k + 512] for k in range(8)]

        with nc.Block(name="sort") as block:
            @block.sync
            def _(sp):
                sp.dma_start(ends_i[0:UP, 1, 0:UE], a["dst"].rearrange("(p c) -> p c", c=UE)).then_inc(s_in, 16)
                sp.dma_start(ends_i[0:UP, 0, 0:UE], a["src"].rearrange("(p c) -> p c", c=UE)).then_inc(s_in, 16)
                sp.dma_start(w_in[0:UP, :], a["edge_weight1"].rearrange("(p c) o -> p (c o)", c=UE)).then_inc(s_in, 16)
                sp.dma_start(attr_in[0:UP], a["edge_attr_16"].rearrange("(p c) k -> p c k", c=UE)).then_inc(s_in, 16)
                sp.wait_ge(s_zero, 1)
                sp.dma_start(g.sorted_d.rearrange("(p c) k -> p (c k)", p=P),
                             rec[:].rearrange("p c k -> p (c k)")).then_inc(s_zero, 16)
                sp.wait_ge(s_zero, 17)

            @block.gpsimd
            def _(pool):
                for side in range(2):
                    last = pool.iota(ends_i[0:UP, side, UE:UC], [[1, UN]], base=0, channel_multiplier=UN)
                last.then_inc(s_self, 1)
                with pool.Fori(0, UC // (2 * RING)) as i:
                    for u in range(2):
                        pool.wait_ge(s_zero, 17)
                        pool.wait_ge(s_stage, 2 * i + u + 1)
                        pool.sem_inc(s_round, 1)
                        for k in range(RING):
                            pool.indirect_dma_start(g.sorted_d, bass.IndirectOffsetOnAxis(ap=stage_i[0:UP, u, k:k + 1], axis=0),
                                                    stage[0:UP, u, k, :], None).then_inc(s_put[u], 16)
                for u in range(2):
                    pool.wait_ge(s_put[u], 16 * RING * (UC // (2 * RING)))

            @block.vector
            def _(dve):
                c = Chain(dve, s_dve)
                dve.memset(rec[:], 0.0).then_inc(s_zero, 1)
                dve.wait_ge(s_in, 64)
                dve.wait_ge(s_self, 1)
                for side in range(2):
                    dve.tensor_scalar(digits_i[0:UP, 2 * side, :], ends_i[0:UP, side, :], 7, None, ALU.arith_shift_right)
                    last = dve.tensor_scalar(digits_i[0:UP, 2 * side + 1, :], ends_i[0:UP, side, :], P - 1, None, ALU.bitwise_and)
                c.step(last)
                dve.wait_ge(s_zero, 17)
                for f, d in ((R_SHI, 0), (R_SLO, 1), (R_DHI, 2)):
                    dve.tensor_copy(rec[0:UP, 0:UC, f], digits_i[0:UP, d, :])
                dve.tensor_scalar(rec[0:UP, 0:UC, R_DLO], digits_i[0:UP, 3, :], 1.0, None, ALU.add)
                dve.tensor_copy(rec[0:UP, 0:UC, R_SRC], ends_i[0:UP, 0, :])
                dve.tensor_copy(rec[0:UP, 0:UE, R_W], w_in[0:UP, :])
                dve.memset(rec[0:UP, 0:UE, R_ORIG], 1.0)
                dve.memset(rec[0:UP, 0:UC, R_REAL], 1.0)
                dve.tensor_copy(rec[0:UP, 0:UE, R_ATTR:R_ATTR + 16], attr_in[0:UP])
                c.step(dve.tensor_copy(dstf[0:UP, :], ends_i[0:UP, 1, :]))
                c.step(dve.tensor_tensor(dhi[0:UP], g.tens[0:UP, :].unsqueeze(1).broadcast_to([UP, UC, T]),
                                         rec[0:UP, 0:UC, R_DHI].unsqueeze(2).broadcast_to([UP, UC, T]), ALU.is_equal))
                with dve.Fori(0, PAIRS) as i:
                    for u in range(2):
                        dve.wait_ge(s_cnt, 2 * i + u + 1)
                        dve.tensor_tensor(hot[0:UP, u], g.lane16[0:UP, :].unsqueeze(1).broadcast_to([UP, B, P]),
                                          rec[0:UP, bass.ds((2 * i + u) * B, B), R_DLO].unsqueeze(2).broadcast_to([UP, B, P]),
                                          ALU.is_equal).then_inc(s_hot, 1)
                dve.wait_ge(s_ev, 2 + 2 * PAIRS)
                for t in range(T):
                    last = dve.tensor_tensor_scan(cum[:, :, t], g.ones[:, 0:1].broadcast_to([P, UC]), cnt[:, :, t],
                                                  0.0, ALU.mult, ALU.add)
                last.then_inc(s_base, 1)
                dve.wait_ge(s_look, 1)
                dve.tensor_copy(nch[:, 0, :], bank[0][:, 0:T])
                c.step(dve.tensor_scalar(nch_i[:], bank[1][:, 0:T], float(P - 1), None, ALU.add))
                c.step(dve.tensor_scalar(nch_i[:], nch_i[:], 7, None, ALU.arith_shift_right))
                c.step(dve.tensor_copy(nch[:, 1, :], nch_i[:]))
                c.step(dve.tensor_tensor_scan(nch[:, 2, :], g.ones[:, 0:T], nch[:, 1, :], 0.0, ALU.mult, ALU.add))
                c.step(dve.tensor_tensor(nch[:, 3, :], nch[:, 2, :], nch[:, 1, :], ALU.subtract))
                c.step(dve.scalar_tensor_tensor(nch[:, 4, :], nch[:, 3, :], float(P), nch[:, 0, :], ALU.mult, ALU.add))
                c.step(dve.tensor_tensor(cum, cum, cnt, ALU.subtract))
                c.step(dve.tensor_tensor(cum, cum, nch[:, 4, :].unsqueeze(1).broadcast_to([P, UC, T]), ALU.add))
                c.step(dve.tensor_copy(before[:, :, 0], cum))
                dve.tensor_tensor(before[:, :, 1], cum, before[:, :, 0], ALU.subtract).then_inc(s_base, 1)
                c.step(dve.tensor_tensor(past[:, :, 0:T - 1], g.chunkid[:].unsqueeze(2).broadcast_to([P, NCH, T - 1]),
                                         nch[:, 2, 0:T - 1].unsqueeze(1).broadcast_to([P, NCH, T - 1]), ALU.is_ge))
                c.step(dve.tensor_reduce(tilef[:], past[:, :, 0:T - 1], AX_X, ALU.add))
                c.step(dve.tensor_scalar(tilef[:], tilef[:], 1.0, None, ALU.add))
                tiles = tilef.rearrange("p (r k) -> p r k", k=RING)
                for k in range(RING - 2, -1, -1):
                    c.step(dve.scalar_tensor_tensor(packed, packed if k < RING - 2 else tiles[:, :, RING - 1], 16.0, tiles[:, :, k],
                                                    ALU.mult, ALU.add))
                dve.tensor_copy(g.round_tiles[:, :, 0], packed)
                c.step(dve.memset(g.round_tiles[:, :, 1], ALL_ONE))
                dve.tensor_scalar(g.round_tiles[:, 0:g.EARLY, 1], tilef[:, g.EARLY0:g.EARLY0 + g.EARLY], float(ALL_ONE - 1), None, ALU.add)
                dve.tensor_copy(g.tile_end[:, 0:T - 1], nch[:, 2, 0:T - 1])
                dve.memset(g.tile_end[:, T - 1:T], g.CH)
                with dve.Fori(0, PAIRS) as i:
                    for u in range(2):
                        dve.wait_ge(s_look, 2 * i + u + 2)
                        for k in range(B):
                            col = (2 * i + u) * B + k
                            dve.scalar_tensor_tensor(eqs[0:UP, u, k, 0:UP], bank[2 + 3 * u + k // 4][0:UP, (k % 4) * P:(k % 4) * P + UP],
                                                     dstf[0:UP, bass.ds(col, 1)], g.lower[0:UP, 0:UP], ALU.is_equal, ALU.mult,
                                                     accum_out=rank[0:UP, bass.ds(col, 1)])
                        dve.tensor_tensor(picked[0:UP, bass.ds((2 * i + u) * B, B)],
                                          bank[4 + 3 * u][0:UP, 0:2 * B * T].rearrange("p (c s t) -> p c s t", s=2, t=T),
                                          dhi[0:UP, bass.ds((2 * i + u) * B, B), :].unsqueeze(2).broadcast_to([UP, B, 2, T]),
                                          ALU.mult).then_inc(s_rank, 1)
                dve.wait_ge(s_rank, 2 + 2 * PAIRS)
                c.step(dve.tensor_reduce(posf[0:UP, :], picked[0:UP].rearrange("p c s t -> p c (s t)"), AX_X, ALU.add))
                dve.tensor_tensor(pos[0:UP, :], posf[0:UP, :], rank[0:UP, :], ALU.add).then_inc(s_pos, 1)

            @block.tensor
            def _(pe):
                pe.sem_inc(s_cnt, 2)
                pe.wait_ge(s_dve, 1)
                with pe.Fori(0, PAIRS) as i:
                    for u in range(2):
                        pe.wait_ge(s_hot, 2 * i + u + 1)
                        pe.wait_ge(s_ev, 2 * i + u + 1)
                        turned = bank[2 + u].bitcast(BF16)
                        for k in range(B):
                            pe.transpose(turned[:, k * P:k * P + UP], hot[0:UP, u, k, :], g.identb[0:UP, 0:UP])
                        for k in range(B):
                            mm = pe.matmul(bank[4 + u][:, k * T:(k + 1) * T], hot[0:UP, u, k, :],
                                           dhi[0:UP, bass.ds((2 * i + u) * B + k, 1), :].rearrange("p o t -> p (o t)"), start=True, stop=True)
                        mm.then_inc(s_cnt, 1)
                pe.wait_ge(s_base, 1)
                pe.wait_ge(s_ev, 2 + 2 * PAIRS)
                pe.matmul(bank[0][:, 0:T], g.upper[:], cum[:, UC - 1, :], start=True, stop=True)
                pe.matmul(bank[1][:, 0:T], g.ones[:], cum[:, UC - 1, :], start=True, stop=True).then_inc(s_look, 1)
                pe.sem_inc(s_rank, 2)
                pe.wait_ge(s_dst16, 1)
                pe.wait_ge(s_base, 2)
                with pe.Fori(0, PAIRS) as i:
                    for u in range(2):
                        pe.wait_ge(s_rank, 2 * i + u + 1)
                        for k in range(B):
                            col = (2 * i + u) * B + k
                            pe.matmul(bank[4 + 3 * u][0:UP, 2 * k * T:2 * (k + 1) * T],
                                      hotT[:, bass.ds(col, 1), 0:UP].rearrange("p o e -> p (o e)"),
                                      before[:, bass.ds(col, 1)].rearrange("p o s t -> p (o s t)"), start=True, stop=True)
                            mm = pe.matmul(bank[2 + 3 * u + k // 4][0:UP, (k % 4) * P:(k % 4) * P + UP],
                                           dst16[0:UP, bass.ds(col, 1)].broadcast_to([UP, UP]), g.ident16[0:UP, 0:UP],
                                           start=True, stop=True)
                        mm.then_inc(s_look, 1)

            @block.scalar
            def _(act):
                act.sem_inc(s_ev, 2)
                act.wait_ge(s_in, 64)
                act.wait_ge(s_self, 1)
                act.copy(dst16[0:UP, :], ends_i[0:UP, 1, :]).then_inc(s_dst16, 1)
                with act.Fori(0, PAIRS) as i:
                    for u in range(2):
                        act.wait_ge(s_cnt, 2 * i + u + 3)
                        turned = bank[2 + u].bitcast(BF16)[:, 0:B * P].rearrange("p (c e) -> p c e", e=P)
                        act.copy(hotT[:, bass.ds((2 * i + u) * B, B), 0:UP], turned[:, :, 0:UP])
                        act.copy(cnt[:, bass.ds((2 * i + u) * B, B), :],
                                 bank[4 + u][:, 0:B * T].rearrange("p (c t) -> p c t", t=T)).then_inc(s_ev, 1)
                act.wait_ge(s_pos, 1)
                for u in range(2):
                    act.copy(stage_i[0:UP, u, :], pos[0:UP, u * RING:(u + 1) * RING])
                    act.copy(stage[0:UP, u], rec[0:UP, u * RING:(u + 1) * RING, :]).then_inc(s_stage, 1)
                with act.Fori(1, UC // (2 * RING)) as i:
                    for u in range(2):
                        act.wait_ge(s_put[u], 16 * RING * i)
                        act.copy(stage_i[0:UP, u, :], pos[0:UP, bass.ds((2 * i + u) * RING, RING)])
                        act.copy(stage[0:UP, u], rec[0:UP, bass.ds((2 * i + u) * RING, RING), :]).then_inc(s_stage, 1)

            weights(g, block, s_pos)


def sorted_views(g):
    nc = g.nc
    P_, T, NCH, GC, G = P, g.T, g.NCH, g.GC, g.G
    rec = g.rec
    B = 4
    NB = g.NP // HALF
    BATCHES = NCH // (2 * B)
    s_rec, s_dve, s_hot, s_tr, s_ev = (g.sem(f"view_{n}") for n in ("records", "dve", "onehot", "turned", "copied"))
    s_dst, s_rows, s_near, s_inner, s_carry = (g.sem(f"view_{n}") for n in ("dst", "dst_rows", "first_last", "inner", "carry"))
    bank = [g.ps[:, 512 * k:512 * k + 512] for k in range(8)]
    lot = Lot(g.scratch[:].bitcast(BF16))
    hot = lot.take([P, 2, B, 2, HALF], BF16)
    digits_i = lot.take([P, 2, 2, NCH], I32)
    digits = lot.take([P, 2, NCH, 2])
    dstf = lot.take([P, NCH])
    ends = lot.take([P, 2, 4])
    dstrow = lot.take([P, G, P])
    inner = lot.take([P, G, 4])
    near = lot.take([P, 2, NCH])

    with nc.Block(name="views") as block:
        @block.sync
        def _(sp):
            sp.dma_start(rec[:], g.chunk_rows).then_inc(s_rec, 16)
            sp.wait_ge(s_rec, 16)

        @block.vector
        def _(dve):
            c = Chain(dve, s_dve)
            dve.tensor_scalar(ends[:, 0, :], g.part[:, 0:1].broadcast_to([P, 4]), 1.0, None, ALU.is_equal)
            dve.tensor_scalar(ends[:, 1, :], g.part[:, 0:1].broadcast_to([P, 4]), float(P), None, ALU.is_equal)
            dve.wait_ge(s_rec, 16)
            dve.tensor_copy(g.idx[:, 0, :], rec[:, :, R_SRC])
            dve.tensor_scalar(g.unreal[:], rec[:, :, R_REAL], -1.0, BIG, ALU.add, ALU.mult)
            dve.scalar_tensor_tensor(dstf, rec[:, :, R_DHI], float(P), rec[:, :, R_DLO], ALU.mult, ALU.add).then_inc(s_dst, 1)
            dve.wait_ge(s_dst, 1)
            c.step(dve.tensor_scalar(g.idx[:, 1, :], dstf, -1.0, 0.0, ALU.add, ALU.max))
            for side in range(2):
                dve.tensor_scalar(digits_i[:, 0, side, :], g.idx[:, 1 - side, :], HALF - 1, None, ALU.bitwise_and)
                last = dve.tensor_scalar(digits_i[:, 1, side, :], g.idx[:, 1 - side, :], 6, None, ALU.arith_shift_right)
            c.step(last)
            for side in range(2):
                dve.tensor_copy(digits[:, 0, :, side], digits_i[:, 0, side, :])
                last = dve.tensor_copy(digits[:, 1, :, side], digits_i[:, 1, side, :])
            c.step(last)
            dve.tensor_tensor(g.blockmask[:], g.nodeid[:, 0:NB].unsqueeze(1).unsqueeze(1).broadcast_to([P, NCH, 2, NB]),
                              digits[:, 1].unsqueeze(3).broadcast_to([P, NCH, 2, NB]), ALU.is_equal)
            with dve.Fori(0, BATCHES) as i:
                for u in range(2):
                    dve.wait_ge(s_tr, 2 * i + u + 1)
                    dve.tensor_tensor(hot[:, u], g.nodeid[:, 0:HALF].unsqueeze(1).unsqueeze(1).broadcast_to([P, B, 2, HALF]),
                                      digits[:, 0, bass.ds((2 * i + u) * B, B), :].unsqueeze(3).broadcast_to([P, B, 2, HALF]),
                                      ALU.is_equal).then_inc(s_hot, 1)
            dve.wait_ge(s_rows, 1)
            rows = bank[6][0:GC, 0:G * P].rearrange("p (g e) -> p g e", g=G)
            c.step(dve.tensor_copy(dstrow[0:GC], rows))
            fwd, bwd = g.reset[:, 0, 0], g.reset[:, 1, 0]
            for way, own, nxt, edge in ((fwd, slice(1, P), slice(0, P - 1), 0), (bwd, slice(0, P - 1), slice(1, P), P - 1)):
                dve.tensor_tensor(way[:, :, own], dstrow[0:GC, :, own], dstrow[0:GC, :, nxt], ALU.not_equal)
                last = dve.memset(way[:, :, edge:edge + 1], 1.0)
            c.step(last)
            for way in (fwd, bwd):
                last = dve.tensor_scalar(way, way, -BIG, None, ALU.mult)
            c.step(last)
            for hd in range(1, 4):
                for d in range(2):
                    dve.tensor_copy(g.reset[:, d, hd], g.reset[:, d, 0])
            for k in range(4):
                last = dve.tensor_reduce(inner[0:GC, :, k], fwd[:, :, 1:P], AX_X, ALU.min)
            last.then_inc(s_inner, 1)
            dve.wait_ge(s_near, 1)
            c.step(dve.tensor_copy(near[0:4], bank[7][0:4, 0:2 * NCH].rearrange("p (s c) -> p s c", s=2)))
            dve.memset(g.carry_in[:, 0, 0:1], 1.0)
            dve.memset(g.carry_in[:, 1, NCH - 1:NCH], 1.0)
            for at in (slice(1, NCH), slice(0, NCH - 1)):
                last = dve.tensor_tensor(g.carry_in[:, 0 if at.start else 1, at], near[0:4, 0, 1:NCH], near[0:4, 1, 0:NCH - 1],
                                         ALU.not_equal)
            c.step(last)
            c.step(dve.tensor_scalar(g.carry_in[:], g.carry_in[:], -BIG, None, ALU.mult))
            dve.wait_ge(s_carry, 1)
            for d in range(2):
                dve.tensor_tensor(g.carry_on[:, d, :], g.carry_in[:, d, :], bank[5][0:4, 0:NCH], ALU.add)

        @block.tensor
        def _(pe):
            pe.sem_inc(s_tr, 2)
            pe.wait_ge(s_dst, 1)
            for n in range(G):
                pe.transpose(bank[6][0:GC, n * P:(n + 1) * P], dstf[:, n * GC:(n + 1) * GC], g.ident[:]).then_inc(s_rows, 1) \
                    if n == G - 1 else pe.transpose(bank[6][0:GC, n * P:(n + 1) * P], dstf[:, n * GC:(n + 1) * GC], g.ident[:])
            for side in range(2):
                mm = pe.matmul(bank[7][0:4, side * NCH:(side + 1) * NCH], ends[:, side, :], dstf, start=True, stop=True)
            mm.then_inc(s_near, 1)
            with pe.Fori(0, BATCHES) as i:
                for u in range(2):
                    pe.wait_ge(s_hot, 2 * i + u + 1)
                    pe.wait_ge(s_ev, 2 * i + u + 1)
                    turned = bank[u].bitcast(BF16)
                    for k in range(B):
                        tr = pe.transpose(turned[:, k * P:(k + 1) * P], hot[:, u, k].rearrange("p s e -> p (s e)"), g.identb[:])
                    tr.then_inc(s_tr, 1)
            pe.wait_ge(s_inner, 1)
            for n in range(G):
                tr = pe.transpose(bank[5][0:4, n * GC:(n + 1) * GC], inner[0:GC, n, :], g.ident[0:GC, 0:GC])
            tr.then_inc(s_carry, 1)

        @block.scalar
        def _(act):
            act.sem_inc(s_ev, 2)
            with act.Fori(0, BATCHES) as i:
                for u in range(2):
                    act.wait_ge(s_tr, 2 * i + u + 3)
                    act.copy(g.onehotT[:, bass.ds((2 * i + u) * B * P, B * P)], bank[u].bitcast(BF16)[:, 0:B * P]).then_inc(s_ev, 1)


def weights(g, block, free):
    a, D, L, H1, F1, H2, F2, HF2, AT = g.a, g.D, g.L, g.H1, g.F1, g.H2, g.F2, g.HF2, g.AT
    s_in, s_dve, s_ewn, s_turn, s_v, s_col = (g.sem(f"wts_{n}") for n in ("loaded", "dve", "edge", "turned", "v", "columns"))
    bank = [g.ps[:, 512 * k:512 * k + 512] for k in range(8)]
    lot = Lot(g.scratch[:].bitcast(BF16))
    att = lot.take([P, L * H2 * 2 * F2])
    a1 = lot.take([P, H1 * 2 * F1])
    ewn = lot.take([P, L, H2, NA])
    attj = lot.take([P, L, H2])
    rows = lot.take([P, P])
    NR = 2 * L * H2 + 4
    count = lot.take([P, 1], I32)
    prod = g.wide[:].rearrange("p t f -> p (t f)")
    LOADS = 19

    @block.sync
    def _(sp):
        def load(dst, src):
            sp.dma_start(dst, src).then_inc(s_in, 16)
        load(g.w2x[:, :, 0:HF2], a["L2_gnn_weights"].rearrange("l i o -> i l o"))
        load(g.w1x[:, 0:D], a["L1_gnn_W_w"])
        load(g.bias1[:, 0:D], a["L1_gnn_W_b"].partition_broadcast(P))
        for n, name in enumerate(("W1", "W2", "Wo", "Wn")):
            load(g.w0[:, n, :], a["L0_gnn_" + name])
        load(g.ab1[:], a["L1_gnn_a_b"].partition_broadcast(P))
        load(g.bias2[:].rearrange("p l d -> p (l d)"), a["L2_gnn_biases"].rearrange("l d -> (l d)").partition_broadcast(P))
        load(g.cols[:, 5:6], a["L3_gnn_clearance"].partition_broadcast(P))
        sp.wait_ge(free, 1)
        load(ewn[:, :, :, 0:NA - 1], a["L2_gnn_edge_ws"].rearrange("l (h f) k -> f l h k", h=H2))
        load(rows[0:L * H2, :], a["L2_gnn_edge_bs"].rearrange("l (h f) -> (l h) f", h=H2))
        load(rows[L * H2:2 * L * H2, :], a["L2_gnn_atts"].rearrange("l h f -> (l h) f")[:, F2:])
        load(rows[2 * L * H2:2 * L * H2 + 1, :], a["L0_gnn_gamma"].unsqueeze(0))
        load(rows[2 * L * H2 + 1:2 * L * H2 + 2, :], a["L0_gnn_beta"].unsqueeze(0))
        load(rows[2 * L * H2 + 2:2 * L * H2 + 4, :], a["L3_gnn_b1"].rearrange("(k p) -> k p", p=P))
        load(att, a["L2_gnn_atts"].rearrange("l h f -> (l h f)").partition_broadcast(P))
        load(a1, a["L1_gnn_a_w"].rearrange("h f -> (h f)").partition_broadcast(P))
        load(count, a["L0_gnn_batch_num"][0:1].partition_broadcast(P))
        sp.wait_ge(s_in, 16 * LOADS)

    @block.vector
    def _(dve):
        c = Chain(dve, s_dve)
        dve.memset(g.floor2[:, 0:L - 1], 0.0)
        dve.memset(g.floor2[:, L - 1:L], -3.0e38)
        dve.wait_ge(s_in, 16 * LOADS)
        dve.tensor_copy(g.cols[:, 4:5], count)
        for src, folded, vec in ((g.w1x, g.w1x, a1), (g.bias1, g.bias1, a1)):
            for side in range(2):
                c.step(dve.tensor_tensor(prod[:, 0:D].rearrange("p (h f) -> p h f", h=H1),
                                         src[:, 0:D].rearrange("p (h f) -> p h f", h=H1),
                                         vec.rearrange("p (h s f) -> p h s f", h=H1, s=2)[:, :, side, :], ALU.mult))
                c.step(dve.tensor_reduce(folded[:, D + side * H1:D + (side + 1) * H1],
                                         prod[:, 0:D].rearrange("p (h f) -> p h f", h=H1), AX_X, ALU.add))
        for l in range(L):
            for side in range(2):
                at = (l * 2 + side) % 4 * HF2
                part = prod[:, at:at + HF2].rearrange("p (h f) -> p h f", h=H2)
                c.step(dve.tensor_tensor(part, g.w2x[:, l, 0:HF2].rearrange("p (h f) -> p h f", h=H2),
                                         att.rearrange("p (l h s f) -> p l h s f", l=L, h=H2, s=2)[:, l, :, side, :], ALU.mult))
                c.step(dve.tensor_reduce(g.w2x[:, l, HF2 + side * H2:HF2 + (side + 1) * H2], part, AX_X, ALU.add))
        dve.wait_ge(s_col, 1)
        dve.tensor_copy(ewn[:, :, :, NA - 1], bank[3][:, 0:L * H2].rearrange("p (l h) -> p l h", l=L))
        dve.tensor_copy(attj, bank[3][:, L * H2:2 * L * H2].rearrange("p (l h) -> p l h", l=L)).then_inc(s_ewn, 1)
        dve.tensor_copy(g.cols[:, 0:4], bank[3][:, 2 * L * H2:NR])
        dve.wait_ge(s_turn, 1)
        dve.tensor_copy(g.ew[:].rearrange("k l d -> k (l d)")[:, 0:512], bank[0][0:AT, 0:512])
        dve.tensor_copy(g.ew[:].rearrange("k l d -> k (l d)")[:, 512:L * D], bank[1][0:AT, 0:L * D - 512])
        dve.wait_ge(s_v, 1)
        dve.tensor_copy(g.attr_vec[:], bank[2][0:NA, 0:L * H2])

    @block.tensor
    def _(pe):
        pe.wait_ge(s_in, 16 * LOADS)
        pe.transpose(bank[3][:, 0:NR], rows[0:NR, :], g.ident[0:NR, 0:NR]).then_inc(s_col, 1)
        pe.wait_ge(s_ewn, 1)
        for l in range(L):
            tr = pe.transpose(bank[l // 4][0:AT, (l % 4) * D:(l % 4) * D + D],
                              ewn[:, l].rearrange("p h k -> p (h k)"), g.ident[:])
        tr.then_inc(s_turn, 1)
        for l in range(L):
            for hd in range(H2):
                mm = pe.matmul(bank[2][0:NA, l * H2 + hd:l * H2 + hd + 1], ewn[:, l, hd, :], attj[:, l, hd:hd + 1],
                               start=True, stop=True)
        mm.then_inc(s_v, 1)


def attribute_logits(g):
    nc, L, H2, NCH = g.nc, g.L, g.H2, g.NCH
    q = {n: g.sem(f"attr_{n}") for n in ("weights", "staged", "turned", "copied", "products", "taken")}
    bank = [g.ps[:, 512 * k:512 * k + 512] for k in range(8)]
    B, ROWS = 4, 32
    PAIRS = NCH // (2 * B)
    lot = Lot(g.scratch[:].bitcast(BF16))
    attr = lot.take([P, 2, B, ROWS])
    attrT = lot.take([P, 2, P])
    four = lot.take([P, B, L * H2])

    with nc.Block(name="attribute_logits") as block:
        @block.vector
        def _(dve):
            dve.memset(attr[:], 0.0).then_inc(q["weights"], 1)
            dve.memset(four[:], 0.0).then_inc(q["weights"], 1)
            dve.wait_ge(q["weights"], 2)
            for k in range(B):
                dve.tensor_copy(four[ROWS * k:ROWS * k + NA, k, :], g.attr_vec[:]).then_inc(q["weights"], 1)

            def stage(n, u):
                dve.wait_ge(q["turned"], n + 1)
                dve.tensor_copy(attr[:, u, :, 0:NA], g.rec[:, bass.ds(n * B, B), R_ATTR:R_ATTR + NA]).then_inc(q["staged"], 1)

            def take(n, u):
                dve.wait_ge(q["products"], n + 1)
                dve.tensor_copy(g.attr_part[:, bass.ds(n * B, B), :],
                                bank[6 + u][:, 0:B * L * H2].rearrange("p (c q) -> p c q", c=B)).then_inc(q["taken"], 1)

            for u in range(2):
                stage(u, u)
            with dve.Fori(0, PAIRS - 1) as i:
                for u in range(2):
                    stage(2 * i + 2 + u, u)
                    take(2 * i + u, u)
            for u in range(2):
                take(2 * PAIRS - 2 + u, u)

        @block.tensor
        def _(pe):
            def turn(n, u):
                pe.wait_ge(q["staged"], n + 1)
                pe.wait_ge(q["copied"], n + 1)
                pe.transpose(bank[4 + u][:, 0:P], attr[:, u].rearrange("p c r -> p (c r)"), g.ident[:]).then_inc(q["turned"], 1)

            def product(n, u):
                pe.wait_ge(q["copied"], n + 3)
                pe.wait_ge(q["taken"], n + 1)
                pe.matmul(bank[6 + u][:, 0:B * L * H2], attrT[:, u, :], four.rearrange("p c q -> p (c q)"),
                          start=True, stop=True).then_inc(q["products"], 1)

            for credit in ("copied", "turned", "taken"):
                pe.sem_inc(q[credit], 2)
            pe.wait_ge(q["weights"], 2 + B)
            turn(0, 0)
            with pe.Fori(0, PAIRS - 1) as i:
                for u in range(2):
                    turn(2 * i + u + 1, 1 - u)
                    product(2 * i + u, u)
            turn(2 * PAIRS - 1, 1)
            for u in range(2):
                product(2 * PAIRS - 2 + u, u)

        @block.scalar
        def _(act):
            with act.Fori(0, PAIRS) as i:
                for u in range(2):
                    act.wait_ge(q["turned"], 2 * i + u + 3)
                    act.copy(attrT[:, u, :], bank[4 + u][:, 0:P]).then_inc(q["copied"], 1)


def node_norm(g, name):
    nc, T, D = g.nc, g.T, g.D
    s_dve, s_var, s_std, s_h, s_turn, s_copy = (g.sem(f"{name}_{n}") for n in ("dve", "var", "std", "h", "turned", "copied"))
    st = g.stat
    with nc.Block(name=name) as block:
        @block.vector
        def _(dve):
            c = Chain(dve, s_dve)
            wide = [P, T, D]
            c.step(dve.tensor_reduce(st[:, 0, :], g.x[:], AX_X, ALU.add))
            c.step(dve.tensor_scalar(st[:, 1, :], st[:, 0, :], 1.0 / D, None, ALU.mult))
            c.step(dve.tensor_tensor(g.h[:], g.x[:], st[:, 1, :].unsqueeze(2).broadcast_to(wide), ALU.subtract))
            c.step(dve.tensor_tensor(g.wide[:, :, 0:D], g.h[:], g.h[:], ALU.mult))
            c.step(dve.tensor_reduce(st[:, 2, :], g.wide[:, :, 0:D], AX_X, ALU.add))
            dve.tensor_scalar(st[:, 2, :], st[:, 2, :], 1.0 / D, 1.0e-5, ALU.mult, ALU.add).then_inc(s_var, 1)
            dve.wait_ge(s_std, 1)
            c.step(dve.reciprocal(st[:, 1, :], st[:, 3, :]))
            dve.scalar_tensor_tensor(g.h[:], g.h[:], 0.0, st[:, 1, :].unsqueeze(2).broadcast_to(wide), ALU.max, ALU.mult).then_inc(s_h, 1)

        @block.scalar
        def _(act):
            act.wait_ge(s_var, 1)
            act.activation(st[:, 3, :], st[:, 2, :], ACT.Sqrt).then_inc(s_std, 1)
            turn_copies(g, act, s_turn)

        @block.tensor
        def _(pe):
            pe.wait_ge(s_h, 1)
            turn_nodes(g, pe, s_turn)


def turn_nodes(g, pe, turned, banks=0):
    for t in range(g.T):
        tr = pe.transpose(g.ps[:, 512 * banks + t * P:512 * banks + (t + 1) * P], g.h[:, t, :], g.ident[:])
        if t % 4 == 3 or t == g.T - 1:
            tr.then_inc(turned, 1)


def turn_copies(g, act, turned, banks=0, start=0):
    for n, at in enumerate(range(0, g.NP, 512)):
        act.wait_ge(turned, start + n + 1)
        to = min(at + 512, g.NP)
        last = act.copy(g.hT[:, at:to], g.ps[:, 512 * banks + at:512 * banks + to])
    return last


def halves(g):
    return [(at, min(at + 512, g.NP)) for at in range(0, g.NP, 512)]


def pool_gathers(pool, g, rows, width, staged, free, round_, got, rounds):
    H = RING // 2
    with pool.Fori(0, rounds) as i:
        for u in range(2):
            pool.wait_ge(staged, 2 * i + u + 1)
            for k in range(H * u, H * (u + 1)):
                pool.wait_ge(free, i * RING + k + 1)
                pool.sem_inc(round_, 1)
                pool.indirect_dma_start(g.ring[:, k, 0:width], None, rows,
                                        bass.IndirectOffsetOnAxis(ap=g.slot_idx[:, k:k + 1], axis=0)).then_inc(got[k], 16)


def block0(g):
    nc, T, D, N, NP, CH = g.nc, g.T, g.D, g.N, g.NP, g.CH
    bank = [g.ps[:, 512 * k:512 * k + 512] for k in range(8)]
    flat = g.wide[:].rearrange("p t f -> p (t f)")
    l1T, h2T = flat[:, 0:NP], flat[:, NP:2 * NP]
    H = RING // 2
    s_mm, s_sc, s_act, s_h2, s_h2c, s_st = (g.sem(f"b0_{n}") for n in
                                            ("hidden", "scaled", "leaky", "h2", "h2_copied", "stored"))
    with nc.Block(name="b0_dense") as block:
        @block.tensor
        def _(pe):
            for n, (p, q) in enumerate(halves(g)):
                pe.matmul(bank[n][:, 0:q - p], g.w0[:, 0, :], g.hT[:, p:q], start=True, stop=True).then_inc(s_mm, 1)
            for n, (p, q) in enumerate(halves(g)):
                pe.wait_ge(s_act, n + 1)
                for t in range(p // P, q // P):
                    mm = pe.matmul(bank[3 + n][:, t * P - p:t * P - p + P], l1T[:, t * P:(t + 1) * P], g.w0[:, 1, :],
                                   start=True, stop=True)
                mm.then_inc(s_h2, 1)
            for n, (p, q) in enumerate(halves(g)):
                pe.matmul(bank[n][:, 0:q - p], g.w0[:, 1, :], l1T[:, p:q], start=True, stop=True).then_inc(s_h2, 1)

        @block.scalar
        def _(act):
            for n, (p, q) in enumerate(halves(g)):
                act.wait_ge(s_mm, n + 1)
                act.activation(l1T[:, p:q], bank[n][:, 0:q - p], ACT.Copy, scale=0.01).then_inc(s_sc, 1)
            for n, (p, q) in enumerate(halves(g)):
                act.wait_ge(s_h2, n + 4)
                act.copy(h2T[:, p:q], bank[n][:, 0:q - p])

        @block.vector
        def _(dve):
            for n, (p, q) in enumerate(halves(g)):
                dve.wait_ge(s_sc, n + 1)
                dve.tensor_tensor(l1T[:, p:q], bank[n][:, 0:q - p], l1T[:, p:q], ALU.max).then_inc(s_act, 1)
            for n, (p, q) in enumerate(halves(g)):
                dve.wait_ge(s_h2, n + 1)
                dve.tensor_copy(g.h[:, p // P:q // P, :].rearrange("p t d -> p (t d)"), bank[3 + n][:, 0:q - p]).then_inc(s_h2c, 1)

        @block.sync
        def _(sp):
            sp.wait_ge(s_h2c, 3)
            sp.dma_start(g.table1.rearrange("(t p) d -> p t d", p=P), g.h[:]).then_inc(s_st, 16)
            sp.wait_ge(s_st, 16)

    staged, free, round_ = g.sem("b0_staged"), g.sem("b0_slot_free"), g.sem("b0_round")
    got, before = g.got, g.gathered
    g.gathered += 16 * (CH // RING)
    s_hi, s_mid, s_rest, s_lo, s_sum = (g.sem(f"b0_{n}") for n in ("hi", "mid", "rest", "lo", "summed"))
    lot = Lot(g.scratch[:].bitcast(BF16))
    parts = lot.take([P, 3, 3, D], BF16)
    rest = lot.take([P, 3, D])
    hot = lot.take([P, 3, NP], BF16)
    with nc.Block(name="b0_edges") as block:
        @block.gpsimd
        def _(pool):
            pool.sem_inc(free, RING)
            pool_gathers(pool, g, g.table1, D, staged, free, round_, got, CH // RING)

        @block.scalar
        def _(act):
            for u in range(2):
                act.copy(g.slot_idx[:, u * H:(u + 1) * H], g.idx[:, 1, u * H:(u + 1) * H]).then_inc(staged, 1)
            with act.Fori(0, CH // RING) as i:
                for u in range(2):
                    for k in range(H * u, H * u + H):
                        c, m = i * RING + k, k % 3
                        act.wait_ge(got[k], before + 16 * (i + 1))
                        act.wait_ge(s_sum, c + 1)
                        act.activation(parts[:, m, 0, :], g.ring[:, k, 0:D], ACT.Copy,
                                       scale=g.rec[:, bass.ds(c, 1), R_W]).then_inc(s_hi, 1)
                        act.wait_ge(s_rest, c + 1)
                        act.copy(parts[:, m, 1, :], rest[:, m, :]).then_inc(s_mid, 1)
                    act.copy(g.slot_idx[:, H * u:H * u + H], g.idx[:, 1, bass.ds((2 * i + u + 2) * H, H)]).then_inc(staged, 1)

        @block.vector
        def _(dve):
            with dve.Fori(0, CH // RING) as i:
                for k in range(RING):
                    c, m = i * RING + k, k % 3
                    dve.wait_ge(s_hi, c + 1)
                    dve.scalar_tensor_tensor(rest[:, m, :], g.ring[:, k, 0:D], g.rec[:, bass.ds(c, 1), R_W], parts[:, m, 0, :],
                                             ALU.mult, ALU.subtract).then_inc(s_rest, 1)
                    dve.tensor_scalar(hot[:, m, :], g.nodeid[:], g.rec[:, bass.ds(c, 1), R_SRC], None, ALU.is_equal)
                    dve.wait_ge(s_mid, c + 1)
                    dve.tensor_tensor(parts[:, m, 2, :], rest[:, m, :], parts[:, m, 1, :], ALU.subtract).then_inc(s_lo, 1)

        @block.tensor
        def _(pe):
            for n, (p, q) in enumerate(halves(g)):
                pe.matmul(bank[n][:, 0:q - p], g.zerob[:, 0:P], g.zerob[:, 0:q - p], start=True, stop=True, skip_group_check=True)
            pe.sem_inc(s_sum, 3)
            with pe.Fori(0, CH // RING) as i:
                for k in range(RING):
                    c, m = i * RING + k, k % 3
                    pe.wait_ge(s_lo, c + 1)
                    pe.sem_inc(free, 1)
                    for part in range(3):
                        for n, (p, q) in enumerate(halves(g)):
                            mm = pe.matmul(bank[n][:, 0:q - p], parts[:, m, part, :], hot[:, m, p:q],
                                           start=False, stop=True, skip_group_check=True)
                    mm.then_inc(s_sum, 1)

    s_xn, s_out, s_dve, s_sq, s_std, s_norm, s_turn = (g.sem(f"b0_{n}") for n in
                                                       ("xn", "out", "dve", "var", "std", "normed", "turned"))
    s_sc2 = g.sem("b0_xn_scaled")
    lot = Lot(g.scratch[:].bitcast(BF16))
    xnT, oT, sq = lot.take([P, NP]), lot.take([P, NP]), l1T
    k = lot.take([P, 8])
    with nc.Block(name="b0_finish") as block:
        @block.scalar
        def _(act):
            for n, (p, q) in enumerate(halves(g)):
                act.activation(xnT[:, p:q], bank[n][:, 0:q - p], ACT.Copy, scale=0.01).then_inc(s_sc2, 1)
            act.wait_ge(s_sq, 1)
            act.activation(k[:, 4:5], k[:, 3:4], ACT.Sqrt).then_inc(s_std, 1)

        @block.tensor
        def _(pe):
            for n, (p, q) in enumerate(halves(g)):
                pe.matmul(bank[3 + n][:, 0:q - p], g.w0[:, 2, :], h2T[:, p:q], start=True, stop=False)
                pe.wait_ge(s_xn, n + 1)
                pe.matmul(bank[3 + n][:, 0:q - p], g.w0[:, 3, :], xnT[:, p:q], start=False, stop=True).then_inc(s_out, 1)
            pe.wait_ge(s_norm, 1)
            for t in range(T):
                w = P if t < T - 1 else g.LAST
                tr = pe.transpose(bank[t // 4][0:w, (t % 4) * D:(t % 4) * D + D], oT[:, t * P:t * P + w], g.ident[:])
                if t % 4 == 3 or t == T - 1:
                    tr.then_inc(s_turn, 1)

        @block.vector
        def _(dve):
            c = Chain(dve, s_dve)
            for n, (p, q) in enumerate(halves(g)):
                dve.wait_ge(s_sc2, n + 1)
                dve.tensor_tensor(xnT[:, p:q], bank[n][:, 0:q - p], xnT[:, p:q], ALU.max).then_inc(s_xn, 1)
            c.step(dve.tensor_scalar(k[:, 5:6], g.cols[:, 4:5], -1.0, None, ALU.add))
            dve.reciprocal(k[:, 6:7], g.cols[:, 4:5])
            c.step(dve.reciprocal(k[:, 7:8], k[:, 5:6]))
            for n, (p, q) in enumerate(halves(g)):
                dve.wait_ge(s_out, n + 1)
                last = dve.tensor_copy(oT[:, p:q], bank[3 + n][:, 0:q - p])
            c.step(last)
            c.step(dve.tensor_reduce(k[:, 0:1], oT[:, 0:N], AX_X, ALU.add))
            c.step(dve.tensor_tensor(k[:, 1:2], k[:, 0:1], k[:, 6:7], ALU.mult))
            c.step(dve.tensor_scalar(oT[:, 0:N], oT[:, 0:N], k[:, 1:2], None, ALU.subtract))
            c.step(dve.tensor_tensor(sq[:, 0:N], oT[:, 0:N], oT[:, 0:N], ALU.mult))
            c.step(dve.tensor_reduce(k[:, 2:3], sq[:, 0:N], AX_X, ALU.add))
            dve.tensor_tensor(k[:, 3:4], k[:, 2:3], k[:, 7:8], ALU.mult).then_inc(s_sq, 1)
            dve.wait_ge(s_std, 1)
            c.step(dve.tensor_scalar(k[:, 4:5], k[:, 4:5], 1.0e-6, None, ALU.add))
            c.step(dve.reciprocal(k[:, 3:4], k[:, 4:5]))
            c.step(dve.tensor_tensor(k[:, 3:4], k[:, 3:4], g.cols[:, 0:1], ALU.mult))
            dve.tensor_scalar(oT[:, 0:N], oT[:, 0:N], k[:, 3:4], g.cols[:, 1:2], ALU.mult, ALU.add).then_inc(s_norm, 1)
            add_nodes(g, dve, bank, s_turn)


def add_nodes(g, dve, bank, turned):
    for t in range(0, g.T, 4):
        dve.wait_ge(turned, t // 4 + 1)
        full = min(4, g.T - 1 - t)
        if full > 0:
            xs = g.x[:, t:t + full, :]
            dve.tensor_tensor(xs, xs, bank[t // 4][:, 0:full * g.D].rearrange("p (t d) -> p t d", d=g.D), ALU.add)
        if t + 4 >= g.T:
            xs = g.x[0:g.LAST, g.T - 1, :]
            at = (g.T - 1 - t) * g.D
            dve.tensor_tensor(xs, xs, bank[t // 4][0:g.LAST, at:at + g.D], ALU.add)


def walk_rounds(pe, g, rounds, walk):
    assert g.T <= 15 and 4 * RING <= 24
    with pe.Fori(0, rounds) as i:
        _, numbers = g.nc.values_load_multi_w_load_instructions(
            g.round_tiles[0:1, bass.ds(i, 1), :].rearrange("p r k -> p (r k)"), engines=[mybir.EngineType.PE],
            min_val=ALL_ONE, max_val=g.T * ALL_ONE)
        walk(i, numbers[0], numbers[1])


def tile_of(packed, k):
    return (packed >> (4 * k)) & 15 if k else packed & 15


def attention(g, name, H, F, weights_, bias, table, logit_terms, extra, layer=0, layers=1):
    nc, T, D, NCH, CH, G, GC = g.nc, g.T, g.D, g.NCH, g.CH, g.G, g.GC
    HF, S = H * F, 2 * H
    NB = g.NP // HALF
    CB = 12 // H
    WIDTH = CB * H * 2 * NB
    GROUPS = NCH // CB
    assert GROUPS % 2 == 0
    HG = H * G
    EX = g.AT if extra == "attributes" else H
    half = RING // 2
    bank = [g.ps[:, 512 * k:512 * k + 512] for k in range(8)]
    names = ("folded", "scores", "rows", "rows_copied", "stored", "dve", "split", "looked", "masked", "logits", "edge_rows",
             "scan0", "row0", "carry0", "carry0_turned", "scan1", "row1", "carry1", "carry1_turned", "maxima", "max_turned",
             "shifted", "weights", "staged", "free", "round", "early", "act_msg", "dve_msg", "summed", "reduced")
    q = {n: g.sem(f"{name}_{n}") for n in names}
    EARLY, ROUND = g.EARLY, RING + 1
    got, before, before_early = g.got, g.gathered + 16 * EARLY * layer, g.gathered_early + 16 * EARLY * layer
    g.gathered += 16 * EARLY * layers
    g.gathered_early += 16 * EARLY * layers
    lot = Lot(g.scratch[:].bitcast(BF16))
    scores = lot.take([P, 3, H, 2, NB], BF16)
    folded = lot.take([P, S])
    left = lot.take([P, 3, NB, S])
    msg = lot.take([P, 4, HF + EX])
    hot = lot.take([P, 4, P])
    masked = lot.take([P, 2, WIDTH])
    ends = lot.take([P, 2, G, H])
    rowbuf = lot.take([4, 4, NCH])
    F0, M0 = g.scan_a[0:GC, 0:HG * P], g.scan_b[0:GC, 0:HG * P]
    lg = g.logits
    rows = bank[0:4]

    with nc.Block(name=name) as block:
        @block.tensor
        def _(pe):
            pe.wait_ge(q["folded"], 1)
            for b in range(NB):
                for on in (0, HALF):
                    mm = pe.matmul(bank[6][on:on + HALF, b * S:(b + 1) * S], g.hT[:, b * HALF:(b + 1) * HALF],
                                   folded, start=True, stop=True)
            mm.then_inc(q["scores"], 1)
            for t in range(T):
                if t >= 4:
                    pe.wait_ge(q["rows_copied"], t - 3)
                pe.matmul(rows[t % 4][:, 0:HF], g.hT[:, t * P:(t + 1) * P], weights_[:, 0:HF], start=True, stop=True).then_inc(q["rows"], 1)
            pe.sem_inc(q["masked"], 2)
            pe.sem_inc(q["reduced"], 2)
            pe.wait_ge(q["split"], 1)
            with pe.Fori(0, GROUPS // 2) as i:
                for u in range(2):
                    pe.wait_ge(q["masked"], 2 * i + u + 1)
                    for k in range(CB):
                        c = (2 * i + u) * CB + k
                        for part in range(3):
                            mm = pe.matmul(bank[4 + u][:, k * H * 2 * NB:(k + 1) * H * 2 * NB], g.onehotT[:, bass.ds(c * P, P)],
                                           scores[:, part].rearrange("p h s b -> p (h s b)"), start=part == 0, stop=part == 2)
                    mm.then_inc(q["looked"], 1)
            pe.wait_ge(q["logits"], 1)
            for b in range(HG):
                tr = pe.transpose(bank[b // 4][0:GC, (b % 4) * P:(b % 4) * P + P], lg[:, (b % G) * GC:(b % G + 1) * GC, b // G], g.ident[:])
            tr.then_inc(q["edge_rows"], 1)
            for way, (scan, row_, carry, back) in enumerate(((q["scan0"], q["row0"], q["carry0"], q["carry0_turned"]),
                                                             (q["scan1"], q["row1"], q["carry1"], q["carry1_turned"]))):
                pe.wait_ge(scan, 1)
                for n in range(G):
                    tr = pe.transpose(bank[2 + way][0:H, n * GC:(n + 1) * GC], ends[0:GC, way, n, :], g.ident[0:GC, 0:GC])
                tr.then_inc(row_, 1)
                pe.wait_ge(carry, 1)
                for n in range(G):
                    tr = pe.transpose(bank[6 + way][0:GC, n * H:(n + 1) * H], rowbuf[0:H, 2 * way + 1, n * GC:(n + 1) * GC],
                                      g.ident[0:H, 0:H])
                tr.then_inc(back, 1)
            pe.wait_ge(q["maxima"], 1)
            for b in range(HG):
                tr = pe.transpose(bank[4 + b // 4][:, (b % 4) * GC:(b % 4 + 1) * GC], M0[:, b * P:(b + 1) * P], g.ident[0:GC, 0:GC])
            tr.then_inc(q["max_turned"], 1)
            pe.wait_ge(q["shifted"], 1)
            for b in range(6):
                pe.matmul(bank[b], g.zerob[:, 0:P], g.zerob[:], start=True, stop=True, skip_group_check=True)
            pe.sem_inc(q["summed"], 3)
            def sum_round(i, packed, early_tile):
                packed, early_tile = packed - ALL_ONE, early_tile - ALL_ONE
                for k in range(ROUND):
                    n, m = i * ROUND + k, 3 if k == RING else k % 3
                    t = tile_of(packed, k) if k < RING else early_tile & 15
                    pe.wait_ge(q["act_msg"], n + 1)
                    pe.wait_ge(q["dve_msg"], n + 1)
                    if k < RING:
                        pe.sem_inc(q["free"], 1)
                    pe.matmul(g.ps[:, bass.ds(t * HF, HF)], hot[:, m, :], msg[:, m, 0:HF], start=False, stop=True,
                              skip_group_check=True)
                    pe.matmul(g.ps[:, bass.ds(t * EX + g.ATT0, EX)], hot[:, m, :], msg[:, m, HF:HF + EX], start=False, stop=True,
                              skip_group_check=True).then_inc(q["summed"], 1)
            walk_rounds(pe, g, EARLY, sum_round)

        @block.vector
        def _(dve):
            c = Chain(dve, q["dve"])
            dve.tensor_copy(folded, weights_[:, HF:HF + S]).then_inc(q["folded"], 1)
            c.step(dve.memset(scores, 0.0))
            dve.wait_ge(q["scores"], 1)
            found = bank[6][:, 0:NB * S].rearrange("p (b s) -> p b s", b=NB)
            if bias is not None:
                last = dve.tensor_tensor(left[:, 0], found, bias[:, HF:HF + S].unsqueeze(1).broadcast_to([P, NB, S]), ALU.add)
            else:
                last = dve.tensor_copy(left[:, 0], found)
            c.step(last)
            ends_of = ((slice(0, HALF), 0, slice(0, H)), (slice(HALF, P), 1, slice(H, S)))
            for n in range(3):
                for on, side, cols in ends_of:
                    last = dve.tensor_copy(scores[on, n, :, side, :].rearrange("p h b -> p b h"), left[on, n, :, cols])
                if n < 2:
                    c.step(last)
                    for on, side, cols in ends_of:
                        last = dve.tensor_tensor(left[on, n + 1, :, cols], left[on, n, :, cols],
                                                 scores[on, n, :, side, :].rearrange("p h b -> p b h"), ALU.subtract)
                    c.step(last)
            last.then_inc(q["split"], 1)
            for t in range(T):
                dve.wait_ge(q["rows"], t + 1)
                if bias is not None:
                    dve.tensor_tensor(g.wide[:, t, 0:HF], rows[t % 4][:, 0:HF], bias[:, 0:HF], ALU.add).then_inc(q["rows_copied"], 1)
                else:
                    dve.tensor_copy(g.wide[:, t, 0:HF], rows[t % 4][:, 0:HF]).then_inc(q["rows_copied"], 1)
            with dve.Fori(0, GROUPS // 2) as i:
                for u in range(2):
                    chunks = bass.ds((2 * i + u) * CB, CB)
                    dve.wait_ge(q["looked"], 2 * i + u + 1)
                    dve.wait_ge(q["reduced"], 2 * i + u + 1)
                    dve.tensor_tensor(masked[:, u, :].rearrange("p (c h w) -> p c h w", c=CB, h=H),
                                      bank[4 + u][:, 0:WIDTH].rearrange("p (c h w) -> p c h w", c=CB, h=H),
                                      g.blockmask[:, chunks].rearrange("p c s b -> p c (s b)").unsqueeze(2).broadcast_to([P, CB, H, 2 * NB]),
                                      ALU.mult).then_inc(q["masked"], 1)
                for u in range(2):
                    chunks = bass.ds((2 * i + u) * CB, CB)
                    dve.wait_ge(q["masked"], 2 * i + u + 3)
                    dve.tensor_reduce(lg[:, chunks, 0:H], masked[:, u, :].rearrange("p (c h w) -> p c h w", c=CB, h=H),
                                      AX_X, ALU.add).then_inc(q["reduced"], 1)
            dve.wait_ge(q["reduced"], 2 + GROUPS)
            ls = lg[:, :, 0:H]
            c.step(dve.tensor_tensor(ls, ls, logit_terms, ALU.add))
            c.step(dve.scalar_tensor_tensor(ls, ls, 0.2, ls, ALU.mult, ALU.max))
            dve.tensor_tensor(ls, ls, g.unreal[:].unsqueeze(2).broadcast_to([P, NCH, H]), ALU.add).then_inc(q["logits"], 1)
            dve.wait_ge(q["edge_rows"], 1)
            line = g.ps[0:GC, 0:HG * P]
            blocks = line.rearrange("p (h n e) -> p h n e", h=H, n=G)
            F4, M4 = (v.rearrange("p (h n e) -> p h n e", h=H, n=G) for v in (F0, M0))
            resets = [g.reset[:, d].rearrange("p h n e -> p (h n e)")[:, 0:HG * P] for d in range(2)]
            for way, (scan, row_, carry, back) in enumerate(((q["scan0"], q["row0"], q["carry0"], q["carry0_turned"]),
                                                             (q["scan1"], q["row1"], q["carry1"], q["carry1_turned"]))):
                into, at, first = (F4, P - 1, 0) if way == 0 else (M4, 0, P - 1)

                def sweep():
                    if way == 0:
                        return dve.tensor_tensor_scan(F0, resets[0], line, -BIG, ALU.add, ALU.max)
                    return dve.tensor_tensor_scan(M0[:, ::-1], resets[1][:, ::-1], F0[:, ::-1], -BIG, ALU.add, ALU.max)
                c.step(sweep())
                dve.tensor_copy(ends[0:GC, way].rearrange("p n h -> p h n"), into[:, :, :, at]).then_inc(scan, 1)
                dve.wait_ge(row_, 1)
                run, out = rowbuf[0:H, 2 * way], rowbuf[0:H, 2 * way + 1]
                ins = bank[2 + way][0:H, 0:NCH]
                on = g.carry_on[0:H, way, :]
                if way == 0:
                    c.step(dve.tensor_tensor_scan(run, on, ins, -BIG, ALU.add, ALU.max))
                    dve.tensor_tensor(out[:, 1:NCH], run[:, 0:NCH - 1], g.carry_in[0:H, 0, 1:NCH], ALU.add)
                else:
                    c.step(dve.tensor_tensor_scan(run[:, ::-1], on[:, ::-1], ins[:, ::-1], -BIG, ALU.add, ALU.max))
                    dve.tensor_tensor(out[:, 0:NCH - 1], run[:, 1:NCH], g.carry_in[0:H, 1, 0:NCH - 1], ALU.add)
                dve.memset(out[:, 0:1] if way == 0 else out[:, NCH - 1:NCH], -BIG).then_inc(carry, 1)
                dve.wait_ge(back, 1)
                held = (blocks if way == 0 else F4)[:, :, :, first]
                c.step(dve.tensor_copy(ends[0:GC, way], bank[6 + way][0:GC, 0:G * H].rearrange("p (n h) -> p n h", n=G)))
                c.step(dve.tensor_tensor(held, held, ends[0:GC, way].rearrange("p n h -> p h n"), ALU.max))
                last = sweep()
                if way == 0:
                    c.step(last)
            last.then_inc(q["maxima"], 1)
            dve.wait_ge(q["max_turned"], 1)
            for b in range(HG // 4):
                hs = lg[:, :, 2 * b:2 * b + 2].rearrange("p c h -> p h c")
                last = dve.tensor_tensor(hs, hs, bank[4 + b][:, 0:2 * NCH].rearrange("p (h c) -> p h c", h=2), ALU.subtract)
            last.then_inc(q["shifted"], 1)
            dve.wait_ge(q["weights"], 1)
            dve.wait_ge(g.got_early, before_early + 16 * EARLY)
            dve.sem_inc(q["early"], 1)
            with dve.Fori(0, EARLY) as i:
                for k in range(ROUND):
                    n, m = i * ROUND + k, 3 if k == RING else k % 3
                    ch = i * RING + k if k < RING else i + g.EARLY0
                    rows_in = g.ring[:, k, 0:HF] if k < RING else g.early[:, bass.ds(i * HF, HF)]
                    one = bass.ds(ch, 1)
                    dve.wait_ge(q["summed"], n + 1)
                    dve.tensor_scalar(hot[:, m, :], g.lane[:], g.rec[:, one, R_DLO], None, ALU.is_equal)
                    wt = lg[:, one, 0:H].rearrange("p o h -> p (o h)")
                    if extra == "attributes":
                        dve.tensor_tensor(msg[:, m, HF:HF + EX].rearrange("p (h k) -> p h k", h=H),
                                          g.rec[:, one, R_ATTR:R_ATTR + NA].broadcast_to([P, H, NA]),
                                          wt.unsqueeze(2).broadcast_to([P, H, NA]), ALU.mult)
                        if k < RING:
                            dve.wait_ge(got[k], before + 16 * (i + 1))
                        dve.tensor_scalar(msg[:, m, F:HF], rows_in[:, F:HF], lg[:, one, 1], None, ALU.mult).then_inc(q["dve_msg"], 1)
                    else:
                        if k < RING:
                            dve.wait_ge(got[k], before + 16 * (i + 1))
                        dve.tensor_tensor(msg[:, m, 0:HF].rearrange("p (h f) -> p h f", h=H),
                                          rows_in.rearrange("p (h f) -> p h f", h=H),
                                          wt.unsqueeze(2).broadcast_to([P, H, F]), ALU.mult).then_inc(q["dve_msg"], 1)

        @block.scalar
        def _(act):
            for u in range(2):
                act.copy(g.slot_idx[:, u * half:(u + 1) * half], g.idx[:, 0, u * half:(u + 1) * half]).then_inc(q["staged"], 1)
            act.wait_ge(q["shifted"], 1)
            act.activation(lg[:, :, 0:H], lg[:, :, 0:H], ACT.Exp).then_inc(q["weights"], 1)
            act.wait_ge(q["weights"], 1)
            act.wait_ge(g.got_early, before_early + 16 * EARLY)
            act.sem_inc(q["early"], 1)

            def message(i, k, rows_in):
                n, m = i * ROUND + k, 3 if k == RING else k % 3
                ch = i * RING + k if k < RING else i + g.EARLY0
                act.wait_ge(q["summed"], n + 1)
                if k < RING:
                    act.wait_ge(got[k], before + 16 * (i + 1))
                if extra == "attributes":
                    act.activation(msg[:, m, 0:F], rows_in[:, 0:F], ACT.Copy, scale=lg[:, bass.ds(ch, 1), 0]).then_inc(q["act_msg"], 1)
                else:
                    act.copy(msg[:, m, HF:HF + H], lg[:, bass.ds(ch, 1), 0:H].rearrange("p o h -> p (o h)")).then_inc(q["act_msg"], 1)

            with act.Fori(0, EARLY) as i:
                for u in range(2):
                    for k in range(half * u, half * u + half):
                        message(i, k, g.ring[:, k, 0:HF])
                    act.copy(g.slot_idx[:, half * u:half * u + half],
                             g.idx[:, 0, bass.ds((2 * i + u + 2) * half, half)]).then_inc(q["staged"], 1)
                message(i, RING, g.early[:, bass.ds(i * HF, HF)])

        @block.sync
        def _(sp):
            for n in range(2):
                ts = slice(n * T // 2, (n + 1) * T // 2)
                sp.wait_ge(q["rows_copied"], (n + 1) * T // 2)
                sp.dma_start(table.rearrange("(t p) d -> p t d", p=P)[:, ts, :], g.wide[:, ts, 0:HF]).then_inc(q["stored"], 16)

        @block.gpsimd
        def _(pool):
            pool.wait_ge(q["stored"], 32)
            pool.sem_inc(q["free"], RING)
            pool.sem_inc(q["round"], 1)
            for k in range(EARLY):
                pool.indirect_dma_start(g.early[:, k * HF:(k + 1) * HF], None, table,
                                        bass.IndirectOffsetOnAxis(ap=g.idx[:, 0, g.EARLY0 + k:g.EARLY0 + k + 1], axis=0)
                                        ).then_inc(g.got_early, 16)
            pool_gathers(pool, g, table, HF, q["staged"], q["free"], q["round"], got, EARLY)


def block1(g):
    nc, T, D, H, F = g.nc, g.T, g.D, g.H1, g.F1
    attention(g, "b1", H, F, g.w1x[:], g.bias1, g.table1, g.ab1[:].unsqueeze(1).broadcast_to([P, g.NCH, H]), "weights")
    s_dve = g.sem("b1_finish")
    with nc.Block(name="b1_finish") as block:
        @block.vector
        def _(dve):
            c = Chain(dve, s_dve)
            den = g.small[:, :, 0:H]
            c.step(dve.tensor_scalar(den, g.ps[:, g.ATT0:g.ATT0 + T * H].rearrange("p (t h) -> p t h", t=T), 1.0e-30, None, ALU.max))
            c.step(dve.reciprocal(den, den))
            c.step(dve.tensor_tensor(g.h[:].rearrange("p t (h f) -> p t h f", h=H),
                                     g.ps[:, 0:T * D].rearrange("p (t h f) -> p t h f", t=T, h=H),
                                     den.unsqueeze(3).broadcast_to([P, T, H, F]), ALU.mult))
            dve.tensor_tensor(g.x[:], g.x[:], g.h[:], ALU.add)


def block2(g):
    nc, T, D, L, H, F, AT = g.nc, g.T, g.D, g.L, g.H2, g.F2, g.AT
    HF = H * F
    bank = [g.ps[:, 512 * k:512 * k + 512] for k in range(8)]
    with nc.Fori(0, L) as l:
        attention(g, "b2", H, F, g.w2x[:, bass.ds(l, 1), :].rearrange("p o w -> p (o w)"), None, g.table,
                         g.attr_part[:, :, bass.ds(l * H, H)], "attributes", l, L)
        names = ("dve", "attr", "attr_turned", "attr_copied", "attr_sum", "read", "h", "turned")
        q = {n: g.sem(f"b2_finish_{n}") for n in names}
        lot = Lot(g.scratch[:].bitcast(BF16))
        den = lot.take([P, T, H])
        att = lot.take([P, T, AT])
        attT = lot.take([AT, g.NP])
        with nc.Block(name="b2_finish") as block:
            @block.vector
            def _(dve):
                c = Chain(dve, q["dve"])
                sums = g.ps[:, g.ATT0:g.ATT0 + T * AT].rearrange("p (t h k) -> p t h k", t=T, h=H)
                c.step(dve.tensor_scalar(den, sums[:, :, :, NA - 1], 1.0e-16, None, ALU.add))
                c.step(dve.reciprocal(den, den))
                c.step(dve.tensor_scalar(den, den, 1.0 / H, None, ALU.mult))
                dve.tensor_tensor(att.rearrange("p t (h k) -> p t h k", h=H), sums,
                                  den.unsqueeze(3).broadcast_to([P, T, H, NA]), ALU.mult).then_inc(q["attr"], 1)
                c.step(dve.tensor_tensor(g.wide[:].rearrange("p t (h f) -> p t h f", h=H),
                                         g.ps[:, 0:T * HF].rearrange("p (t h f) -> p t h f", t=T, h=H),
                                         den.unsqueeze(3).broadcast_to([P, T, H, F]), ALU.mult))
                dve.sem_inc(q["read"], 1)
                c.step(dve.tensor_tensor(g.h[:], g.wide[:, :, 0:F], g.wide[:, :, F:HF], ALU.add))
                c.step(dve.tensor_tensor(g.h[:], g.h[:], g.bias2[:, bass.ds(l, 1), :].broadcast_to([P, T, D]), ALU.add))
                dve.wait_ge(q["attr_sum"], 1)
                c.step(dve.tensor_tensor(g.h[:], g.h[:], g.ps[:, 0:T * D].rearrange("p (t d) -> p t d", d=D), ALU.add))
                dve.tensor_scalar(g.h[:], g.h[:], g.floor2[:, bass.ds(l, 1)], None, ALU.max).then_inc(q["h"], 1)

            @block.tensor
            def _(pe):
                pe.wait_ge(q["attr"], 1)
                for t in range(T):
                    if t == 8:
                        pe.wait_ge(q["attr_copied"], 1)
                    b = 6 + t // 4 if t < 8 else 6
                    tr = pe.transpose(bank[b][0:AT, (t % 4) * P:(t % 4) * P + P], att[:, t, :], g.ident[:])
                    if t % 4 == 3 or t == T - 1:
                        tr.then_inc(q["attr_turned"], 1)
                pe.wait_ge(q["attr_copied"], 3)
                pe.wait_ge(q["read"], 1)
                for t in range(T):
                    mm = pe.matmul(g.ps[:, t * D:(t + 1) * D], attT[:, t * P:(t + 1) * P],
                                   g.ew[:, bass.ds(l, 1), :].rearrange("p o d -> p (o d)"), start=True, stop=True)
                mm.then_inc(q["attr_sum"], 1)
                pe.wait_ge(q["h"], 1)
                turn_nodes(g, pe, q["turned"], banks=4)

            @block.scalar
            def _(act):
                for n in range(3):
                    act.wait_ge(q["attr_turned"], n + 1)
                    w = min(4, T - 4 * n) * P
                    act.copy(attT[:, n * 512:n * 512 + w], bank[6 + n % 2][0:AT, 0:w]).then_inc(q["attr_copied"], 1)
                turn_copies(g, act, q["turned"], banks=4)
        g.stage.clear()
    with nc.Block(name="b2_add") as block:
        @block.vector
        def _(dve):
            dve.tensor_tensor(g.x[:], g.x[:], g.h[:], ALU.add)


def block3(g):
    nc, a, T, D, NP, CH, HID, DT = g.nc, g.a, g.T, g.D, g.NP, g.CH, g.HID, g.DT
    bank = [g.ps[:, 512 * k:512 * k + 512] for k in range(8)]
    flat = g.arena[:].rearrange("p s e -> p (s e)")
    C = flat[:, 0:2 * T * NP].bitcast(F32).rearrange("p (t n) -> p t n", t=T)
    lot = Lot(flat[:, 2 * T * NP:])
    w_in, w1, w2 = lot.take([P, D]), lot.take([P, HID]), lot.take([P, 2, D])
    b_in, b2 = lot.take([P, D]), lot.take([P, D])
    keep = lot.take([P, 1])
    deg, rdeg = lot.take([P, T]), lot.take([P, T])
    aggT = lot.take([P, NP])
    tmp = lot.take([P, T, D])
    hot_d = lot.take([P, RING, P], BF16)
    lots = [Lot(g.scratch[:].bitcast(BF16)), Lot(g.wide[:].rearrange("p t f -> p (t f)").bitcast(BF16))]
    hot_s = [lots[k % 2].take([P, NP], BF16) for k in range(RING)]
    zT = g.wide[:].rearrange("p t f -> p (t f)").rearrange("p (k n) -> p k n", k=2)

    REGION = 4 * 512
    assert REGION == 1 << 11
    names = ("loaded", "hots", "summed", "taken", "dve", "degrees", "apart", "divided", "turned", "rows_back", "cols_back")
    q = {n: g.sem(f"b3_{n}") for n in names}
    assert T % 2 == 0
    with nc.Block(name="b3_counts") as block:
        @block.sync
        def _(sp):
            for dst, src in ((w_in, a["L3_gnn_W_in"]), (w1, a["L3_gnn_W1"]), (w2, a["L3_gnn_W2"].rearrange("(k p) o -> p k o", p=P)),
                             (b_in, a["L3_gnn_b_in"].partition_broadcast(P)), (b2, a["L3_gnn_b2"].partition_broadcast(P))):
                sp.dma_start(dst, src).then_inc(q["loaded"], 16)
            sp.wait_ge(q["loaded"], 16 * 5)

        @block.vector
        def _(dve):
            c = Chain(dve, q["dve"])
            c.step(dve.tensor_scalar(keep, g.cols[:, 5:6], 0.0, None, ALU.max))
            c.step(dve.tensor_scalar(keep, keep, -DT, 1.0, ALU.mult, ALU.add))
            with dve.Fori(0, CH // RING) as i:
                for k in range(RING):
                    ch = i * RING + k
                    one = bass.ds(ch, 1)
                    dve.wait_ge(q["summed"], ch + 1)
                    dve.tensor_scalar(hot_d[:, k, :], g.lane16[:], g.rec[:, one, R_DLO], g.rec[:, one, R_ORIG],
                                      ALU.is_equal, ALU.mult)
                    dve.tensor_scalar(hot_s[k], g.nodeid[:], g.rec[:, one, R_SRC], None, ALU.is_equal).then_inc(q["hots"], 1)
            dve.wait_ge(q["taken"], 2 + T)
            c.step(dve.tensor_copy(rdeg, deg))
            c.step(dve.tensor_tensor(rdeg[:, 2:T], deg[:, 2:T], deg[:, 0:T - 2], ALU.subtract))
            c.step(dve.tensor_scalar(rdeg, rdeg, 1.0, None, ALU.max))
            dve.reciprocal(rdeg, rdeg).then_inc(q["degrees"], 1)
            for t in range(T - 2, 0, -2):
                dve.tensor_tensor(C[:, t:t + 2, :], C[:, t:t + 2, :], C[:, t - 2:t, :], ALU.subtract).then_inc(q["apart"], 1)
                dve.wait_ge(q["apart"], (T - t) // 2)
            for t in range(T - 1):
                dve.wait_ge(q["turned"], 2 * t + 2)
                dve.tensor_copy(C[:, t, (t + 1) * P:NP], g.ps[:, REGION:REGION + (T - 1 - t) * P]).then_inc(q["cols_back"], 1)

        @block.tensor
        def _(pe):
            pe.sem_inc(q["summed"], RING)
            pe.sem_inc(q["taken"], 2)
            for b in range(8):
                pe.matmul(bank[b], g.zerob[:, 0:P], g.zerob[:], start=True, stop=True, skip_group_check=True)

            def count_round(i, packed, _):
                for k in range(RING):
                    pe.wait_ge(q["taken"], tile_of(packed, k))
                    pe.wait_ge(q["hots"], i * RING + k + 1)
                    up = 11 - 4 * k
                    region = (packed & (1 << 4 * k)) << up if up > 0 else (packed >> -up) & REGION
                    for p, e in halves(g):
                        mm = pe.matmul(g.ps[:, bass.ds(region + p, e - p)], hot_d[:, k, :], hot_s[k][:, p:e],
                                       start=False, stop=True, skip_group_check=True)
                    mm.then_inc(q["summed"], 1)
            walk_rounds(pe, g, CH // RING, count_round)
            pe.wait_ge(q["divided"], T)
            for t in range(T):
                if t:
                    pe.wait_ge(q["rows_back"], t)
                for s_ in range(t, T):
                    tr = pe.transpose(g.ps[:, (s_ - t) * P:(s_ - t + 1) * P], C[:, t, s_ * P:(s_ + 1) * P], g.ident[:])
                tr.then_inc(q["turned"], 1)
                if t < T - 1:
                    if t:
                        pe.wait_ge(q["cols_back"], t)
                    for s_ in range(t + 1, T):
                        tr = pe.transpose(g.ps[:, REGION + (s_ - t - 1) * P:REGION + (s_ - t) * P], C[:, s_, t * P:(t + 1) * P], g.ident[:])
                    tr.then_inc(q["turned"], 1)

        @block.scalar
        def _(act):
            with act.Fori(0, T // 2) as i:
                _, last_ = nc.values_load_multi_w_load_instructions(g.tile_end[0:1, bass.ds(2 * i, 2)], min_val=1, max_val=CH,
                                                                    engines=[mybir.EngineType.Activation])
                for u in range(2):
                    act.wait_ge(q["summed"], last_[u] + RING)
                    act.activation(C[:, bass.ds(2 * i + u, 1), :].rearrange("p o n -> p (o n)"), g.ps[:, (1 - u) * REGION:(1 - u) * REGION + NP],
                                   ACT.Copy, accum_out=deg[:, bass.ds(2 * i + u, 1)]).then_inc(q["taken"], 1)
            act.wait_ge(q["degrees"], 1)
            for n, t in enumerate(range(T - 2, -1, -2)):
                act.wait_ge(q["apart"], min(n + 1, T // 2 - 1))
                for t_ in (t, t + 1):
                    act.activation(C[:, t_, :], C[:, t_, :], ACT.Copy, scale=rdeg[:, t_:t_ + 1]).then_inc(q["divided"], 1)
            for t in range(T):
                act.wait_ge(q["turned"], min(2 * t + 2, 2 * T - 1))
                act.copy(C[:, t:T, t * P:(t + 1) * P], g.ps[:, 0:(T - t) * P].rearrange("p (s n) -> p s n", n=P)).then_inc(q["rows_back"], 1)
    g.stage.end()

    names = ("agg", "aggT", "z", "gelu", "out", "pre", "tanh", "h", "start", "start_sum", "dve", "kept", "done")
    q = {n: g.sem(f"b3_{n}") for n in names}
    parts = halves(g)
    with nc.Block(name="b3_steps") as block:
        @block.tensor
        def _(pe):
            for n, (p, e) in enumerate(parts):
                for t in range(p // P, e // P):
                    mm = pe.matmul(bank[5 + n][:, t * P - p:t * P - p + P], g.hT[:, t * P:(t + 1) * P], w_in, start=True, stop=True)
                mm.then_inc(q["start"], 1)

            def gather(i, n):
                p, e = parts[n]
                for s_ in range(T):
                    if n == 0 and s_ % 4 == 0:
                        pe.wait_ge(q["h"], 3 * i + s_ // 4 + 1)
                    mm = pe.matmul(bank[n][:, 0:e - p], g.h[:, s_, :], C[:, s_, p:e], start=s_ == 0, stop=s_ == T - 1)
                mm.then_inc(q["agg"], 1)

            def hidden(i, n):
                p, e = parts[n]
                pe.wait_ge(q["aggT"], 3 * i + n + 1)
                pe.wait_ge(q["gelu"], 3 * i + n + 1)
                for k in range(2):
                    mm = pe.matmul(bank[3 + k][:, 0:e - p], w1[:, k * P:(k + 1) * P], aggT[:, p:e], start=True, stop=True)
                mm.then_inc(q["z"], 1)

            def output(i, n):
                p, e = parts[n]
                pe.wait_ge(q["gelu"], 3 * i + n + 2)
                for t in range(p // P, e // P):
                    for k in range(2):
                        mm = pe.matmul(bank[5 + n][:, t * P - p:t * P - p + P], zT[:, k, t * P:(t + 1) * P], w2[:, k, :],
                                       start=k == 0, stop=k == 1)
                mm.then_inc(q["out"], 1)

            pe.sem_inc(q["gelu"], 1)
            with pe.Fori(0, g.STEPS) as i:
                gather(i, 0)
                gather(i, 1)
                hidden(i, 0)
                gather(i, 2)
                hidden(i, 1)
                output(i, 0)
                hidden(i, 2)
                output(i, 1)
                output(i, 2)

        @block.scalar
        def _(act):
            for n, (p, e) in enumerate(parts):
                act.wait_ge(q["start_sum"], n + 1)
                act.activation(g.h[:, p // P:e // P, :], tmp[:, p // P:e // P, :], ACT.Tanh).then_inc(q["h"], 1)

            def copy(i, n):
                p, e = parts[n]
                act.wait_ge(q["agg"], 3 * i + n + 1)
                act.copy(aggT[:, p:e], bank[n][:, 0:e - p]).then_inc(q["aggT"], 1)

            def gelu(i, n):
                p, e = parts[n]
                act.wait_ge(q["z"], 3 * i + n + 1)
                for k in range(2):
                    last = act.activation(zT[:, k, p:e], bank[3 + k][:, 0:e - p], ACT.Gelu, bias=g.cols[:, 2 + k:3 + k])
                last.then_inc(q["gelu"], 1)

            def tanh(i, n):
                p, e = parts[n]
                act.wait_ge(q["pre"], 3 * i + n + 1)
                act.activation(tmp[:, p // P:e // P, :], tmp[:, p // P:e // P, :], ACT.Tanh).then_inc(q["tanh"], 1)

            with act.Fori(0, g.STEPS) as i:
                copy(i, 0)
                copy(i, 1)
                gelu(i, 0)
                copy(i, 2)
                gelu(i, 1)
                gelu(i, 2)
                tanh(i, 0)
                tanh(i, 1)
                tanh(i, 2)

        @block.vector
        def _(dve):
            def summed(n, bias):
                p, e = parts[n]
                ts = slice(p // P, e // P)
                return dve.tensor_tensor(tmp[:, ts, :], bank[5 + n][:, 0:e - p].rearrange("p (t d) -> p t d", d=D),
                                         bias.unsqueeze(1).broadcast_to([P, (e - p) // P, D]), ALU.add)
            for n in range(3):
                dve.wait_ge(q["start"], n + 1)
                summed(n, b_in).then_inc(q["start_sum"], 1)
            dve.wait_ge(q["h"], 3)
            with dve.Fori(0, g.STEPS) as i:
                for n, (p, e) in enumerate(parts):
                    ts = slice(p // P, e // P)
                    dve.wait_ge(q["out"], 3 * i + n + 1)
                    summed(n, b2).then_inc(q["pre"], 1)
                    dve.tensor_scalar(g.h[:, ts, :], g.h[:, ts, :], keep, None, ALU.mult).then_inc(q["kept"], 1)
                for n, (p, e) in enumerate(parts):
                    ts = slice(p // P, e // P)
                    dve.wait_ge(q["tanh"], 3 * i + n + 1)
                    dve.wait_ge(q["kept"], 3 * i + n + 1)
                    dve.scalar_tensor_tensor(g.h[:, ts, :], tmp[:, ts, :], DT, g.h[:, ts, :], ALU.mult, ALU.add).then_inc(q["h"], 1)
            dve.wait_ge(q["h"], 3 + 3 * g.STEPS)
            dve.tensor_tensor(g.x[:], g.x[:], g.h[:], ALU.add).then_inc(q["dve"], 1)

        @block.sync
        def _(sp):
            sp.wait_ge(q["dve"], 1)
            sp.dma_start(g.out[0:(T - 1) * P, :].rearrange("(t p) d -> p t d", p=P), g.x[:, 0:T - 1, :]).then_inc(q["done"], 16)
            sp.dma_start(g.out[(T - 1) * P:, :], g.x[0:g.LAST, T - 1, :]).then_inc(q["done"], 16)
            sp.wait_ge(q["done"], 32)


_INS = ["x", "src", "dst", "edge_attr_16", "edge_weight1", "L0_gnn_batch_num", "L0_gnn_W1", "L0_gnn_W2", "L0_gnn_Wo",
        "L0_gnn_Wn", "L0_gnn_gamma", "L0_gnn_beta", "L1_gnn_W_w", "L1_gnn_W_b", "L1_gnn_a_w", "L1_gnn_a_b",
        "L2_gnn_weights", "L2_gnn_atts", "L2_gnn_biases", "L2_gnn_edge_ws", "L2_gnn_edge_bs", "L3_gnn_W_in",
        "L3_gnn_b_in", "L3_gnn_W1", "L3_gnn_b1", "L3_gnn_W2", "L3_gnn_b2", "L3_gnn_clearance"]


def kernel(**inputs):
    import numpy as _np
    import concourse.bacc as _bacc
    from concourse import mybir as _mybir
    from concourse.bass_utils import run_bass_kernel_spmd as _run

    nc = _bacc.Bacc("TRN2", target_bir_lowering=False, num_devices=1)
    arrays, views = {}, {}
    for name in _INS:
        v = _np.ascontiguousarray(inputs[name])
        arrays[f"in_{name}"] = v
        views[name] = nc.dram_tensor(f"in_{name}", v.shape, _mybir.dt.from_np(v.dtype), kind="ExternalInput").ap()
    out = nc.dram_tensor("out_0", inputs["x"].shape, _mybir.dt.float32, kind="ExternalOutput").ap()
    graph_kernel(nc, views, out)
    r = _run(nc, [arrays], core_ids=[0])
    return r.results[0]["out_0"]
```

```python
from contextlib import ExitStack

import concourse.bass as bass
from concourse import mybir

F32 = mybir.dt.float32
BF16 = mybir.dt.bfloat16
F16 = mybir.dt.float16
I32 = mybir.dt.int32
ALU = mybir.AluOpType
ACT = mybir.ActivationFunctionType
AX_X = mybir.AxisListType.X

P = 128
BIG = 1.0e30
NA = 17
(R_DHI, R_DLO, R_W, R_ORIG, R_SRC, R_ATTR) = range(6)
REC = R_ATTR + NA
R_REAL = R_ATTR + NA - 1
HALF = 64
RING = 6
SLOTS0 = 10
PUT0 = 4
ALL_ONE = (16 ** RING - 1) // 15


class Chain:

    def __init__(self, eng, done, start=0):
        self.eng, self.done, self.start, self.n = eng, done, start, 0

    def step(self, ins):
        self.n += 1
        ins.then_inc(self.done, 1)
        self.eng.wait_ge(self.done, self.start + self.n)


class Lot:

    def __init__(self, area):
        self.area, self.at = area, 0

    def take(self, shape, dt=F32):
        n = 1
        for k in shape[1:]:
            n *= k
        size = mybir.dt.size(dt) * n
        view = self.area[0:shape[0], self.at // 2:(self.at + size) // 2].bitcast(dt)
        self.at += -(-size // 32) * 32
        assert self.at <= 2 * self.area.shape[1]
        names = "abcd"[:len(shape) - 1]
        return view.rearrange(f"p ({' '.join(names)}) -> p {' '.join(names)}", **dict(zip(names, shape[1:])))


class Graph:
    pass


class Stage:

    def __init__(self, nc):
        self.nc, self.first = nc, min(nc.free_semaphores)
        self.used, self.held = 0, ExitStack()

    def sem(self, name):
        self.used += 1
        return self.held.enter_context(self.nc.semaphore(name, num=self.first + self.used - 1))

    def clear(self):
        self.nc.gpsimd.sem_clear(range(self.first, self.first + self.used))
        self.nc.all_engine_barrier()

    def end(self):
        if self.used:
            self.clear()
        self.held.close()
        self.used, self.held = 0, ExitStack()


def graph_kernel(nc, a, out):
    N, D = a["x"].shape
    E = a["src"].shape[0]
    T = -(-N // P)
    LAST = N - (T - 1) * P
    NP = T * P
    EA = E + N
    UP = 125
    UE, UN = E // UP, N // UP
    UC = UE + UN
    assert UP * UE == E and UP * UN == N and UC % 10 == 0
    USED = (EA + T * (P - 1)) // P
    CH = -(-USED // RING) * RING
    EARLY = -(-USED // (RING + 1))
    EARLY0 = EARLY * RING
    G = 2
    GC = 96
    NCH = G * GC
    assert CH <= NCH
    H1, F1 = a["L1_gnn_a_w"].shape[0], a["L1_gnn_a_w"].shape[1] // 2
    L, _, HF2 = a["L2_gnn_weights"].shape
    H2, F2 = a["L2_gnn_atts"].shape[1], a["L2_gnn_atts"].shape[2] // 2
    HID = a["L3_gnn_W1"].shape[1]
    STEPS, DT = 12, 0.5
    AT = H2 * NA
    ATT0 = 5 * 512

    table = nc.dram_tensor("node_rows", [NP, HF2], F32).ap()
    table1 = nc.dram_tensor("node_rows_narrow", [NP, D], F32).ap()
    sorted_d = nc.dram_tensor("sorted_edges", [NCH * P, REC], F32).ap()

    ctx = ExitStack()
    with ctx:
        def sb(name, shape, dt=F32):
            return ctx.enter_context(nc.sbuf_tensor(name, shape, dt))

        ps = ctx.enter_context(nc.psum_tensor("ps", [P, 4096], F32))

        lane = sb("lane", [P, P])
        lane16 = sb("lane16", [P, P], BF16)
        part = sb("part", [P, 1])
        ident = sb("ident", [P, P])
        ident16 = sb("ident16", [P, P], F16)
        identb = sb("identb", [P, P], BF16)
        upper = sb("upper", [P, P])
        lower = sb("lower", [P, P])
        ones = sb("ones", [P, P])
        zerob = sb("zerob", [P, 512], BF16)
        tens = sb("tens", [P, 10])
        nodeid = sb("nodeid", [P, NP], F16)
        chunkid = sb("chunkid", [P, NCH])
        x = sb("x_sb", [P, T, D])
        h = sb("h_sb", [P, T, D])
        hT = sb("hT", [P, NP])
        wide = sb("wide", [P, T, HF2])
        small = sb("small", [P, T, 8])
        stat = sb("stat", [P, 4, T])
        rec = sb("rec", [P, NCH, REC])
        arena = sb("arena", [P, 2, NCH * P], BF16)
        onehotT = arena[:, 0, :]
        NB = NP // HALF
        blockmask = arena[:, 1, 0:NCH * 2 * NB].rearrange("p (c s b) -> p c s b", s=2, b=NB)
        early = arena[:, 1, NCH * 2 * NB:NCH * 2 * NB + 2 * EARLY * HF2].bitcast(F32)
        idx = sb("idx", [P, 2, NCH], I32)
        round_tiles = sb("round_tiles", [P, NCH // RING, 2], I32)
        tile_end = sb("tile_end", [P, T], I32)
        ring = sb("ring", [P, RING, HF2])
        slot_idx = sb("slot_idx", [P, SLOTS0], I32)
        scratch = sb("scratch", [P, 5300])
        carry_in = sb("carry_in", [4, 2, NCH])
        carry_on = sb("carry_on", [4, 2, NCH])
        reset = sb("reset", [GC, 2, 4, G, P], BF16)
        unreal = sb("unreal", [P, NCH])
        logits = sb("logits", [P, NCH, 4])
        attr_part = sb("attr_part", [P, NCH, L * H2])
        w0 = logits[:].rearrange("p c h -> p (c h)")[:, 0:4 * D].rearrange("p (n d) -> p n d", n=4)
        w1x = sb("w1x", [P, D + 2 * H1])
        w2x = sb("w2x", [P, L, HF2 + 2 * H2])
        ew = sb("ew", [AT, L, D])
        attr_vec = sb("attr_vec", [NA, L * H2])
        bias1 = sb("bias1", [P, D + 2 * H1])
        ab1 = sb("ab1", [P, H1])
        bias2 = sb("bias2", [P, L, D])
        floor2 = sb("floor2", [P, L])
        cols = sb("cols", [P, 8])

        g = Graph()
        g.nc, g.a, g.out, g.N, g.D, g.T = nc, a, out, N, D, T
        g.LAST, g.NP, g.E, g.EA, g.UP, g.UE = LAST, NP, E, EA, UP, UE
        g.UN, g.UC, g.CH, g.G, g.GC, g.NCH = UN, UC, CH, G, GC, NCH
        g.H1, g.F1, g.H2, g.F2, g.L, g.HF2 = H1, F1, H2, F2, L, HF2
        g.HID, g.STEPS, g.DT, g.AT, g.ATT0, g.table = HID, STEPS, DT, AT, ATT0, table
        g.table1, g.sorted_d, g.ps, g.lane, g.lane16, g.part = table1, sorted_d, ps, lane, lane16, part
        g.ident, g.ident16, g.identb, g.upper, g.lower, g.ones = ident, ident16, identb, upper, lower, ones
        g.zerob, g.tens, g.nodeid, g.chunkid, g.x, g.h = zerob, tens, nodeid, chunkid, x, h
        g.hT, g.wide, g.small, g.stat, g.rec, g.arena, g.onehotT = hT, wide, small, stat, rec, arena, onehotT
        g.blockmask, g.idx, g.round_tiles, g.tile_end, g.ring, g.slot_idx, g.scratch = blockmask, idx, round_tiles, tile_end, ring, slot_idx, scratch
        g.carry_in, g.carry_on, g.reset, g.unreal, g.logits, g.attr_part = carry_in, carry_on, reset, unreal, logits, attr_part
        g.w0, g.w1x, g.w2x, g.ew, g.attr_vec, g.bias1, g.ab1 = w0, w1x, w2x, ew, attr_vec, bias1, ab1
        g.bias2, g.floor2, g.cols = bias2, floor2, cols
        g.EARLY, g.EARLY0, g.early = EARLY, EARLY0, early
        g.chunk_rows = sorted_d.rearrange("(c p) k -> p c k", p=P)
        g.got = [ctx.enter_context(nc.semaphore(f"gathered{k}")) for k in range(SLOTS0)]
        g.put = [ctx.enter_context(nc.semaphore(f"scattered{k}")) for k in range(2)]
        g.got_early = ctx.enter_context(nc.semaphore("gathered_early"))
        g.gathered_early = 0
        g.gathered = 0
        g.stage = Stage(nc)
        g.sem = g.stage.sem
        g.scan_a, g.scan_b = h[:].rearrange("p t d -> p (t d)"), hT[:]
        for work in (constants, sort_edges, norm0, block0, sorted_views, norm1, block1, norm2, block2, norm3, block3):
            work(g)
            g.stage.end()
    return nc


def norm0(g):
    node_norm(g, "n0")


def norm1(g):
    node_norm(g, "n1")


def norm2(g):
    node_norm(g, "n2")


def norm3(g):
    node_norm(g, "n3")


def constants(g):
    nc = g.nc
    made, split, xin = g.sem("const_made"), g.sem("const_dve"), g.sem("x_loaded")
    T, LAST, NP = g.T, g.LAST, g.NP
    with nc.Block(name="constants") as block:
        @block.gpsimd
        def _(pool):
            pool.iota(g.lane[:], [[1, P]], base=1, channel_multiplier=0, allow_small_or_imprecise_dtypes=True)
            pool.iota(g.lane16[:], [[1, P]], base=1, channel_multiplier=0, allow_small_or_imprecise_dtypes=True)
            pool.iota(g.part[:], [[0, 1]], base=1, channel_multiplier=1, allow_small_or_imprecise_dtypes=True)
            pool.iota(g.tens[:], [[1, T]], base=0, channel_multiplier=0, allow_small_or_imprecise_dtypes=True)
            pool.iota(g.nodeid[:], [[1, NP]], base=0, channel_multiplier=0, allow_small_or_imprecise_dtypes=True)
            pool.iota(g.chunkid[:], [[1, g.NCH]], base=0, channel_multiplier=0,
                      allow_small_or_imprecise_dtypes=True).then_inc(made, 1)

        @block.vector
        def _(dve):
            dve.memset(g.x[:, T - 1, :], 0.0).then_inc(split, 1)
            dve.memset(g.ones[:], 1.0)
            dve.memset(g.zerob[:], 0.0)
            dve.wait_ge(made, 1)
            for out, op in ((g.ident, ALU.is_equal), (g.ident16, ALU.is_equal), (g.identb, ALU.is_equal),
                            (g.upper, ALU.is_gt), (g.lower, ALU.is_lt)):
                dve.tensor_scalar(out[:], g.lane[:], g.part[:, 0:1], None, op)

        @block.sync
        def _(sp):
            sp.dma_start(g.x[:, 0:T - 1, :], g.a["x"][0:(T - 1) * P, :].rearrange("(t p) d -> p t d", p=P)).then_inc(xin, 16)
            sp.wait_ge(split, 1)
            sp.dma_start(g.x[0:LAST, T - 1, :], g.a["x"][(T - 1) * P:, :]).then_inc(xin, 16)
            sp.wait_ge(xin, 32)


def sort_edges(g):
    nc, a = g.nc, g.a
    UP, UC, UE, UN, T, NCH = g.UP, g.UC, g.UE, g.UN, g.T, g.NCH
    B = 5
    PAIRS = UC // (2 * B)
    rec, scr = g.rec, g.scratch
    s_in, s_self, s_dve = g.sem("sort_in"), g.sem("sort_self"), g.sem("sort_dve")
    s_hot, s_ev = g.sem("sort_onehot"), g.sem("sort_evacuated")
    s_cnt, s_base, s_look, s_rank = g.sem("sort_counted"), g.sem("sort_base"), g.sem("sort_looked"), g.sem("sort_ranked")
    s_zero, s_pos = g.sem("sort_zeroed"), g.sem("sort_positions")
    s_put = g.put
    s_stage, s_round, s_dst16 = g.sem("sort_staged"), g.sem("sort_put_round"), g.sem("sort_dst16")

    lot = Lot(g.arena[:, 1, :])

    def sb(name, shape, dt=F32):
        return lot.take(shape, dt)
    ends_i = sb("ends_i", [P, 2, UC], I32)
    digits_i = sb("digits_i", [P, 2, UC], I32)
    attr_in = sb("attr_in", [P, UE, 16])
    w_in = sb("w_in", [P, UE])
    dst16 = sb("dst16", [P, 2, B], F16)
    dstf = sb("dstf", [P, UC])
    dhi = sb("dhi", [P, UC, T], BF16)
    hot = sb("hot", [P, 2, B, P], BF16)
    before = sb("before", [P, UC, 2, T], BF16)
    rank = sb("rank", [P, UC])
    eqs = sb("eqs", [P, 2, B, P], BF16)
    pos = sb("pos", [P, UC], I32)
    posf = sb("posf", [P, UC])
    stage = sb("stage", [P, 2, PUT0, REC])
    stage_i = sb("stage_i", [P, 2, PUT0], I32)
    nch = sb("nch", [P, 6, T])
    nch_i = sb("nch_i", [P, T], I32)
    tilef = sb("tilef", [P, NCH])
    past = sb("past", [P, NCH, T])
    packed = sb("packed", [P, NCH // RING])
    cnt = scr[:, 0:UC * T].rearrange("p (c t) -> p c t", t=T)
    cum = scr[:, UC * T:2 * UC * T].rearrange("p (c t) -> p c t", t=T)
    picked = scr[:, 0:2 * UC * T].rearrange("p (c s t) -> p c s t", s=2, t=T)
    hotT = g.arena[:, 0, 0:UC * P].rearrange("p (c e) -> p c e", e=P)
    bank = [g.ps[:, 512 * k:512 * k + 512] for k in range(8)]
    g.LATER = UE // SLOTS0 * 2 * PUT0
    PUT = 2
    ROUNDS = (UC - g.LATER) // (2 * PUT)
    assert UE % SLOTS0 == 0 and ROUNDS * 2 * PUT == UC - g.LATER
    g.put_before = 16 * PUT * ROUNDS
    g.ends_i, g.pos, g.put_rows, g.put_slots = ends_i, pos, stage, stage_i

    with nc.Block(name="sort") as block:
        @block.sync
        def _(sp):
            sp.dma_start(ends_i[0:UP, 1, 0:UE], a["dst"].rearrange("(p c) -> p c", c=UE)).then_inc(s_in, 16)
            sp.dma_start(ends_i[0:UP, 0, 0:UE], a["src"].rearrange("(p c) -> p c", c=UE)).then_inc(s_in, 16)
            sp.dma_start(w_in[0:UP, :], a["edge_weight1"].rearrange("(p c) o -> p (c o)", c=UE)).then_inc(s_in, 16)
            sp.dma_start(attr_in[0:UP], a["edge_attr_16"].rearrange("(p c) k -> p c k", c=UE)).then_inc(s_in, 16)
            sp.wait_ge(s_zero, 1)
            sp.dma_start(g.sorted_d.rearrange("(p c) k -> p (c k)", p=P),
                         rec[:].rearrange("p c k -> p (c k)")).then_inc(s_zero, 16)
            sp.wait_ge(s_zero, 17)

        @block.gpsimd
        def _(pool):
            for side in range(2):
                last = pool.iota(ends_i[0:UP, side, UE:UC], [[1, UN]], base=0, channel_multiplier=UN)
            last.then_inc(s_self, 1)
            pool.wait_ge(s_zero, 17)
            with pool.Fori(0, ROUNDS) as i:
                for u in range(2):
                    pool.wait_ge(s_stage, 2 * i + u + 1)
                    pool.sem_inc(s_round, 1)
                    for k in range(PUT):
                        pool.indirect_dma_start(g.sorted_d, bass.IndirectOffsetOnAxis(ap=stage_i[0:UP, u, k:k + 1], axis=0),
                                                stage[0:UP, u, k, :], None).then_inc(s_put[u], 16)
            for u in range(2):
                pool.wait_ge(s_put[u], g.put_before)

        @block.vector
        def _(dve):
            c = Chain(dve, s_dve)
            dve.memset(rec[:], 0.0).then_inc(s_zero, 1)
            dve.wait_ge(s_in, 64)
            dve.wait_ge(s_self, 1)
            dve.tensor_scalar(digits_i[0:UP, 0, :], ends_i[0:UP, 1, :], 7, None, ALU.arith_shift_right)
            c.step(dve.tensor_scalar(digits_i[0:UP, 1, :], ends_i[0:UP, 1, :], P - 1, None, ALU.bitwise_and))
            dve.wait_ge(s_zero, 17)
            dve.tensor_copy(rec[0:UP, 0:UC, R_DHI], digits_i[0:UP, 0, :])
            dve.tensor_scalar(rec[0:UP, 0:UC, R_DLO], digits_i[0:UP, 1, :], 1.0, None, ALU.add)
            dve.tensor_copy(rec[0:UP, 0:UC, R_SRC], ends_i[0:UP, 0, :])
            dve.tensor_copy(rec[0:UP, 0:UE, R_W], w_in[0:UP, :])
            dve.memset(rec[0:UP, 0:UE, R_ORIG], 1.0)
            dve.memset(rec[0:UP, 0:UC, R_REAL], 1.0)
            dve.tensor_copy(rec[0:UP, 0:UE, R_ATTR:R_ATTR + 16], attr_in[0:UP])
            c.step(dve.tensor_copy(dstf[0:UP, :], ends_i[0:UP, 1, :]))
            c.step(dve.tensor_tensor(dhi[0:UP], g.tens[0:UP, :].unsqueeze(1).broadcast_to([UP, UC, T]),
                                     rec[0:UP, 0:UC, R_DHI].unsqueeze(2).broadcast_to([UP, UC, T]), ALU.is_equal))
            with dve.Fori(0, PAIRS) as i:
                for u in range(2):
                    dve.wait_ge(s_cnt, 2 * i + u + 1)
                    dve.tensor_tensor(hot[0:UP, u], g.lane16[0:UP, :].unsqueeze(1).broadcast_to([UP, B, P]),
                                      rec[0:UP, bass.ds((2 * i + u) * B, B), R_DLO].unsqueeze(2).broadcast_to([UP, B, P]),
                                      ALU.is_equal).then_inc(s_hot, 1)
            dve.wait_ge(s_ev, 2 + 2 * PAIRS)
            for t in range(T):
                last = dve.tensor_tensor_scan(cum[:, :, t], g.ones[:, 0:1].broadcast_to([P, UC]), cnt[:, :, t],
                                              0.0, ALU.mult, ALU.add)
            last.then_inc(s_base, 1)
            dve.wait_ge(s_look, 1)
            dve.tensor_copy(nch[:, 0, :], bank[0][:, 0:T])
            c.step(dve.tensor_scalar(nch_i[:], bank[1][:, 0:T], float(P - 1), None, ALU.add))
            c.step(dve.tensor_scalar(nch_i[:], nch_i[:], 7, None, ALU.arith_shift_right))
            c.step(dve.tensor_copy(nch[:, 1, :], nch_i[:]))
            c.step(dve.tensor_tensor_scan(nch[:, 2, :], g.ones[:, 0:T], nch[:, 1, :], 0.0, ALU.mult, ALU.add))
            c.step(dve.tensor_tensor(nch[:, 3, :], nch[:, 2, :], nch[:, 1, :], ALU.subtract))
            c.step(dve.scalar_tensor_tensor(nch[:, 4, :], nch[:, 3, :], float(P), nch[:, 0, :], ALU.mult, ALU.add))
            c.step(dve.tensor_tensor(cum, cum, cnt, ALU.subtract))
            c.step(dve.tensor_tensor(cum, cum, nch[:, 4, :].unsqueeze(1).broadcast_to([P, UC, T]), ALU.add))
            c.step(dve.tensor_copy(before[:, :, 0], cum))
            dve.tensor_tensor(before[:, :, 1], cum, before[:, :, 0], ALU.subtract).then_inc(s_base, 1)
            c.step(dve.tensor_tensor(past[:, :, 0:T - 1], g.chunkid[:].unsqueeze(2).broadcast_to([P, NCH, T - 1]),
                                     nch[:, 2, 0:T - 1].unsqueeze(1).broadcast_to([P, NCH, T - 1]), ALU.is_ge))
            c.step(dve.tensor_reduce(tilef[:], past[:, :, 0:T - 1], AX_X, ALU.add))
            c.step(dve.tensor_scalar(tilef[:], tilef[:], 1.0, None, ALU.add))
            tiles = tilef.rearrange("p (r k) -> p r k", k=RING)
            for k in range(RING - 2, -1, -1):
                c.step(dve.scalar_tensor_tensor(packed, packed if k < RING - 2 else tiles[:, :, RING - 1], 16.0, tiles[:, :, k],
                                                ALU.mult, ALU.add))
            dve.tensor_copy(g.round_tiles[:, :, 0], packed)
            c.step(dve.memset(g.round_tiles[:, :, 1], ALL_ONE))
            dve.tensor_scalar(g.round_tiles[:, 0:g.EARLY, 1], tilef[:, g.EARLY0:g.EARLY0 + g.EARLY], float(ALL_ONE - 1), None, ALU.add)
            dve.tensor_copy(g.tile_end[:, 0:T - 1], nch[:, 2, 0:T - 1])
            dve.memset(g.tile_end[:, T - 1:T], g.CH)
            with dve.Fori(0, PAIRS) as i:
                for u in range(2):
                    dve.wait_ge(s_look, 2 * i + u + 2)
                    for k in range(B):
                        col = (2 * i + u) * B + k
                        dve.scalar_tensor_tensor(eqs[0:UP, u, k, 0:UP], bank[2 + 3 * u + k // 4][0:UP, (k % 4) * P:(k % 4) * P + UP],
                                                 dstf[0:UP, bass.ds(col, 1)], g.lower[0:UP, 0:UP], ALU.is_equal, ALU.mult,
                                                 accum_out=rank[0:UP, bass.ds(col, 1)])
                    dve.tensor_tensor(picked[0:UP, bass.ds((2 * i + u) * B, B)],
                                      bank[4 + 3 * u][0:UP, 0:2 * B * T].rearrange("p (c s t) -> p c s t", s=2, t=T),
                                      dhi[0:UP, bass.ds((2 * i + u) * B, B), :].unsqueeze(2).broadcast_to([UP, B, 2, T]),
                                      ALU.mult).then_inc(s_rank, 1)
            dve.wait_ge(s_rank, 2 + 2 * PAIRS)
            c.step(dve.tensor_reduce(posf[0:UP, :], picked[0:UP].rearrange("p c s t -> p c (s t)"), AX_X, ALU.add))
            dve.tensor_tensor(pos[0:UP, :], posf[0:UP, :], rank[0:UP, :], ALU.add).then_inc(s_pos, 1)

        @block.tensor
        def _(pe):
            pe.sem_inc(s_cnt, 2)
            pe.wait_ge(s_dve, 1)
            with pe.Fori(0, PAIRS) as i:
                for u in range(2):
                    pe.wait_ge(s_hot, 2 * i + u + 1)
                    pe.wait_ge(s_ev, 2 * i + u + 1)
                    turned = bank[2 + u].bitcast(BF16)
                    for k in range(B):
                        pe.transpose(turned[:, k * P:k * P + UP], hot[0:UP, u, k, :], g.identb[0:UP, 0:UP])
                    for k in range(B):
                        mm = pe.matmul(bank[4 + u][:, k * T:(k + 1) * T], hot[0:UP, u, k, :],
                                       dhi[0:UP, bass.ds((2 * i + u) * B + k, 1), :].rearrange("p o t -> p (o t)"), start=True, stop=True)
                    mm.then_inc(s_cnt, 1)
            pe.wait_ge(s_base, 1)
            pe.wait_ge(s_ev, 2 + 2 * PAIRS)
            pe.matmul(bank[0][:, 0:T], g.upper[:], cum[:, UC - 1, :], start=True, stop=True)
            pe.matmul(bank[1][:, 0:T], g.ones[:], cum[:, UC - 1, :], start=True, stop=True).then_inc(s_look, 1)
            pe.sem_inc(s_rank, 2)
            pe.wait_ge(s_base, 2)
            with pe.Fori(0, PAIRS) as i:
                for u in range(2):
                    pe.wait_ge(s_dst16, 2 * i + u + 1)
                    pe.wait_ge(s_rank, 2 * i + u + 1)
                    for k in range(B):
                        col = (2 * i + u) * B + k
                        pe.matmul(bank[4 + 3 * u][0:UP, 2 * k * T:2 * (k + 1) * T],
                                  hotT[:, bass.ds(col, 1), 0:UP].rearrange("p o e -> p (o e)"),
                                  before[:, bass.ds(col, 1)].rearrange("p o s t -> p (o s t)"), start=True, stop=True)
                        mm = pe.matmul(bank[2 + 3 * u + k // 4][0:UP, (k % 4) * P:(k % 4) * P + UP],
                                       dst16[0:UP, u, k:k + 1].broadcast_to([UP, UP]), g.ident16[0:UP, 0:UP],
                                       start=True, stop=True)
                    mm.then_inc(s_look, 1)

        @block.scalar
        def _(act):
            act.sem_inc(s_ev, 2)
            act.wait_ge(s_in, 64)
            act.wait_ge(s_self, 1)
            for u in range(2):
                act.copy(dst16[0:UP, u, :], ends_i[0:UP, 1, u * B:(u + 1) * B]).then_inc(s_dst16, 1)
            with act.Fori(0, PAIRS) as i:
                for u in range(2):
                    act.wait_ge(s_cnt, 2 * i + u + 3)
                    turned = bank[2 + u].bitcast(BF16)[:, 0:B * P].rearrange("p (c e) -> p c e", e=P)
                    act.copy(hotT[:, bass.ds((2 * i + u) * B, B), 0:UP], turned[:, :, 0:UP])
                    act.copy(cnt[:, bass.ds((2 * i + u) * B, B), :],
                             bank[4 + u][:, 0:B * T].rearrange("p (c t) -> p c t", t=T)).then_inc(s_ev, 1)
            with act.Fori(0, PAIRS - 1) as i:
                for u in range(2):
                    act.wait_ge(s_look, 2 * i + u + 2)
                    act.copy(dst16[0:UP, u, :], ends_i[0:UP, 1, bass.ds((2 * i + u + 2) * B, B)]).then_inc(s_dst16, 1)
            act.wait_ge(s_pos, 1)
            for u in range(2):
                columns = slice(u * PUT + g.LATER, (u + 1) * PUT + g.LATER)
                act.copy(stage_i[0:UP, u, 0:PUT], pos[0:UP, columns])
                act.copy(stage[0:UP, u, 0:PUT], rec[0:UP, columns, :]).then_inc(s_stage, 1)
            with act.Fori(1, ROUNDS) as i:
                for u in range(2):
                    act.wait_ge(s_put[u], 16 * PUT * i)
                    columns = bass.ds((2 * i + u) * PUT + g.LATER, PUT)
                    act.copy(stage_i[0:UP, u, 0:PUT], pos[0:UP, columns])
                    act.copy(stage[0:UP, u, 0:PUT], rec[0:UP, columns, :]).then_inc(s_stage, 1)

        weights(g, block, s_pos)


def sorted_views(g):
    nc, NCH, GC, G, L, H2 = g.nc, g.NCH, g.GC, g.G, g.L, g.H2
    rec = g.rec
    B = 4
    NB = g.NP // HALF
    BATCHES = NCH // (2 * B)
    s_rec, s_dve, s_hot, s_tr, s_ev = (g.sem(f"view_{n}") for n in ("records", "dve", "onehot", "turned", "copied"))
    s_dst, s_rows, s_near, s_inner, s_carry = (g.sem(f"view_{n}") for n in ("dst", "dst_rows", "first_last", "inner", "carry"))
    bank = [g.ps[:, 512 * k:512 * k + 512] for k in range(8)]
    lot = Lot(g.scratch[:].bitcast(BF16))
    hot = lot.take([P, 2, B, 2, HALF], BF16)
    digits_i = lot.take([P, 2, 2, NCH], I32)
    digits = lot.take([P, 2, NCH, 2])
    dstf = lot.take([P, NCH])
    ends = lot.take([P, 2, 4])
    dstrow = lot.take([P, G, P])
    inner = lot.take([P, G, 4])
    near = lot.take([P, 2, NCH])
    ROWS = P // B
    assert NA <= ROWS
    a_weights, a_staged, a_turned, a_copied, a_products, a_taken = (
        g.sem(f"attr_{n}") for n in ("weights", "staged", "turned", "copied", "products", "taken"))
    attr = lot.take([P, 2, B, ROWS])
    attrT = lot.take([P, 2, P])
    four = lot.take([P, B, L * H2])

    with nc.Block(name="views") as block:
        @block.sync
        def _(sp):
            sp.dma_start(rec[:], g.chunk_rows).then_inc(s_rec, 16)
            sp.wait_ge(s_rec, 16)

        @block.vector
        def _(dve):
            c = Chain(dve, s_dve)
            dve.tensor_scalar(ends[:, 0, :], g.part[:, 0:1].broadcast_to([P, 4]), 1.0, None, ALU.is_equal)
            dve.tensor_scalar(ends[:, 1, :], g.part[:, 0:1].broadcast_to([P, 4]), float(P), None, ALU.is_equal)
            dve.memset(attr[:], 0.0).then_inc(a_weights, 1)
            dve.memset(four[:], 0.0).then_inc(a_weights, 1)
            dve.wait_ge(a_weights, 2)
            for k in range(B):
                dve.tensor_copy(four[ROWS * k:ROWS * k + NA, k, :], g.attr_vec[:]).then_inc(a_weights, 1)
            dve.wait_ge(s_rec, 16)
            dve.tensor_copy(g.idx[:, 0, :], rec[:, :, R_SRC])
            dve.tensor_scalar(g.unreal[:], rec[:, :, R_REAL], -1.0, BIG, ALU.add, ALU.mult)
            dve.scalar_tensor_tensor(dstf, rec[:, :, R_DHI], float(P), rec[:, :, R_DLO], ALU.mult, ALU.add).then_inc(s_dst, 1)
            dve.wait_ge(s_dst, 1)
            c.step(dve.tensor_scalar(g.idx[:, 1, :], dstf, -1.0, 0.0, ALU.add, ALU.max))
            for side in range(2):
                dve.tensor_scalar(digits_i[:, 0, side, :], g.idx[:, 1 - side, :], HALF - 1, None, ALU.bitwise_and)
                last = dve.tensor_scalar(digits_i[:, 1, side, :], g.idx[:, 1 - side, :], 6, None, ALU.arith_shift_right)
            c.step(last)
            for side in range(2):
                dve.tensor_copy(digits[:, 0, :, side], digits_i[:, 0, side, :])
                last = dve.tensor_copy(digits[:, 1, :, side], digits_i[:, 1, side, :])
            c.step(last)
            dve.tensor_tensor(g.blockmask[:], g.nodeid[:, 0:NB].unsqueeze(1).unsqueeze(1).broadcast_to([P, NCH, 2, NB]),
                              digits[:, 1].unsqueeze(3).broadcast_to([P, NCH, 2, NB]), ALU.is_equal)

            def turned_inputs(i):
                for u in range(2):
                    dve.wait_ge(a_turned, 2 * i + u + 1)
                    dve.tensor_copy(attr[:, u, :, 0:NA], rec[:, bass.ds((2 * i + u) * B, B), R_ATTR:R_ATTR + NA]).then_inc(a_staged, 1)
                for u in range(2):
                    dve.wait_ge(s_tr, 2 * i + u + 1)
                    dve.tensor_tensor(hot[:, u], g.nodeid[:, 0:HALF].unsqueeze(1).unsqueeze(1).broadcast_to([P, B, 2, HALF]),
                                      digits[:, 0, bass.ds((2 * i + u) * B, B), :].unsqueeze(3).broadcast_to([P, B, 2, HALF]),
                                      ALU.is_equal).then_inc(s_hot, 1)

            def take_products(i):
                for u in range(2):
                    dve.wait_ge(a_products, 2 * i + u + 1)
                    dve.tensor_copy(g.attr_part[:, bass.ds((2 * i + u) * B, B), :],
                                    bank[4 + u][:, 0:B * L * H2].rearrange("p (c q) -> p c q", c=B)).then_inc(a_taken, 1)

            turned_inputs(0)
            with dve.Fori(0, BATCHES - 1) as i:
                turned_inputs(i + 1)
                take_products(i)
            take_products(BATCHES - 1)
            dve.wait_ge(s_rows, 1)
            rows = bank[6][0:GC, 0:G * P].rearrange("p (g e) -> p g e", g=G)
            c.step(dve.tensor_copy(dstrow[0:GC], rows))
            fwd, bwd = g.reset[:, 0, 0], g.reset[:, 1, 0]
            for way, own, nxt, edge in ((fwd, slice(1, P), slice(0, P - 1), 0), (bwd, slice(0, P - 1), slice(1, P), P - 1)):
                dve.tensor_tensor(way[:, :, own], dstrow[0:GC, :, own], dstrow[0:GC, :, nxt], ALU.not_equal)
                last = dve.memset(way[:, :, edge:edge + 1], 1.0)
            c.step(last)
            for way in (fwd, bwd):
                last = dve.tensor_scalar(way, way, -BIG, None, ALU.mult)
            c.step(last)
            for hd in range(1, 4):
                for d in range(2):
                    dve.tensor_copy(g.reset[:, d, hd], g.reset[:, d, 0])
            for k in range(4):
                last = dve.tensor_reduce(inner[0:GC, :, k], fwd[:, :, 1:P], AX_X, ALU.min)
            last.then_inc(s_inner, 1)
            dve.wait_ge(s_near, 1)
            c.step(dve.tensor_copy(near[0:4], bank[7][0:4, 0:2 * NCH].rearrange("p (s c) -> p s c", s=2)))
            dve.memset(g.carry_in[:, 0, 0:1], 1.0)
            dve.memset(g.carry_in[:, 1, NCH - 1:NCH], 1.0)
            for at in (slice(1, NCH), slice(0, NCH - 1)):
                last = dve.tensor_tensor(g.carry_in[:, 0 if at.start else 1, at], near[0:4, 0, 1:NCH], near[0:4, 1, 0:NCH - 1],
                                         ALU.not_equal)
            c.step(last)
            c.step(dve.tensor_scalar(g.carry_in[:], g.carry_in[:], -BIG, None, ALU.mult))
            dve.wait_ge(s_carry, 1)
            for d in range(2):
                dve.tensor_tensor(g.carry_on[:, d, :], g.carry_in[:, d, :], bank[5][0:4, 0:NCH], ALU.add)

        @block.tensor
        def _(pe):
            pe.sem_inc(s_tr, 2)
            pe.wait_ge(s_dst, 1)
            for n in range(G):
                tr = pe.transpose(bank[6][0:GC, n * P:(n + 1) * P], dstf[:, n * GC:(n + 1) * GC], g.ident[:])
            tr.then_inc(s_rows, 1)
            for side in range(2):
                mm = pe.matmul(bank[7][0:4, side * NCH:(side + 1) * NCH], ends[:, side, :], dstf, start=True, stop=True)
            mm.then_inc(s_near, 1)
            for credit in (a_copied, a_turned, a_taken):
                pe.sem_inc(credit, 2)
            pe.wait_ge(a_weights, 2 + B)
            with pe.Fori(0, BATCHES) as i:
                for u in range(2):
                    pe.wait_ge(a_staged, 2 * i + u + 1)
                    pe.wait_ge(a_copied, 2 * i + u + 1)
                    pe.transpose(bank[2 + u][:, 0:P], attr[:, u].rearrange("p c r -> p (c r)"), g.ident[:]).then_inc(a_turned, 1)
                for u in range(2):
                    pe.wait_ge(s_hot, 2 * i + u + 1)
                    pe.wait_ge(s_ev, 2 * i + u + 1)
                    turned = bank[u].bitcast(BF16)
                    for k in range(B):
                        tr = pe.transpose(turned[:, k * P:(k + 1) * P], hot[:, u, k].rearrange("p s e -> p (s e)"), g.identb[:])
                    tr.then_inc(s_tr, 1)
                for u in range(2):
                    pe.wait_ge(a_copied, 2 * i + u + 3)
                    pe.wait_ge(a_taken, 2 * i + u + 1)
                    pe.matmul(bank[4 + u][:, 0:B * L * H2], attrT[:, u, :], four.rearrange("p c q -> p (c q)"),
                              start=True, stop=True).then_inc(a_products, 1)
            pe.wait_ge(s_inner, 1)
            for n in range(G):
                tr = pe.transpose(bank[5][0:4, n * GC:(n + 1) * GC], inner[0:GC, n, :], g.ident[0:GC, 0:GC])
            tr.then_inc(s_carry, 1)

        @block.scalar
        def _(act):
            act.sem_inc(s_ev, 2)
            with act.Fori(0, BATCHES) as i:
                for u in range(2):
                    act.wait_ge(a_turned, 2 * i + u + 3)
                    act.copy(attrT[:, u, :], bank[2 + u][:, 0:P]).then_inc(a_copied, 1)
                for u in range(2):
                    act.wait_ge(s_tr, 2 * i + u + 3)
                    act.copy(g.onehotT[:, bass.ds((2 * i + u) * B * P, B * P)], bank[u].bitcast(BF16)[:, 0:B * P]).then_inc(s_ev, 1)


def weights(g, block, free):
    a, D, L, H1, F1, H2, F2, HF2, AT = g.a, g.D, g.L, g.H1, g.F1, g.H2, g.F2, g.HF2, g.AT
    s_in, s_dve, s_ewn, s_turn, s_v, s_col = (g.sem(f"wts_{n}") for n in ("loaded", "dve", "edge", "turned", "v", "columns"))
    bank = [g.ps[:, 512 * k:512 * k + 512] for k in range(8)]
    lot = Lot(g.scratch[:].bitcast(BF16))
    att = lot.take([P, L * H2 * 2 * F2])
    a1 = lot.take([P, H1 * 2 * F1])
    ewn = lot.take([P, L, H2, NA])
    attj = lot.take([P, L, H2])
    rows = lot.take([P, P])
    NR = 2 * L * H2 + 4
    count = lot.take([P, 1], I32)
    prod = g.wide[:].rearrange("p t f -> p (t f)")
    LOADS = 19

    @block.sync
    def _(sp):
        def load(dst, src):
            sp.dma_start(dst, src).then_inc(s_in, 16)
        load(g.w2x[:, :, 0:HF2], a["L2_gnn_weights"].rearrange("l i o -> i l o"))
        load(g.w1x[:, 0:D], a["L1_gnn_W_w"])
        load(g.bias1[:, 0:D], a["L1_gnn_W_b"].partition_broadcast(P))
        for n, name in enumerate(("W1", "W2", "Wo", "Wn")):
            load(g.w0[:, n, :], a["L0_gnn_" + name])
        load(g.ab1[:], a["L1_gnn_a_b"].partition_broadcast(P))
        load(g.bias2[:].rearrange("p l d -> p (l d)"), a["L2_gnn_biases"].rearrange("l d -> (l d)").partition_broadcast(P))
        load(g.cols[:, 5:6], a["L3_gnn_clearance"].partition_broadcast(P))
        sp.wait_ge(free, 1)
        load(ewn[:, :, :, 0:NA - 1], a["L2_gnn_edge_ws"].rearrange("l (h f) k -> f l h k", h=H2))
        load(rows[0:L * H2, :], a["L2_gnn_edge_bs"].rearrange("l (h f) -> (l h) f", h=H2))
        load(rows[L * H2:2 * L * H2, :], a["L2_gnn_atts"].rearrange("l h f -> (l h) f")[:, F2:])
        load(rows[2 * L * H2:2 * L * H2 + 1, :], a["L0_gnn_gamma"].unsqueeze(0))
        load(rows[2 * L * H2 + 1:2 * L * H2 + 2, :], a["L0_gnn_beta"].unsqueeze(0))
        load(rows[2 * L * H2 + 2:2 * L * H2 + 4, :], a["L3_gnn_b1"].rearrange("(k p) -> k p", p=P))
        load(att, a["L2_gnn_atts"].rearrange("l h f -> (l h f)").partition_broadcast(P))
        load(a1, a["L1_gnn_a_w"].rearrange("h f -> (h f)").partition_broadcast(P))
        load(count, a["L0_gnn_batch_num"][0:1].partition_broadcast(P))
        sp.wait_ge(s_in, 16 * LOADS)

    @block.vector
    def _(dve):
        c = Chain(dve, s_dve)
        dve.memset(g.floor2[:, 0:L - 1], 0.0)
        dve.memset(g.floor2[:, L - 1:L], -3.0e38)
        dve.wait_ge(s_in, 16 * LOADS)
        dve.tensor_copy(g.cols[:, 4:5], count)
        for src, folded, vec in ((g.w1x, g.w1x, a1), (g.bias1, g.bias1, a1)):
            for side in range(2):
                c.step(dve.tensor_tensor(prod[:, 0:D].rearrange("p (h f) -> p h f", h=H1),
                                         src[:, 0:D].rearrange("p (h f) -> p h f", h=H1),
                                         vec.rearrange("p (h s f) -> p h s f", h=H1, s=2)[:, :, side, :], ALU.mult))
                c.step(dve.tensor_reduce(folded[:, D + side * H1:D + (side + 1) * H1],
                                         prod[:, 0:D].rearrange("p (h f) -> p h f", h=H1), AX_X, ALU.add))
        for l in range(L):
            for side in range(2):
                at = (l * 2 + side) % 4 * HF2
                part = prod[:, at:at + HF2].rearrange("p (h f) -> p h f", h=H2)
                c.step(dve.tensor_tensor(part, g.w2x[:, l, 0:HF2].rearrange("p (h f) -> p h f", h=H2),
                                         att.rearrange("p (l h s f) -> p l h s f", l=L, h=H2, s=2)[:, l, :, side, :], ALU.mult))
                c.step(dve.tensor_reduce(g.w2x[:, l, HF2 + side * H2:HF2 + (side + 1) * H2], part, AX_X, ALU.add))
        dve.wait_ge(s_col, 1)
        dve.tensor_copy(ewn[:, :, :, NA - 1], bank[3][:, 0:L * H2].rearrange("p (l h) -> p l h", l=L))
        dve.tensor_copy(attj, bank[3][:, L * H2:2 * L * H2].rearrange("p (l h) -> p l h", l=L)).then_inc(s_ewn, 1)
        dve.tensor_copy(g.cols[:, 0:4], bank[3][:, 2 * L * H2:NR])
        dve.wait_ge(s_turn, 1)
        dve.tensor_copy(g.ew[:].rearrange("k l d -> k (l d)")[:, 0:512], bank[0][0:AT, 0:512])
        dve.tensor_copy(g.ew[:].rearrange("k l d -> k (l d)")[:, 512:L * D], bank[1][0:AT, 0:L * D - 512])
        dve.wait_ge(s_v, 1)
        dve.tensor_copy(g.attr_vec[:], bank[2][0:NA, 0:L * H2])

    @block.tensor
    def _(pe):
        pe.wait_ge(s_in, 16 * LOADS)
        pe.transpose(bank[3][:, 0:NR], rows[0:NR, :], g.ident[0:NR, 0:NR]).then_inc(s_col, 1)
        pe.wait_ge(s_ewn, 1)
        for l in range(L):
            tr = pe.transpose(bank[l // 4][0:AT, (l % 4) * D:(l % 4) * D + D],
                              ewn[:, l].rearrange("p h k -> p (h k)"), g.ident[:])
        tr.then_inc(s_turn, 1)
        for l in range(L):
            for hd in range(H2):
                mm = pe.matmul(bank[2][0:NA, l * H2 + hd:l * H2 + hd + 1], ewn[:, l, hd, :], attj[:, l, hd:hd + 1],
                               start=True, stop=True)
        mm.then_inc(s_v, 1)


def node_norm(g, name):
    nc, T, D = g.nc, g.T, g.D
    s_dve, s_var, s_std, s_h, s_turn = (g.sem(f"{name}_{n}") for n in ("dve", "var", "std", "h", "turned"))
    st = g.stat
    with nc.Block(name=name) as block:
        @block.vector
        def _(dve):
            c = Chain(dve, s_dve)
            wide = [P, T, D]
            c.step(dve.tensor_reduce(st[:, 0, :], g.x[:], AX_X, ALU.add))
            c.step(dve.tensor_scalar(st[:, 1, :], st[:, 0, :], 1.0 / D, None, ALU.mult))
            c.step(dve.tensor_tensor(g.h[:], g.x[:], st[:, 1, :].unsqueeze(2).broadcast_to(wide), ALU.subtract))
            c.step(dve.tensor_tensor(g.wide[:, :, 0:D], g.h[:], g.h[:], ALU.mult))
            c.step(dve.tensor_reduce(st[:, 2, :], g.wide[:, :, 0:D], AX_X, ALU.add))
            dve.tensor_scalar(st[:, 2, :], st[:, 2, :], 1.0 / D, 1.0e-5, ALU.mult, ALU.add).then_inc(s_var, 1)
            dve.wait_ge(s_std, 1)
            c.step(dve.reciprocal(st[:, 1, :], st[:, 3, :]))
            dve.scalar_tensor_tensor(g.h[:], g.h[:], 0.0, st[:, 1, :].unsqueeze(2).broadcast_to(wide), ALU.max, ALU.mult).then_inc(s_h, 1)

        @block.scalar
        def _(act):
            act.wait_ge(s_var, 1)
            act.activation(st[:, 3, :], st[:, 2, :], ACT.Sqrt).then_inc(s_std, 1)
            turn_copies(g, act, s_turn)

        @block.tensor
        def _(pe):
            pe.wait_ge(s_h, 1)
            turn_nodes(g, pe, s_turn)


def turn_nodes(g, pe, turned, banks=0):
    for t in range(g.T):
        tr = pe.transpose(g.ps[:, 512 * banks + t * P:512 * banks + (t + 1) * P], g.h[:, t, :], g.ident[:])
        if t % 4 == 3 or t == g.T - 1:
            tr.then_inc(turned, 1)


def turn_copies(g, act, turned, banks=0, start=0):
    for n, at in enumerate(range(0, g.NP, 512)):
        act.wait_ge(turned, start + n + 1)
        to = min(at + 512, g.NP)
        last = act.copy(g.hT[:, at:to], g.ps[:, 512 * banks + at:512 * banks + to])
    return last


def halves(g):
    return [(at, min(at + 512, g.NP)) for at in range(0, g.NP, 512)]


def block0(g):
    nc, T, D, N, NP = g.nc, g.T, g.D, g.N, g.NP
    bank = [g.ps[:, 512 * k:512 * k + 512] for k in range(8)]
    flat = g.wide[:].rearrange("p t f -> p (t f)")
    l1T, h2T = flat[:, 0:NP], flat[:, NP:2 * NP]
    s_mm, s_sc, s_act, s_h2, s_h2c, s_st = (g.sem(f"b0_{n}") for n in
                                            ("hidden", "scaled", "leaky", "h2", "h2_copied", "stored"))
    with nc.Block(name="b0_dense") as block:
        @block.tensor
        def _(pe):
            for n, (p, q) in enumerate(halves(g)):
                pe.matmul(bank[n][:, 0:q - p], g.w0[:, 0, :], g.hT[:, p:q], start=True, stop=True).then_inc(s_mm, 1)
            for n, (p, q) in enumerate(halves(g)):
                pe.wait_ge(s_act, n + 1)
                for t in range(p // P, q // P):
                    mm = pe.matmul(bank[3 + n][:, t * P - p:t * P - p + P], l1T[:, t * P:(t + 1) * P], g.w0[:, 1, :],
                                   start=True, stop=True)
                mm.then_inc(s_h2, 1)
            for n, (p, q) in enumerate(halves(g)):
                pe.matmul(bank[n][:, 0:q - p], g.w0[:, 1, :], l1T[:, p:q], start=True, stop=True).then_inc(s_h2, 1)

        @block.scalar
        def _(act):
            for n, (p, q) in enumerate(halves(g)):
                act.wait_ge(s_mm, n + 1)
                act.activation(l1T[:, p:q], bank[n][:, 0:q - p], ACT.Copy, scale=0.01).then_inc(s_sc, 1)
            for n, (p, q) in enumerate(halves(g)):
                act.wait_ge(s_h2, n + 4)
                act.copy(h2T[:, p:q], bank[n][:, 0:q - p])

        @block.vector
        def _(dve):
            for n, (p, q) in enumerate(halves(g)):
                dve.wait_ge(s_sc, n + 1)
                dve.tensor_tensor(l1T[:, p:q], bank[n][:, 0:q - p], l1T[:, p:q], ALU.max).then_inc(s_act, 1)
            for n, (p, q) in enumerate(halves(g)):
                dve.wait_ge(s_h2, n + 1)
                dve.tensor_copy(g.h[:, p // P:q // P, :].rearrange("p t d -> p (t d)"), bank[3 + n][:, 0:q - p]).then_inc(s_h2c, 1)

        @block.sync
        def _(sp):
            sp.wait_ge(s_h2c, 3)
            sp.dma_start(g.table1.rearrange("(t p) d -> p t d", p=P), g.h[:]).then_inc(s_st, 16)
            sp.wait_ge(s_st, 16)

    staged, free, round_ = g.sem("b0_staged"), g.sem("b0_slot_free"), g.sem("b0_round")
    put_staged = g.sem("b0_put_staged")
    got, before = g.got, g.gathered
    UP, ROUNDS, half = g.UP, g.UE // SLOTS0, SLOTS0 // 2
    g.gathered += 16 * ROUNDS
    s_hi, s_mid, s_rest, s_lo, s_sum = (g.sem(f"b0_{n}") for n in ("hi", "mid", "rest", "lo", "summed"))
    lot = Lot(g.scratch[:].bitcast(BF16))
    parts = lot.take([P, 2, 3, D], BF16)
    rest = lot.take([P, 2, D])
    hot = lot.take([P, 2, NP], BF16)
    ring = g.ring[:].rearrange("p k (s d) -> p (k s) d", d=D)
    ends = [(p, min(q, N)) for p, q in halves(g)]
    assert SLOTS0 <= 2 * RING and SLOTS0 % 2 == 0
    with nc.Block(name="b0_edges") as block:
        @block.gpsimd
        def _(pool):
            pool.sem_inc(free, SLOTS0)
            with pool.Fori(0, ROUNDS) as i:
                for u in range(2):
                    pool.wait_ge(staged, 2 * i + u + 1)
                    for k in range(half * u, half * (u + 1)):
                        pool.wait_ge(free, i * SLOTS0 + k + 1)
                        pool.sem_inc(round_, 1)
                        pool.indirect_dma_start(ring[0:UP, k, :], None, g.table1,
                                                bass.IndirectOffsetOnAxis(ap=g.slot_idx[0:UP, k:k + 1], axis=0)).then_inc(got[k], 16)
                    pool.wait_ge(put_staged, 2 * i + u + 1)
                    pool.sem_inc(round_, 1)
                    for k in range(PUT0):
                        pool.indirect_dma_start(g.sorted_d, bass.IndirectOffsetOnAxis(ap=g.put_slots[0:UP, u, k:k + 1], axis=0),
                                                g.put_rows[0:UP, u, k, :], None).then_inc(g.put[u], 16)
            for u in range(2):
                pool.wait_ge(g.put[u], g.put_before + 16 * PUT0 * ROUNDS)

        @block.scalar
        def _(act):
            def stage_put(i, u):
                act.wait_ge(g.put[u], g.put_before + 16 * PUT0 * i)
                columns = bass.ds((2 * i + u) * PUT0, PUT0)
                act.copy(g.put_slots[0:UP, u, :], g.pos[0:UP, columns])
                act.copy(g.put_rows[0:UP, u], g.rec[0:UP, columns, :]).then_inc(put_staged, 1)

            for u in range(2):
                act.copy(g.slot_idx[0:UP, u * half:(u + 1) * half], g.ends_i[0:UP, 1, u * half:(u + 1) * half]).then_inc(staged, 1)
            stage_put(0, 0)
            with act.Fori(0, ROUNDS) as i:
                for u in range(2):
                    stage_put(i + u, 1 - u)
                    for k in range(half * u, half * u + half):
                        c, m = i * SLOTS0 + k, k % 2
                        act.wait_ge(got[k], before + 16 * (i + 1))
                        act.wait_ge(s_sum, c + 1)
                        act.activation(parts[0:UP, m, 0, :], ring[0:UP, k, :], ACT.Copy,
                                       scale=g.rec[0:UP, bass.ds(c, 1), R_W]).then_inc(s_hi, 1)
                        act.wait_ge(s_rest, c + 1)
                        act.copy(parts[0:UP, m, 1, :], rest[0:UP, m, :]).then_inc(s_mid, 1)
                    act.copy(g.slot_idx[0:UP, half * u:half * u + half],
                             g.ends_i[0:UP, 1, bass.ds((2 * i + u + 2) * half, half)]).then_inc(staged, 1)

        @block.vector
        def _(dve):
            with dve.Fori(0, ROUNDS) as i:
                for k in range(SLOTS0):
                    c, m = i * SLOTS0 + k, k % 2
                    dve.wait_ge(s_hi, c + 1)
                    dve.scalar_tensor_tensor(rest[0:UP, m, :], ring[0:UP, k, :], g.rec[0:UP, bass.ds(c, 1), R_W], parts[0:UP, m, 0, :],
                                             ALU.mult, ALU.subtract).then_inc(s_rest, 1)
                    dve.tensor_scalar(hot[0:UP, m, 0:N], g.nodeid[0:UP, 0:N], g.rec[0:UP, bass.ds(c, 1), R_SRC], None, ALU.is_equal)
                    dve.wait_ge(s_mid, c + 1)
                    dve.tensor_tensor(parts[0:UP, m, 2, :], rest[0:UP, m, :], parts[0:UP, m, 1, :], ALU.subtract).then_inc(s_lo, 1)

        @block.tensor
        def _(pe):
            for n, (p, q) in enumerate(halves(g)):
                pe.matmul(bank[n][:, 0:q - p], g.zerob[:, 0:P], g.zerob[:, 0:q - p], start=True, stop=True, skip_group_check=True)
            pe.sem_inc(s_sum, 2)
            with pe.Fori(0, ROUNDS) as i:
                for k in range(SLOTS0):
                    c, m = i * SLOTS0 + k, k % 2
                    pe.wait_ge(s_lo, c + 1)
                    pe.sem_inc(free, 1)
                    for part in range(3):
                        for n, (p, q) in enumerate(ends):
                            mm = pe.matmul(bank[n][:, 0:q - p], parts[0:UP, m, part, :], hot[0:UP, m, p:q],
                                           start=False, stop=True, skip_group_check=True)
                    mm.then_inc(s_sum, 1)

    s_xn, s_out, s_dve, s_sq, s_std, s_norm, s_turn = (g.sem(f"b0_{n}") for n in
                                                       ("xn", "out", "dve", "var", "std", "normed", "turned"))
    s_sc2 = g.sem("b0_xn_scaled")
    lot = Lot(g.scratch[:].bitcast(BF16))
    xnT, oT, sq = lot.take([P, NP]), lot.take([P, NP]), l1T
    k = lot.take([P, 8])
    with nc.Block(name="b0_finish") as block:
        @block.scalar
        def _(act):
            for n, (p, q) in enumerate(halves(g)):
                act.activation(xnT[:, p:q], bank[n][:, 0:q - p], ACT.Copy, scale=0.01).then_inc(s_sc2, 1)
            act.wait_ge(s_sq, 1)
            act.activation(k[:, 4:5], k[:, 3:4], ACT.Sqrt).then_inc(s_std, 1)

        @block.tensor
        def _(pe):
            for n, (p, q) in enumerate(halves(g)):
                pe.matmul(bank[3 + n][:, 0:q - p], g.w0[:, 2, :], h2T[:, p:q], start=True, stop=False)
                pe.wait_ge(s_xn, n + 1)
                pe.matmul(bank[3 + n][:, 0:q - p], g.w0[:, 3, :], xnT[:, p:q], start=False, stop=True).then_inc(s_out, 1)
            pe.wait_ge(s_norm, 1)
            for t in range(T):
                w = P if t < T - 1 else g.LAST
                tr = pe.transpose(bank[t // 4][0:w, (t % 4) * D:(t % 4) * D + D], oT[:, t * P:t * P + w], g.ident[:])
                if t % 4 == 3 or t == T - 1:
                    tr.then_inc(s_turn, 1)

        @block.vector
        def _(dve):
            c = Chain(dve, s_dve)
            for n, (p, q) in enumerate(halves(g)):
                dve.wait_ge(s_sc2, n + 1)
                dve.tensor_tensor(xnT[:, p:q], bank[n][:, 0:q - p], xnT[:, p:q], ALU.max).then_inc(s_xn, 1)
            c.step(dve.tensor_scalar(k[:, 5:6], g.cols[:, 4:5], -1.0, None, ALU.add))
            dve.reciprocal(k[:, 6:7], g.cols[:, 4:5])
            c.step(dve.reciprocal(k[:, 7:8], k[:, 5:6]))
            for n, (p, q) in enumerate(halves(g)):
                dve.wait_ge(s_out, n + 1)
                last = dve.tensor_copy(oT[:, p:q], bank[3 + n][:, 0:q - p])
            c.step(last)
            c.step(dve.tensor_reduce(k[:, 0:1], oT[:, 0:N], AX_X, ALU.add))
            c.step(dve.tensor_tensor(k[:, 1:2], k[:, 0:1], k[:, 6:7], ALU.mult))
            c.step(dve.tensor_scalar(oT[:, 0:N], oT[:, 0:N], k[:, 1:2], None, ALU.subtract))
            c.step(dve.tensor_tensor(sq[:, 0:N], oT[:, 0:N], oT[:, 0:N], ALU.mult))
            c.step(dve.tensor_reduce(k[:, 2:3], sq[:, 0:N], AX_X, ALU.add))
            dve.tensor_tensor(k[:, 3:4], k[:, 2:3], k[:, 7:8], ALU.mult).then_inc(s_sq, 1)
            dve.wait_ge(s_std, 1)
            c.step(dve.tensor_scalar(k[:, 4:5], k[:, 4:5], 1.0e-6, None, ALU.add))
            c.step(dve.reciprocal(k[:, 3:4], k[:, 4:5]))
            c.step(dve.tensor_tensor(k[:, 3:4], k[:, 3:4], g.cols[:, 0:1], ALU.mult))
            dve.tensor_scalar(oT[:, 0:N], oT[:, 0:N], k[:, 3:4], g.cols[:, 1:2], ALU.mult, ALU.add).then_inc(s_norm, 1)
            add_nodes(g, dve, bank, s_turn)


def add_nodes(g, dve, bank, turned):
    for t in range(0, g.T, 4):
        dve.wait_ge(turned, t // 4 + 1)
        full = min(4, g.T - 1 - t)
        if full > 0:
            xs = g.x[:, t:t + full, :]
            dve.tensor_tensor(xs, xs, bank[t // 4][:, 0:full * g.D].rearrange("p (t d) -> p t d", d=g.D), ALU.add)
        if t + 4 >= g.T:
            xs = g.x[0:g.LAST, g.T - 1, :]
            at = (g.T - 1 - t) * g.D
            dve.tensor_tensor(xs, xs, bank[t // 4][0:g.LAST, at:at + g.D], ALU.add)


def walk_rounds(pe, g, rounds, walk):
    assert g.T <= 15 and 4 * RING <= 24

    def some(first, n):
        _, numbers = g.nc.values_load_multi_w_load_instructions(
            g.round_tiles[0:1, bass.ds(first, n), :].rearrange("p r k -> p (r k)"), engines=[mybir.EngineType.PE],
            min_val=ALL_ONE, max_val=g.T * ALL_ONE)
        for r in range(n):
            walk(first + r, numbers[2 * r], numbers[2 * r + 1])

    with pe.Fori(0, rounds // 2) as j:
        some(2 * j, 2)
    if rounds % 2:
        some(rounds - 1, 1)


def tile_of(packed, k):
    return (packed >> (4 * k)) & 15 if k else packed & 15


def attention(g, name, H, F, weights_, bias, table, logit_terms, extra, layer=0, layers=1):
    nc, T, NCH, G, GC = g.nc, g.T, g.NCH, g.G, g.GC
    HF, S = H * F, 2 * H
    NB = g.NP // HALF
    CB = 12 // H
    WIDTH = CB * H * 2 * NB
    GROUPS = NCH // CB
    assert GROUPS % 2 == 0
    HG = H * G
    EX = g.AT if extra == "attributes" else H
    half = RING // 2
    bank = [g.ps[:, 512 * k:512 * k + 512] for k in range(8)]
    names = ("folded", "scores", "rows", "rows_copied", "stored", "dve", "split", "looked", "masked", "logits", "edge_rows",
             "scan0", "row0", "carry0", "carry0_turned", "scan1", "row1", "carry1", "carry1_turned", "maxima", "max_turned",
             "shifted", "weights", "staged", "round", "early", "act_msg", "dve_msg", "summed", "reduced")
    q = {n: g.sem(f"{name}_{n}") for n in names}
    EARLY, ROUND = g.EARLY, RING + 1
    got, before, before_early = g.got, g.gathered + 16 * EARLY * layer, g.gathered_early + 16 * EARLY * layer
    g.gathered += 16 * EARLY * layers
    g.gathered_early += 16 * EARLY * layers
    lot = Lot(g.scratch[:].bitcast(BF16))
    scores = lot.take([P, 3, H, 2, NB], BF16)
    folded = lot.take([P, S])
    left = lot.take([P, 3, NB, S])
    msg = lot.take([P, ROUND, HF + EX])
    hot = lot.take([P, ROUND, P])
    masked = lot.take([P, 2, WIDTH])
    ends = lot.take([P, 2, G, H])
    rowbuf = lot.take([4, 4, NCH])
    warm = lot.take([P, 1])
    F0, M0 = g.scan_a[0:GC, 0:HG * P], g.scan_b[0:GC, 0:HG * P]
    lg = g.logits
    rows = bank[0:4]

    with nc.Block(name=name) as block:
        @block.tensor
        def _(pe):
            pe.wait_ge(q["folded"], 1)
            for b in range(NB):
                for on in (0, HALF):
                    mm = pe.matmul(bank[6][on:on + HALF, b * S:(b + 1) * S], g.hT[:, b * HALF:(b + 1) * HALF],
                                   folded, start=True, stop=True)
            mm.then_inc(q["scores"], 1)
            for t in range(T):
                if t >= 4:
                    pe.wait_ge(q["rows_copied"], t - 3)
                pe.matmul(rows[t % 4][:, 0:HF], g.hT[:, t * P:(t + 1) * P], weights_[:, 0:HF], start=True, stop=True).then_inc(q["rows"], 1)
            pe.sem_inc(q["masked"], 2)
            pe.sem_inc(q["reduced"], 2)
            pe.wait_ge(q["split"], 1)
            with pe.Fori(0, GROUPS // 2) as i:
                for u in range(2):
                    pe.wait_ge(q["masked"], 2 * i + u + 1)
                    for k in range(CB):
                        c = (2 * i + u) * CB + k
                        for part in range(3):
                            mm = pe.matmul(bank[4 + u][:, k * H * 2 * NB:(k + 1) * H * 2 * NB], g.onehotT[:, bass.ds(c * P, P)],
                                           scores[:, part].rearrange("p h s b -> p (h s b)"), start=part == 0, stop=part == 2)
                    mm.then_inc(q["looked"], 1)
            pe.wait_ge(q["logits"], 1)
            for b in range(HG):
                tr = pe.transpose(bank[b // 4][0:GC, (b % 4) * P:(b % 4) * P + P], lg[:, (b % G) * GC:(b % G + 1) * GC, b // G], g.ident[:])
            tr.then_inc(q["edge_rows"], 1)
            for way, (scan, row_, carry, back) in enumerate(((q["scan0"], q["row0"], q["carry0"], q["carry0_turned"]),
                                                             (q["scan1"], q["row1"], q["carry1"], q["carry1_turned"]))):
                pe.wait_ge(scan, 1)
                for n in range(G):
                    tr = pe.transpose(bank[2 + way][0:H, n * GC:(n + 1) * GC], ends[0:GC, way, n, :], g.ident[0:GC, 0:GC])
                tr.then_inc(row_, 1)
                pe.wait_ge(carry, 1)
                for n in range(G):
                    tr = pe.transpose(bank[6 + way][0:GC, n * H:(n + 1) * H], rowbuf[0:H, 2 * way + 1, n * GC:(n + 1) * GC],
                                      g.ident[0:H, 0:H])
                tr.then_inc(back, 1)
            pe.wait_ge(q["maxima"], 1)
            for b in range(HG):
                tr = pe.transpose(bank[4 + b // 4][:, (b % 4) * GC:(b % 4 + 1) * GC], M0[:, b * P:(b + 1) * P], g.ident[0:GC, 0:GC])
            tr.then_inc(q["max_turned"], 1)
            pe.wait_ge(q["shifted"], 1)
            for b in range(6):
                pe.matmul(bank[b], g.zerob[:, 0:P], g.zerob[:], start=True, stop=True, skip_group_check=True)
            pe.sem_inc(q["summed"], ROUND)
            def sum_round(i, packed, early_tile):
                packed, early_tile = packed - ALL_ONE, early_tile - ALL_ONE
                for k in range(ROUND):
                    n = i * ROUND + k
                    t = tile_of(packed, k) if k < RING else early_tile & 15
                    pe.wait_ge(q["act_msg"], n + 1 + ROUND)
                    pe.wait_ge(q["dve_msg"], n + 1 + ROUND)
                    pe.matmul(g.ps[:, bass.ds(t * HF, HF)], hot[:, k, :], msg[:, k, 0:HF], start=False, stop=True,
                              skip_group_check=True)
                    pe.matmul(g.ps[:, bass.ds(t * EX + g.ATT0, EX)], hot[:, k, :], msg[:, k, HF:HF + EX], start=False, stop=True,
                              skip_group_check=True).then_inc(q["summed"], 1)
            walk_rounds(pe, g, EARLY, sum_round)

        @block.vector
        def _(dve):
            c = Chain(dve, q["dve"])
            dve.tensor_copy(folded, weights_[:, HF:HF + S]).then_inc(q["folded"], 1)
            c.step(dve.memset(scores, 0.0))
            dve.wait_ge(q["scores"], 1)
            found = bank[6][:, 0:NB * S].rearrange("p (b s) -> p b s", b=NB)
            if bias is not None:
                last = dve.tensor_tensor(left[:, 0], found, bias[:, HF:HF + S].unsqueeze(1).broadcast_to([P, NB, S]), ALU.add)
            else:
                last = dve.tensor_copy(left[:, 0], found)
            c.step(last)
            ends_of = ((slice(0, HALF), 0, slice(0, H)), (slice(HALF, P), 1, slice(H, S)))
            for n in range(3):
                for on, side, cols in ends_of:
                    last = dve.tensor_copy(scores[on, n, :, side, :].rearrange("p h b -> p b h"), left[on, n, :, cols])
                if n < 2:
                    c.step(last)
                    for on, side, cols in ends_of:
                        last = dve.tensor_tensor(left[on, n + 1, :, cols], left[on, n, :, cols],
                                                 scores[on, n, :, side, :].rearrange("p h b -> p b h"), ALU.subtract)
                    c.step(last)
            last.then_inc(q["split"], 1)
            for t in range(T):
                dve.wait_ge(q["rows"], t + 1)
                if bias is not None:
                    dve.tensor_tensor(g.wide[:, t, 0:HF], rows[t % 4][:, 0:HF], bias[:, 0:HF], ALU.add).then_inc(q["rows_copied"], 1)
                else:
                    dve.tensor_copy(g.wide[:, t, 0:HF], rows[t % 4][:, 0:HF]).then_inc(q["rows_copied"], 1)
            with dve.Fori(0, GROUPS // 2) as i:
                for u in range(2):
                    chunks = bass.ds((2 * i + u) * CB, CB)
                    dve.wait_ge(q["looked"], 2 * i + u + 1)
                    dve.wait_ge(q["reduced"], 2 * i + u + 1)
                    dve.tensor_tensor(masked[:, u, :].rearrange("p (c h w) -> p c h w", c=CB, h=H),
                                      bank[4 + u][:, 0:WIDTH].rearrange("p (c h w) -> p c h w", c=CB, h=H),
                                      g.blockmask[:, chunks].rearrange("p c s b -> p c (s b)").unsqueeze(2).broadcast_to([P, CB, H, 2 * NB]),
                                      ALU.mult).then_inc(q["masked"], 1)
                for u in range(2):
                    chunks = bass.ds((2 * i + u) * CB, CB)
                    dve.wait_ge(q["masked"], 2 * i + u + 3)
                    dve.tensor_reduce(lg[:, chunks, 0:H], masked[:, u, :].rearrange("p (c h w) -> p c h w", c=CB, h=H),
                                      AX_X, ALU.add).then_inc(q["reduced"], 1)
            dve.wait_ge(q["reduced"], 2 + GROUPS)
            ls = lg[:, :, 0:H]
            c.step(dve.tensor_tensor(ls, ls, logit_terms, ALU.add))
            c.step(dve.scalar_tensor_tensor(ls, ls, 0.2, ls, ALU.mult, ALU.max))
            dve.tensor_tensor(ls, ls, g.unreal[:].unsqueeze(2).broadcast_to([P, NCH, H]), ALU.add).then_inc(q["logits"], 1)
            dve.wait_ge(q["edge_rows"], 1)
            line = g.ps[0:GC, 0:HG * P]
            blocks = line.rearrange("p (h n e) -> p h n e", h=H, n=G)
            F4, M4 = (v.rearrange("p (h n e) -> p h n e", h=H, n=G) for v in (F0, M0))
            resets = [g.reset[:, d].rearrange("p h n e -> p (h n e)")[:, 0:HG * P] for d in range(2)]
            for way, (scan, row_, carry, back) in enumerate(((q["scan0"], q["row0"], q["carry0"], q["carry0_turned"]),
                                                             (q["scan1"], q["row1"], q["carry1"], q["carry1_turned"]))):
                into, at, first = (F4, P - 1, 0) if way == 0 else (M4, 0, P - 1)

                def sweep():
                    if way == 0:
                        return dve.tensor_tensor_scan(F0, resets[0], line, -BIG, ALU.add, ALU.max)
                    return dve.tensor_tensor_scan(M0[:, ::-1], resets[1][:, ::-1], F0[:, ::-1], -BIG, ALU.add, ALU.max)
                c.step(sweep())
                dve.tensor_copy(ends[0:GC, way].rearrange("p n h -> p h n"), into[:, :, :, at]).then_inc(scan, 1)
                dve.wait_ge(row_, 1)
                run, out = rowbuf[0:H, 2 * way], rowbuf[0:H, 2 * way + 1]
                ins = bank[2 + way][0:H, 0:NCH]
                on = g.carry_on[0:H, way, :]
                if way == 0:
                    c.step(dve.tensor_tensor_scan(run, on, ins, -BIG, ALU.add, ALU.max))
                    dve.tensor_tensor(out[:, 1:NCH], run[:, 0:NCH - 1], g.carry_in[0:H, 0, 1:NCH], ALU.add)
                else:
                    c.step(dve.tensor_tensor_scan(run[:, ::-1], on[:, ::-1], ins[:, ::-1], -BIG, ALU.add, ALU.max))
                    dve.tensor_tensor(out[:, 0:NCH - 1], run[:, 1:NCH], g.carry_in[0:H, 1, 0:NCH - 1], ALU.add)
                dve.memset(out[:, 0:1] if way == 0 else out[:, NCH - 1:NCH], -BIG).then_inc(carry, 1)
                dve.wait_ge(back, 1)
                held = (blocks if way == 0 else F4)[:, :, :, first]
                c.step(dve.tensor_copy(ends[0:GC, way], bank[6 + way][0:GC, 0:G * H].rearrange("p (n h) -> p n h", n=G)))
                c.step(dve.tensor_tensor(held, held, ends[0:GC, way].rearrange("p n h -> p h n"), ALU.max))
                last = sweep()
                if way == 0:
                    c.step(last)
            last.then_inc(q["maxima"], 1)
            dve.wait_ge(q["max_turned"], 1)
            for b in range(HG // 4):
                hs = lg[:, :, 2 * b:2 * b + 2].rearrange("p c h -> p h c")
                last = dve.tensor_tensor(hs, hs, bank[4 + b][:, 0:2 * NCH].rearrange("p (h c) -> p h c", h=2), ALU.subtract)
            last.then_inc(q["shifted"], 1)
            dve.wait_ge(q["weights"], 1)
            dve.wait_ge(g.got_early, before_early + 16 * EARLY)
            dve.sem_inc(q["early"], 1)
            with dve.Fori(0, EARLY) as i:
                for k in range(ROUND):
                    n = i * ROUND + k
                    ch = i * RING + k if k < RING else i + g.EARLY0
                    rows_in = g.ring[:, k, 0:HF] if k < RING else g.early[:, bass.ds(i * HF, HF)]
                    one = bass.ds(ch, 1)
                    dve.wait_ge(q["summed"], n + 1)
                    dve.tensor_scalar(hot[:, k, :], g.lane[:], g.rec[:, one, R_DLO], None, ALU.is_equal)
                    wt = lg[:, one, 0:H].rearrange("p o h -> p (o h)")
                    if extra == "attributes":
                        dve.tensor_tensor(msg[:, k, HF:HF + EX].rearrange("p (h k) -> p h k", h=H),
                                          g.rec[:, one, R_ATTR:R_ATTR + NA].broadcast_to([P, H, NA]),
                                          wt.unsqueeze(2).broadcast_to([P, H, NA]), ALU.mult)
                        if k < RING:
                            dve.wait_ge(got[k], before + 16 * (i + 1))
                        dve.tensor_scalar(msg[:, k, F:HF], rows_in[:, F:HF], lg[:, one, 1], None, ALU.mult).then_inc(q["dve_msg"], 1)
                    else:
                        if k < RING:
                            dve.wait_ge(got[k], before + 16 * (i + 1))
                        dve.tensor_tensor(msg[:, k, 0:HF].rearrange("p (h f) -> p h f", h=H),
                                          rows_in.rearrange("p (h f) -> p h f", h=H),
                                          wt.unsqueeze(2).broadcast_to([P, H, F]), ALU.mult).then_inc(q["dve_msg"], 1)

        @block.scalar
        def _(act):
            for u in range(2):
                act.copy(g.slot_idx[:, u * half:(u + 1) * half], g.idx[:, 0, u * half:(u + 1) * half]).then_inc(q["staged"], 1)
            act.activation(warm, g.ones[:, 0:1], ACT.Exp)
            act.wait_ge(q["shifted"], 1)
            act.activation(lg[:, :, 0:H], lg[:, :, 0:H], ACT.Exp).then_inc(q["weights"], 1)
            act.wait_ge(q["weights"], 1)
            act.wait_ge(g.got_early, before_early + 16 * EARLY)
            act.sem_inc(q["early"], 1)

            def message(i, k, rows_in):
                n = i * ROUND + k
                ch = i * RING + k if k < RING else i + g.EARLY0
                act.wait_ge(q["summed"], n + 1)
                if k < RING:
                    act.wait_ge(got[k], before + 16 * (i + 1))
                if extra == "attributes":
                    act.activation(msg[:, k, 0:F], rows_in[:, 0:F], ACT.Copy, scale=lg[:, bass.ds(ch, 1), 0]).then_inc(q["act_msg"], 1)
                else:
                    act.copy(msg[:, k, HF:HF + H], lg[:, bass.ds(ch, 1), 0:H].rearrange("p o h -> p (o h)")).then_inc(q["act_msg"], 1)

            with act.Fori(0, EARLY) as i:
                for u in range(2):
                    for k in range(half * u, half * u + half):
                        message(i, k, g.ring[:, k, 0:HF])
                    act.copy(g.slot_idx[:, half * u:half * u + half],
                             g.idx[:, 0, bass.ds((2 * i + u + 2) * half, half)]).then_inc(q["staged"], 1)
                message(i, RING, g.early[:, bass.ds(i * HF, HF)])

        @block.sync
        def _(sp):
            for n in range(2):
                ts = slice(n * T // 2, (n + 1) * T // 2)
                sp.wait_ge(q["rows_copied"], (n + 1) * T // 2)
                sp.dma_start(table.rearrange("(t p) d -> p t d", p=P)[:, ts, :], g.wide[:, ts, 0:HF]).then_inc(q["stored"], 16)

        @block.gpsimd
        def _(pool):
            pool.wait_ge(q["stored"], 32)
            pool.sem_inc(q["act_msg"], ROUND)
            pool.sem_inc(q["dve_msg"], ROUND)
            pool.sem_inc(q["round"], 1)
            for k in range(EARLY):
                pool.indirect_dma_start(g.early[:, k * HF:(k + 1) * HF], None, table,
                                        bass.IndirectOffsetOnAxis(ap=g.idx[:, 0, g.EARLY0 + k:g.EARLY0 + k + 1], axis=0)
                                        ).then_inc(g.got_early, 16)
            with pool.Fori(0, EARLY) as i:
                for u in range(2):
                    pool.wait_ge(q["staged"], 2 * i + u + 1)
                    for k in range(half * u, half * (u + 1)):
                        pool.wait_ge(q["act_msg"], i * ROUND + k + 1)
                        pool.wait_ge(q["dve_msg"], i * ROUND + k + 1)
                        pool.sem_inc(q["round"], 1)
                        pool.indirect_dma_start(g.ring[:, k, 0:HF], None, table,
                                                bass.IndirectOffsetOnAxis(ap=g.slot_idx[:, k:k + 1], axis=0)).then_inc(got[k], 16)


def block1(g):
    nc, T, D, H, F = g.nc, g.T, g.D, g.H1, g.F1
    attention(g, "b1", H, F, g.w1x[:], g.bias1, g.table1, g.ab1[:].unsqueeze(1).broadcast_to([P, g.NCH, H]), "weights")
    s_dve = g.sem("b1_finish")
    with nc.Block(name="b1_finish") as block:
        @block.vector
        def _(dve):
            c = Chain(dve, s_dve)
            den = g.small[:, :, 0:H]
            c.step(dve.tensor_scalar(den, g.ps[:, g.ATT0:g.ATT0 + T * H].rearrange("p (t h) -> p t h", t=T), 1.0e-30, None, ALU.max))
            c.step(dve.reciprocal(den, den))
            c.step(dve.tensor_tensor(g.h[:].rearrange("p t (h f) -> p t h f", h=H),
                                     g.ps[:, 0:T * D].rearrange("p (t h f) -> p t h f", t=T, h=H),
                                     den.unsqueeze(3).broadcast_to([P, T, H, F]), ALU.mult))
            dve.tensor_tensor(g.x[:], g.x[:], g.h[:], ALU.add)


def block2(g):
    nc, T, D, L, H, F, AT = g.nc, g.T, g.D, g.L, g.H2, g.F2, g.AT
    HF = H * F
    bank = [g.ps[:, 512 * k:512 * k + 512] for k in range(8)]
    with nc.Fori(0, L) as l:
        attention(g, "b2", H, F, g.w2x[:, bass.ds(l, 1), :].rearrange("p o w -> p (o w)"), None, g.table,
                         g.attr_part[:, :, bass.ds(l * H, H)], "attributes", l, L)
        names = ("dve", "attr", "attr_turned", "attr_copied", "attr_sum", "read", "h", "turned")
        q = {n: g.sem(f"b2_finish_{n}") for n in names}
        lot = Lot(g.scratch[:].bitcast(BF16))
        den = lot.take([P, T, H])
        att = lot.take([P, T, AT])
        attT = lot.take([AT, g.NP])
        with nc.Block(name="b2_finish") as block:
            @block.vector
            def _(dve):
                c = Chain(dve, q["dve"])
                sums = g.ps[:, g.ATT0:g.ATT0 + T * AT].rearrange("p (t h k) -> p t h k", t=T, h=H)
                c.step(dve.tensor_scalar(den, sums[:, :, :, NA - 1], 1.0e-16, None, ALU.add))
                c.step(dve.reciprocal(den, den))
                c.step(dve.tensor_scalar(den, den, 1.0 / H, None, ALU.mult))
                dve.tensor_tensor(att.rearrange("p t (h k) -> p t h k", h=H), sums,
                                  den.unsqueeze(3).broadcast_to([P, T, H, NA]), ALU.mult).then_inc(q["attr"], 1)
                c.step(dve.tensor_tensor(g.wide[:].rearrange("p t (h f) -> p t h f", h=H),
                                         g.ps[:, 0:T * HF].rearrange("p (t h f) -> p t h f", t=T, h=H),
                                         den.unsqueeze(3).broadcast_to([P, T, H, F]), ALU.mult))
                dve.sem_inc(q["read"], 1)
                c.step(dve.tensor_tensor(g.h[:], g.wide[:, :, 0:F], g.wide[:, :, F:HF], ALU.add))
                c.step(dve.tensor_tensor(g.h[:], g.h[:], g.bias2[:, bass.ds(l, 1), :].broadcast_to([P, T, D]), ALU.add))
                dve.wait_ge(q["attr_sum"], 1)
                c.step(dve.tensor_tensor(g.h[:], g.h[:], g.ps[:, 0:T * D].rearrange("p (t d) -> p t d", d=D), ALU.add))
                dve.tensor_scalar(g.h[:], g.h[:], g.floor2[:, bass.ds(l, 1)], None, ALU.max).then_inc(q["h"], 1)

            @block.tensor
            def _(pe):
                pe.wait_ge(q["attr"], 1)
                for t in range(T):
                    if t == 8:
                        pe.wait_ge(q["attr_copied"], 1)
                    b = 6 + t // 4 if t < 8 else 6
                    tr = pe.transpose(bank[b][0:AT, (t % 4) * P:(t % 4) * P + P], att[:, t, :], g.ident[:])
                    if t % 4 == 3 or t == T - 1:
                        tr.then_inc(q["attr_turned"], 1)
                pe.wait_ge(q["attr_copied"], 3)
                pe.wait_ge(q["read"], 1)
                for t in range(T):
                    mm = pe.matmul(g.ps[:, t * D:(t + 1) * D], attT[:, t * P:(t + 1) * P],
                                   g.ew[:, bass.ds(l, 1), :].rearrange("p o d -> p (o d)"), start=True, stop=True)
                mm.then_inc(q["attr_sum"], 1)
                pe.wait_ge(q["h"], 1)
                turn_nodes(g, pe, q["turned"], banks=4)

            @block.scalar
            def _(act):
                for n in range(3):
                    act.wait_ge(q["attr_turned"], n + 1)
                    w = min(4, T - 4 * n) * P
                    act.copy(attT[:, n * 512:n * 512 + w], bank[6 + n % 2][0:AT, 0:w]).then_inc(q["attr_copied"], 1)
                turn_copies(g, act, q["turned"], banks=4)
        g.stage.clear()
    with nc.Block(name="b2_add") as block:
        @block.vector
        def _(dve):
            dve.tensor_tensor(g.x[:], g.x[:], g.h[:], ALU.add)


def block3(g):
    nc, a, T, D, NP, CH, HID, DT = g.nc, g.a, g.T, g.D, g.NP, g.CH, g.HID, g.DT
    bank = [g.ps[:, 512 * k:512 * k + 512] for k in range(8)]
    flat = g.arena[:].rearrange("p s e -> p (s e)")
    C = flat[:, 0:2 * T * NP].bitcast(F32).rearrange("p (t n) -> p t n", t=T)
    lot = Lot(flat[:, 2 * T * NP:])
    w_in, w1, w2 = lot.take([P, D]), lot.take([P, HID]), lot.take([P, 2, D])
    b_in, b2 = lot.take([P, D]), lot.take([P, D])
    keep = lot.take([P, 1])
    deg, rdeg = lot.take([P, T]), lot.take([P, T])
    aggT = lot.take([P, NP])
    tmp = lot.take([P, T, D])
    hot_d = lot.take([P, RING, P], BF16)
    lots = [Lot(g.scratch[:].bitcast(BF16)), Lot(g.wide[:].rearrange("p t f -> p (t f)").bitcast(BF16))]
    hot_s = [lots[k % 2].take([P, NP], BF16) for k in range(RING)]
    zT = g.wide[:].rearrange("p t f -> p (t f)").rearrange("p (k n) -> p k n", k=2)

    REGION = 4 * 512
    assert REGION == 1 << 11
    names = ("loaded", "hots", "summed", "taken", "dve", "degrees", "apart", "divided", "turned", "rows_back", "cols_back")
    q = {n: g.sem(f"b3_{n}") for n in names}
    assert T % 2 == 0
    with nc.Block(name="b3_counts") as block:
        @block.sync
        def _(sp):
            for dst, src in ((w_in, a["L3_gnn_W_in"]), (w1, a["L3_gnn_W1"]), (w2, a["L3_gnn_W2"].rearrange("(k p) o -> p k o", p=P)),
                             (b_in, a["L3_gnn_b_in"].partition_broadcast(P)), (b2, a["L3_gnn_b2"].partition_broadcast(P))):
                sp.dma_start(dst, src).then_inc(q["loaded"], 16)
            sp.wait_ge(q["loaded"], 16 * 5)

        @block.vector
        def _(dve):
            c = Chain(dve, q["dve"])
            c.step(dve.tensor_scalar(keep, g.cols[:, 5:6], 0.0, None, ALU.max))
            c.step(dve.tensor_scalar(keep, keep, -DT, 1.0, ALU.mult, ALU.add))
            with dve.Fori(0, CH // RING) as i:
                for k in range(RING):
                    ch = i * RING + k
                    one = bass.ds(ch, 1)
                    dve.wait_ge(q["summed"], ch + 1)
                    dve.tensor_scalar(hot_d[:, k, :], g.lane16[:], g.rec[:, one, R_DLO], g.rec[:, one, R_ORIG],
                                      ALU.is_equal, ALU.mult)
                    dve.tensor_scalar(hot_s[k], g.nodeid[:], g.rec[:, one, R_SRC], None, ALU.is_equal).then_inc(q["hots"], 1)
            dve.wait_ge(q["taken"], 2 + T)
            c.step(dve.tensor_copy(rdeg, deg))
            c.step(dve.tensor_tensor(rdeg[:, 2:T], deg[:, 2:T], deg[:, 0:T - 2], ALU.subtract))
            c.step(dve.tensor_scalar(rdeg, rdeg, 1.0, None, ALU.max))
            dve.reciprocal(rdeg, rdeg).then_inc(q["degrees"], 1)
            for t in range(T - 2, 0, -2):
                dve.tensor_tensor(C[:, t:t + 2, :], C[:, t:t + 2, :], C[:, t - 2:t, :], ALU.subtract).then_inc(q["apart"], 1)
                dve.wait_ge(q["apart"], (T - t) // 2)
            for t in range(T - 1):
                dve.wait_ge(q["turned"], 2 * t + 2)
                dve.tensor_copy(C[:, t, (t + 1) * P:NP], g.ps[:, REGION:REGION + (T - 1 - t) * P]).then_inc(q["cols_back"], 1)

        @block.tensor
        def _(pe):
            pe.sem_inc(q["summed"], RING)
            pe.sem_inc(q["taken"], 2)
            for b in range(8):
                pe.matmul(bank[b], g.zerob[:, 0:P], g.zerob[:], start=True, stop=True, skip_group_check=True)

            def count_round(i, packed, _):
                for k in range(RING):
                    pe.wait_ge(q["taken"], tile_of(packed, k))
                    pe.wait_ge(q["hots"], i * RING + k + 1)
                    up = 11 - 4 * k
                    region = (packed & (1 << 4 * k)) << up if up > 0 else (packed >> -up) & REGION
                    for p, e in halves(g):
                        mm = pe.matmul(g.ps[:, bass.ds(region + p, e - p)], hot_d[:, k, :], hot_s[k][:, p:e],
                                       start=False, stop=True, skip_group_check=True)
                    mm.then_inc(q["summed"], 1)
            walk_rounds(pe, g, CH // RING, count_round)
            pe.wait_ge(q["divided"], T)
            for t in range(T):
                if t:
                    pe.wait_ge(q["rows_back"], t)
                for s_ in range(t, T):
                    tr = pe.transpose(g.ps[:, (s_ - t) * P:(s_ - t + 1) * P], C[:, t, s_ * P:(s_ + 1) * P], g.ident[:])
                tr.then_inc(q["turned"], 1)
                if t < T - 1:
                    if t:
                        pe.wait_ge(q["cols_back"], t)
                    for s_ in range(t + 1, T):
                        tr = pe.transpose(g.ps[:, REGION + (s_ - t - 1) * P:REGION + (s_ - t) * P], C[:, s_, t * P:(t + 1) * P], g.ident[:])
                    tr.then_inc(q["turned"], 1)

        @block.scalar
        def _(act):
            with act.Fori(0, T // 2) as i:
                _, last_ = nc.values_load_multi_w_load_instructions(g.tile_end[0:1, bass.ds(2 * i, 2)], min_val=1, max_val=CH,
                                                                    engines=[mybir.EngineType.Activation])
                for u in range(2):
                    act.wait_ge(q["summed"], last_[u] + RING)
                    act.activation(C[:, bass.ds(2 * i + u, 1), :].rearrange("p o n -> p (o n)"), g.ps[:, (1 - u) * REGION:(1 - u) * REGION + NP],
                                   ACT.Copy, accum_out=deg[:, bass.ds(2 * i + u, 1)]).then_inc(q["taken"], 1)
            act.wait_ge(q["degrees"], 1)
            for n, t in enumerate(range(T - 2, -1, -2)):
                act.wait_ge(q["apart"], min(n + 1, T // 2 - 1))
                for t_ in (t, t + 1):
                    act.activation(C[:, t_, :], C[:, t_, :], ACT.Copy, scale=rdeg[:, t_:t_ + 1]).then_inc(q["divided"], 1)
            for t in range(T):
                act.wait_ge(q["turned"], min(2 * t + 2, 2 * T - 1))
                act.copy(C[:, t:T, t * P:(t + 1) * P], g.ps[:, 0:(T - t) * P].rearrange("p (s n) -> p s n", n=P)).then_inc(q["rows_back"], 1)
    g.stage.end()

    names = ("agg", "aggT", "z", "gelu", "out", "pre", "tanh", "h", "start", "start_sum", "dve", "kept", "done")
    q = {n: g.sem(f"b3_{n}") for n in names}
    parts = halves(g)
    with nc.Block(name="b3_steps") as block:
        @block.tensor
        def _(pe):
            for n, (p, e) in enumerate(parts):
                for t in range(p // P, e // P):
                    mm = pe.matmul(bank[5 + n][:, t * P - p:t * P - p + P], g.hT[:, t * P:(t + 1) * P], w_in, start=True, stop=True)
                mm.then_inc(q["start"], 1)

            def gather(i, n):
                p, e = parts[n]
                for s_ in range(T):
                    if n == 0 and s_ % 4 == 0:
                        pe.wait_ge(q["h"], 3 * i + s_ // 4 + 1)
                    mm = pe.matmul(bank[n][:, 0:e - p], g.h[:, s_, :], C[:, s_, p:e], start=s_ == 0, stop=s_ == T - 1)
                mm.then_inc(q["agg"], 1)

            def hidden(i, n):
                p, e = parts[n]
                pe.wait_ge(q["aggT"], 3 * i + n + 1)
                pe.wait_ge(q["gelu"], 3 * i + n + 1)
                for k in range(2):
                    mm = pe.matmul(bank[3 + k][:, 0:e - p], w1[:, k * P:(k + 1) * P], aggT[:, p:e], start=True, stop=True)
                mm.then_inc(q["z"], 1)

            def output(i, n):
                p, e = parts[n]
                pe.wait_ge(q["gelu"], 3 * i + n + 2)
                for t in range(p // P, e // P):
                    for k in range(2):
                        mm = pe.matmul(bank[5 + n][:, t * P - p:t * P - p + P], zT[:, k, t * P:(t + 1) * P], w2[:, k, :],
                                       start=k == 0, stop=k == 1)
                mm.then_inc(q["out"], 1)

            pe.sem_inc(q["gelu"], 1)
            with pe.Fori(0, g.STEPS) as i:
                gather(i, 0)
                gather(i, 1)
                hidden(i, 0)
                gather(i, 2)
                hidden(i, 1)
                output(i, 0)
                hidden(i, 2)
                output(i, 1)
                output(i, 2)

        @block.scalar
        def _(act):
            for n, (p, e) in enumerate(parts):
                act.wait_ge(q["start_sum"], n + 1)
                act.activation(g.h[:, p // P:e // P, :], tmp[:, p // P:e // P, :], ACT.Tanh).then_inc(q["h"], 1)

            def copy(i, n):
                p, e = parts[n]
                act.wait_ge(q["agg"], 3 * i + n + 1)
                act.copy(aggT[:, p:e], bank[n][:, 0:e - p]).then_inc(q["aggT"], 1)

            def gelu(i, n):
                p, e = parts[n]
                act.wait_ge(q["z"], 3 * i + n + 1)
                for k in range(2):
                    last = act.activation(zT[:, k, p:e], bank[3 + k][:, 0:e - p], ACT.Gelu, bias=g.cols[:, 2 + k:3 + k])
                last.then_inc(q["gelu"], 1)

            def tanh(i, n):
                p, e = parts[n]
                act.wait_ge(q["pre"], 3 * i + n + 1)
                act.activation(tmp[:, p // P:e // P, :], tmp[:, p // P:e // P, :], ACT.Tanh).then_inc(q["tanh"], 1)

            with act.Fori(0, g.STEPS) as i:
                copy(i, 0)
                copy(i, 1)
                gelu(i, 0)
                copy(i, 2)
                gelu(i, 1)
                gelu(i, 2)
                tanh(i, 0)
                tanh(i, 1)
                tanh(i, 2)

        @block.vector
        def _(dve):
            def summed(n, bias):
                p, e = parts[n]
                ts = slice(p // P, e // P)
                return dve.tensor_tensor(tmp[:, ts, :], bank[5 + n][:, 0:e - p].rearrange("p (t d) -> p t d", d=D),
                                         bias.unsqueeze(1).broadcast_to([P, (e - p) // P, D]), ALU.add)
            for n in range(3):
                dve.wait_ge(q["start"], n + 1)
                summed(n, b_in).then_inc(q["start_sum"], 1)
            dve.wait_ge(q["h"], 3)
            with dve.Fori(0, g.STEPS) as i:
                for n, (p, e) in enumerate(parts):
                    ts = slice(p // P, e // P)
                    dve.wait_ge(q["out"], 3 * i + n + 1)
                    summed(n, b2).then_inc(q["pre"], 1)
                    dve.tensor_scalar(g.h[:, ts, :], g.h[:, ts, :], keep, None, ALU.mult).then_inc(q["kept"], 1)
                for n, (p, e) in enumerate(parts):
                    ts = slice(p // P, e // P)
                    dve.wait_ge(q["tanh"], 3 * i + n + 1)
                    dve.wait_ge(q["kept"], 3 * i + n + 1)
                    dve.scalar_tensor_tensor(g.h[:, ts, :], tmp[:, ts, :], DT, g.h[:, ts, :], ALU.mult, ALU.add).then_inc(q["h"], 1)
            dve.wait_ge(q["h"], 3 + 3 * g.STEPS)
            dve.tensor_tensor(g.x[:], g.x[:], g.h[:], ALU.add).then_inc(q["dve"], 1)

        @block.sync
        def _(sp):
            sp.wait_ge(q["dve"], 1)
            sp.dma_start(g.out[0:(T - 1) * P, :].rearrange("(t p) d -> p t d", p=P), g.x[:, 0:T - 1, :]).then_inc(q["done"], 16)
            sp.dma_start(g.out[(T - 1) * P:, :], g.x[0:g.LAST, T - 1, :]).then_inc(q["done"], 16)
            sp.wait_ge(q["done"], 32)


_INS = ["x", "src", "dst", "edge_attr_16", "edge_weight1", "L0_gnn_batch_num", "L0_gnn_W1", "L0_gnn_W2", "L0_gnn_Wo",
        "L0_gnn_Wn", "L0_gnn_gamma", "L0_gnn_beta", "L1_gnn_W_w", "L1_gnn_W_b", "L1_gnn_a_w", "L1_gnn_a_b",
        "L2_gnn_weights", "L2_gnn_atts", "L2_gnn_biases", "L2_gnn_edge_ws", "L2_gnn_edge_bs", "L3_gnn_W_in",
        "L3_gnn_b_in", "L3_gnn_W1", "L3_gnn_b1", "L3_gnn_W2", "L3_gnn_b2", "L3_gnn_clearance"]


def kernel(**inputs):
    import numpy as _np
    import concourse.bacc as _bacc
    from concourse import mybir as _mybir
    from concourse.bass_utils import run_bass_kernel_spmd as _run

    nc = _bacc.Bacc("TRN2", target_bir_lowering=False, num_devices=1)
    arrays, views = {}, {}
    for name in _INS:
        v = _np.ascontiguousarray(inputs[name])
        arrays[f"in_{name}"] = v
        views[name] = nc.dram_tensor(f"in_{name}", v.shape, _mybir.dt.from_np(v.dtype), kind="ExternalInput").ap()
    out = nc.dram_tensor("out_0", inputs["x"].shape, _mybir.dt.float32, kind="ExternalOutput").ap()
    graph_kernel(nc, views, out)
    r = _run(nc, [arrays], core_ids=[0])
    return r.results[0]["out_0"]
```
